# Optimizing a Trainium2 kernel written in Bass

```python
import numpy as np
import jax
import jax.numpy as jnp

def _softmax(x, axis=-1):
    return jax.nn.softmax(x, axis=axis)

def _gelu(x):
    return jax.nn.gelu(x, approximate=True)

def _silu(x):
    return jax.nn.silu(x)

def _sigmoid(x):
    return jax.nn.sigmoid(x)

def _layernorm(x, axis=-1, eps=1e-05):
    m = jnp.mean(x, axis=axis, keepdims=True)
    v = jnp.var(x, axis=axis, keepdims=True)
    return (x - m) / jnp.sqrt(v + eps)

def _scatter_add(tgt, idx, src, axis=0):
    return tgt.at[idx].add(src)

def _segment_sum(src, seg, n):
    return jax.ops.segment_sum(src, seg, n)
kernel_name = 'mk_sandwich_d1_jaxref_r4_55cc02'

def setup_inputs(seed: int=0):
    np.random.seed(seed)
    _w = jnp.asarray

    def _L0_attn_setup():
        import jax, jax.numpy as jnp
        import numpy as np
        D_MODEL = 256
        N_HEADS = 16
        NUM_PATTERN = 32
        HEAD_DIM = D_MODEL // N_HEADS

        def sparsemax(z):
            S = z.shape[-1]
            z_sorted = -jnp.sort(-z, axis=-1)
            cum = jnp.cumsum(z_sorted, axis=-1)
            k = jnp.arange(1, S + 1, dtype=z.dtype)
            support = 1.0 + k * z_sorted > cum
            k_sup = jnp.sum(support, axis=-1, keepdims=True)
            cum_sel = jnp.take_along_axis(cum, k_sup - 1, axis=-1)
            tau = (cum_sel - 1.0) / k_sup.astype(z.dtype)
            return jnp.maximum(z - tau, 0.0)
        key = jax.random.key(seed)
        ks = jax.random.split(key, 10)
        s = 1.0 / np.sqrt(D_MODEL)
        inp = {'query': jax.random.normal(ks[0], (8, 1024, D_MODEL), dtype=jnp.float32), 'key_param': jax.random.normal(ks[1], (1, NUM_PATTERN, D_MODEL), dtype=jnp.float32), 'Wq': jax.random.normal(ks[2], (D_MODEL, N_HEADS * HEAD_DIM), dtype=jnp.float32) * s, 'bq': jnp.zeros((N_HEADS * HEAD_DIM,), dtype=jnp.float32), 'Wk': jax.random.normal(ks[3], (D_MODEL, N_HEADS * HEAD_DIM), dtype=jnp.float32) * s, 'bk': jnp.zeros((N_HEADS * HEAD_DIM,), dtype=jnp.float32), 'Wv': jax.random.normal(ks[4], (N_HEADS * HEAD_DIM, N_HEADS * HEAD_DIM), dtype=jnp.float32) * s, 'bv': jnp.zeros((N_HEADS * HEAD_DIM,), dtype=jnp.float32), 'Wo': jax.random.normal(ks[5], (N_HEADS * HEAD_DIM, D_MODEL), dtype=jnp.float32) * s, 'bo': jnp.zeros((D_MODEL,), dtype=jnp.float32)}
        return inp
    _L0_attn_in = _L0_attn_setup()

    def _L0_ffn_setup():
        import jax, jax.numpy as jnp
        import numpy as np
        B, L, D = (4, 512, 256)
        H = 16
        E = 16
        NS = 16
        S = NS // E
        F = 1024
        EPS = 1e-05

        def _layernorm(x, g, b):
            mu = jnp.mean(x, axis=-1, keepdims=True)
            var = jnp.mean(jnp.square(x - mu), axis=-1, keepdims=True)
            return (x - mu) * jax.lax.rsqrt(var + EPS) * g + b

        def _mha(q, k, v, Wq, bq, Wk, bk, Wv, bv, Wo, bo):
            Bq, Lq, Dm = q.shape
            dh = Dm // H
            qh = (q @ Wq + bq).reshape(Bq, Lq, H, dh)
            kh = (k @ Wk + bk).reshape(Bq, -1, H, dh)
            vh = (v @ Wv + bv).reshape(Bq, -1, H, dh)
            scores = jnp.einsum('bqhd,bkhd->bhqk', qh, kh) / jnp.asarray(np.sqrt(dh), q.dtype)
            attn = jax.nn.softmax(scores, axis=-1)
            out = jnp.einsum('bhqk,bkhd->bqhd', attn, vh).reshape(Bq, Lq, Dm)
            return out @ Wo + bo
        key = jax.random.key(seed)
        ks = jax.random.split(key, 32)
        s = 0.02
        d = {}
        d['x'] = jax.random.normal(ks[0], (B, L, D), jnp.float32)
        d['slot_query'] = jax.random.normal(ks[1], (1, NS, D), jnp.float32) * 0.01
        for i, nm in enumerate(['d_Wq', 'd_Wk', 'd_Wv', 'd_Wo']):
            d[nm] = jax.random.normal(ks[2 + i], (D, D), jnp.float32) * s
        for nm in ['d_bq', 'd_bk', 'd_bv', 'd_bo']:
            d[nm] = jnp.zeros((D,), jnp.float32)
        for i, nm in enumerate(['c_Wq', 'c_Wk', 'c_Wv', 'c_Wo']):
            d[nm] = jax.random.normal(ks[6 + i], (D, D), jnp.float32) * s
        for nm in ['c_bq', 'c_bk', 'c_bv', 'c_bo']:
            d[nm] = jnp.zeros((D,), jnp.float32)
        d['e_ln_g'] = jnp.ones((E, D), jnp.float32)
        d['e_ln_b'] = jnp.zeros((E, D), jnp.float32)
        d['e_W1'] = jax.random.normal(ks[10], (E, D, F), jnp.float32) * s
        d['e_b1'] = jnp.zeros((E, F), jnp.float32)
        d['e_Wg'] = jax.random.normal(ks[11], (E, D, F), jnp.float32) * s
        d['e_bg'] = jnp.zeros((E, F), jnp.float32)
        d['e_W2'] = jax.random.normal(ks[12], (E, F, D), jnp.float32) * s
        d['e_b2'] = jnp.zeros((E, D), jnp.float32)
        return d
    _L0_ffn_in = _L0_ffn_setup()
    _d = {'L0_attn_query': _L0_attn_in['query'], 'L0_attn_key_param': _L0_attn_in['key_param'], 'L0_attn_Wq': _L0_attn_in['Wq'], 'L0_attn_bq': _L0_attn_in['bq'], 'L0_attn_Wk': _L0_attn_in['Wk'], 'L0_attn_bk': _L0_attn_in['bk'], 'L0_attn_Wv': _L0_attn_in['Wv'], 'L0_attn_bv': _L0_attn_in['bv'], 'L0_attn_Wo': _L0_attn_in['Wo'], 'L0_attn_bo': _L0_attn_in['bo'], 'L0_ffn_slot_query': _L0_ffn_in['slot_query'], 'L0_ffn_d_Wq': _L0_ffn_in['d_Wq'], 'L0_ffn_d_Wk': _L0_ffn_in['d_Wk'], 'L0_ffn_d_Wv': _L0_ffn_in['d_Wv'], 'L0_ffn_d_Wo': _L0_ffn_in['d_Wo'], 'L0_ffn_d_bq': _L0_ffn_in['d_bq'], 'L0_ffn_d_bk': _L0_ffn_in['d_bk'], 'L0_ffn_d_bv': _L0_ffn_in['d_bv'], 'L0_ffn_d_bo': _L0_ffn_in['d_bo'], 'L0_ffn_c_Wq': _L0_ffn_in['c_Wq'], 'L0_ffn_c_Wk': _L0_ffn_in['c_Wk'], 'L0_ffn_c_Wv': _L0_ffn_in['c_Wv'], 'L0_ffn_c_Wo': _L0_ffn_in['c_Wo'], 'L0_ffn_c_bq': _L0_ffn_in['c_bq'], 'L0_ffn_c_bk': _L0_ffn_in['c_bk'], 'L0_ffn_c_bv': _L0_ffn_in['c_bv'], 'L0_ffn_c_bo': _L0_ffn_in['c_bo'], 'L0_ffn_e_ln_g': _L0_ffn_in['e_ln_g'], 'L0_ffn_e_ln_b': _L0_ffn_in['e_ln_b'], 'L0_ffn_e_W1': _L0_ffn_in['e_W1'], 'L0_ffn_e_b1': _L0_ffn_in['e_b1'], 'L0_ffn_e_Wg': _L0_ffn_in['e_Wg'], 'L0_ffn_e_bg': _L0_ffn_in['e_bg'], 'L0_ffn_e_W2': _L0_ffn_in['e_W2'], 'L0_ffn_e_b2': _L0_ffn_in['e_b2']}
    _x0 = _d['L0_attn_query']
    _d['L0_attn_query'] = jax.random.normal(jax.random.fold_in(jax.random.key(seed), 1), (2, 2048, 256), dtype=_x0.dtype)
    del _x0
    return _d

def reference(L0_attn_query, L0_attn_key_param, L0_attn_Wq, L0_attn_bq, L0_attn_Wk, L0_attn_bk, L0_attn_Wv, L0_attn_bv, L0_attn_Wo, L0_attn_bo, L0_ffn_slot_query, L0_ffn_d_Wq, L0_ffn_d_Wk, L0_ffn_d_Wv, L0_ffn_d_Wo, L0_ffn_d_bq, L0_ffn_d_bk, L0_ffn_d_bv, L0_ffn_d_bo, L0_ffn_c_Wq, L0_ffn_c_Wk, L0_ffn_c_Wv, L0_ffn_c_Wo, L0_ffn_c_bq, L0_ffn_c_bk, L0_ffn_c_bv, L0_ffn_c_bo, L0_ffn_e_ln_g, L0_ffn_e_ln_b, L0_ffn_e_W1, L0_ffn_e_b1, L0_ffn_e_Wg, L0_ffn_e_bg, L0_ffn_e_W2, L0_ffn_e_b2):

    def _L0_attn_ref(query, key_param, Wq, bq, Wk, bk, Wv, bv, Wo, bo):
        import jax, jax.numpy as jnp
        import numpy as np
        D_MODEL = 256
        N_HEADS = 16
        NUM_PATTERN = 32
        HEAD_DIM = D_MODEL // N_HEADS

        def sparsemax(z):
            S = z.shape[-1]
            z_sorted = -jnp.sort(-z, axis=-1)
            cum = jnp.cumsum(z_sorted, axis=-1)
            k = jnp.arange(1, S + 1, dtype=z.dtype)
            support = 1.0 + k * z_sorted > cum
            k_sup = jnp.sum(support, axis=-1, keepdims=True)
            cum_sel = jnp.take_along_axis(cum, k_sup - 1, axis=-1)
            tau = (cum_sel - 1.0) / k_sup.astype(z.dtype)
            return jnp.maximum(z - tau, 0.0)
        B, L, _ = query.shape
        S = key_param.shape[1]
        H, E = (N_HEADS, HEAD_DIM)
        D = HEAD_DIM
        k = jnp.broadcast_to(key_param, (B, S, D_MODEL))
        queries = (query @ Wq + bq).reshape(B, L, H, E)
        keys_flat = k @ Wk + bk
        values = (keys_flat @ Wv + bv).reshape(B, S, H, D)
        keys = keys_flat.reshape(B, S, H, E)
        scale = 1.0 / np.sqrt(E)
        scores = jnp.einsum('blhe,bshe->bhls', queries, keys)
        A = sparsemax(scale * scores)
        out = jnp.einsum('bhls,bshd->blhd', A, values)
        out = jnp.transpose(out, (0, 2, 1, 3)).reshape(B, L, H * D)
        return out @ Wo + bo

    def _L0_ffn_ref(x, slot_query, d_Wq, d_Wk, d_Wv, d_Wo, d_bq, d_bk, d_bv, d_bo, c_Wq, c_Wk, c_Wv, c_Wo, c_bq, c_bk, c_bv, c_bo, e_ln_g, e_ln_b, e_W1, e_b1, e_Wg, e_bg, e_W2, e_b2):
        import jax, jax.numpy as jnp
        import numpy as np
        B, L, D = (4, 512, 256)
        H = 16
        E = 16
        NS = 16
        S = NS // E
        F = 1024
        EPS = 1e-05

        def _layernorm(x, g, b):
            mu = jnp.mean(x, axis=-1, keepdims=True)
            var = jnp.mean(jnp.square(x - mu), axis=-1, keepdims=True)
            return (x - mu) * jax.lax.rsqrt(var + EPS) * g + b

        def _mha(q, k, v, Wq, bq, Wk, bk, Wv, bv, Wo, bo):
            Bq, Lq, Dm = q.shape
            dh = Dm // H
            qh = (q @ Wq + bq).reshape(Bq, Lq, H, dh)
            kh = (k @ Wk + bk).reshape(Bq, -1, H, dh)
            vh = (v @ Wv + bv).reshape(Bq, -1, H, dh)
            scores = jnp.einsum('bqhd,bkhd->bhqk', qh, kh) / jnp.asarray(np.sqrt(dh), q.dtype)
            attn = jax.nn.softmax(scores, axis=-1)
            out = jnp.einsum('bhqk,bkhd->bqhd', attn, vh).reshape(Bq, Lq, Dm)
            return out @ Wo + bo
        Bx = x.shape[0]
        q = jnp.broadcast_to(slot_query, (Bx, NS, D))
        o = q + _mha(q, x, x, d_Wq, d_bq, d_Wk, d_bk, d_Wv, d_bv, d_Wo, d_bo)
        os = o.reshape(Bx, E, S, D)
        h = _layernorm(os, e_ln_g[None, :, None, :], e_ln_b[None, :, None, :])
        u = jax.nn.silu(jnp.einsum('besd,edf->besf', h, e_W1) + e_b1[None, :, None, :])
        g = jax.nn.silu(jnp.einsum('besd,edf->besf', h, e_Wg) + e_bg[None, :, None, :])
        y = jnp.einsum('besf,efd->besd', u * g, e_W2) + e_b2[None, :, None, :]
        o = o + y.reshape(Bx, NS, D)
        out = _mha(x, o, o, c_Wq, c_bq, c_Wk, c_bk, c_Wv, c_bv, c_Wo, c_bo)
        return out
    x = L0_attn_query
    x = x + _layernorm(_L0_attn_ref(_layernorm(x, axis=-1), L0_attn_key_param, L0_attn_Wq, L0_attn_bq, L0_attn_Wk, L0_attn_bk, L0_attn_Wv, L0_attn_bv, L0_attn_Wo, L0_attn_bo), axis=-1)
    x = x + _layernorm(_L0_ffn_ref(_layernorm(x, axis=-1), L0_ffn_slot_query, L0_ffn_d_Wq, L0_ffn_d_Wk, L0_ffn_d_Wv, L0_ffn_d_Wo, L0_ffn_d_bq, L0_ffn_d_bk, L0_ffn_d_bv, L0_ffn_d_bo, L0_ffn_c_Wq, L0_ffn_c_Wk, L0_ffn_c_Wv, L0_ffn_c_Wo, L0_ffn_c_bq, L0_ffn_c_bk, L0_ffn_c_bv, L0_ffn_c_bo, L0_ffn_e_ln_g, L0_ffn_e_ln_b, L0_ffn_e_W1, L0_ffn_e_b1, L0_ffn_e_Wg, L0_ffn_e_bg, L0_ffn_e_W2, L0_ffn_e_b2), axis=-1)
    return x

_drawn_inputs = setup_inputs


def setup_inputs(seed=0):
    import zlib

    import numpy as np

    out = dict(_drawn_inputs(seed))
    spreads = {'L0_attn_bq': (0.0, 0.1),
     'L0_attn_bk': (0.0, 0.1),
     'L0_attn_bv': (0.0, 0.1),
     'L0_attn_bo': (0.0, 0.1),
     'L0_ffn_d_bq': (0.0, 0.8),
     'L0_ffn_d_bk': (0.0, 2.0),
     'L0_ffn_d_bv': (0.0, 0.37),
     'L0_ffn_d_bo': (0.0, 0.1),
     'L0_ffn_c_bq': (0.0, 0.8),
     'L0_ffn_c_bk': (0.0, 2.0),
     'L0_ffn_c_bv': (0.0, 2.0),
     'L0_ffn_c_bo': (0.0, 0.729),
     'L0_ffn_e_ln_g': (1.0, 0.6),
     'L0_ffn_e_ln_b': (0.0, 0.8),
     'L0_ffn_e_b1': (0.0, 0.8),
     'L0_ffn_e_bg': (0.0, 0.8),
     'L0_ffn_e_b2': (0.0, 0.624)}
    factors = {'L0_ffn_slot_query': 8.0,
     'L0_ffn_d_Wq': 8.0,
     'L0_ffn_d_Wk': 8.0,
     'L0_ffn_d_Wv': 8.0,
     'L0_ffn_d_Wo': 2.887,
     'L0_ffn_c_Wq': 8.0,
     'L0_ffn_c_Wk': 8.0,
     'L0_ffn_e_W1': 8.0,
     'L0_ffn_e_Wg': 8.0,
     'L0_ffn_e_W2': 8.0}
    for name, (base, spread) in spreads.items():
        noise = np.random.default_rng([zlib.crc32(name.encode()), seed]).standard_normal(out[name].shape)
        drawn = base * np.exp(spread * noise) if base else spread * noise
        out[name] = jnp.asarray(drawn.astype(out[name].dtype))
    for name, factor in factors.items():
        out[name] = (out[name] * factor).astype(out[name].dtype)
    return out
```

```python
from contextlib import ExitStack

import concourse.bass as bass
from concourse import mybir

ALU = mybir.AluOpType
ACT = mybir.ActivationFunctionType
F32 = mybir.dt.float32
BF16 = mybir.dt.bfloat16
I32 = mybir.dt.int32
AX_X = mybir.AxisListType.X

P = 128
D = 256
C = D // P
NB, L = 2, 2048
NH, DH = 16, 16
NS = 32
NE, FF = 16, 1024
J = FF // P
TG = 4
GT = TG * P
NG = NB * L // GT
GB = L // GT
KT = L // P
HR = TG * NH
TOP = 8
EPS = 1e-5
FIXES = NS - TOP
EB = 3
SCALE = DH ** -0.5


def build(nc, A, out):
    with ExitStack() as ctx:
        def sb(name, shape, dt=F32):
            return ctx.enter_context(nc.sbuf_tensor(name, shape, dt))

        def sem(name):
            return ctx.enter_context(nc.semaphore(name))

        bank = [ctx.enter_context(nc.psum_tensor(f"bank{i}", [P, 512], F32)) for i in range(8)]

        x = sb("x", [P, NB * KT, D])
        arena = sb("arena", [P, 14336])
        ynT = arena[:, 0:8192].rearrange("p (b c l) -> p b c l", b=NB, c=C)
        ring0 = arena[:, 8192:14336].rearrange("p (k n) -> p k n", k=3)
        work = sb("work", [P, 8192])
        s_all = work[:, 0:4096].rearrange("p (m k) -> p m k", m=2)
        yn = work[:, 4096:8192].rearrange("p (t d) -> p t d", d=D)
        scr1 = sb("scr1", [P, KT * 512])
        ring = (ring0, scr1[:, 0:6144].rearrange("p (k n) -> p k n", k=3), work[:, 0:6144].rearrange("p (k n) -> p k n", k=3))
        scr = tuple(a.rearrange("p (h j s) -> p h j s", h=NH, j=KT) for a in (arena[:, 4096:12288], scr1[:, :]))

        aWq, aWk, aWv, dWq, dWk = (
            work[:, 512 * i:512 * i + 512].rearrange("p (c d) -> p c d", c=C) for i in range(5))
        kp = work[0:NS, 2560:2816]
        b2 = work[0:NE, 2816:3072]
        aWo = sb("aWo", [P, C, D])
        sq = sb("sq", [NE, D])
        cWq, cWk, cWv, cWo = (scr1[:, 6144 + 512 * i:6656 + 512 * i].rearrange("p (c d) -> p c d", c=C) for i in range(4))

        def fold(at, n, parts=P):
            return work[0:parts, 4096 + at:4096 + at + n]

        aWqT = fold(0, 512).rearrange("p (m c q) -> p m c q", m=2, c=C)
        dWkT = fold(512, 512).rearrange("p (m c q) -> p m c q", m=2, c=C)
        bdK = fold(1024, 512).rearrange("p (m h s) -> p m h s", m=2, h=8)
        bdQ = fold(2048, 256).rearrange("p (m h s) -> p m h s", m=2, h=8)
        aKT = fold(2304, 64).rearrange("p (m s) -> p m s", m=2)
        aKT4 = fold(3488, 256).rearrange("p (m s) -> p m s", m=2)
        dQT = fold(2432, 32).rearrange("p (m s) -> p m s", m=2)
        brow = fold(2464, P, 18)
        bo3 = fold(2592, 512, 3).rearrange("p (a d) -> p a d", a=2)
        bvrow = fold(3104, D, 1)
        ones1 = fold(3360, P, 1)

        ident = sb("ident", [P, P])
        mask = sb("mask", [P, 8])
        masks = sb("masks", [P, 8])
        sel = sb("sel", [P, NE])
        ones3 = sb("ones3", [3, P], BF16)
        mhalf = sb("mhalf", [P, TG])
        rk = sb("rk", [P, TOP])
        miscT = sb("miscT", [P, 146])
        kpT = miscT[:, 0:64].rearrange("p (c s) -> p c s", c=C)
        sqT = miscT[:, 64:96].rearrange("p (c s) -> p c s", c=C)
        b2T = miscT[:, 96:128].rearrange("p (c s) -> p c s", c=C)
        bcol = miscT[:, 128:146].rearrange("p (v m) -> p v m", m=2)
        ABQ, ABK, ABV, DBQ, DBK, DBV, CBQ, CBK, CBV = range(9)
        bq3 = sb("bq3", [P, 2, 2, 3])
        Wz = sb("Wz", [P, C, 512])
        Wd = sb("Wd", [P, C, D])
        vrep = sb("vrep", [P, NH, DH])
        jmask = sb("jmask", [P, 2, 8])
        dconst = sb("dconst", [P, 2])
        zb3 = sb("zb3", [3, 512], BF16)
        ab3 = sb("ab3", [3, 512], BF16)
        cb3 = sb("cb3", [3, 512], BF16)

        stats = sb("stats", [P, 3, TG, 6])
        mv = sb("mv", [P, 3, TG, 2])
        veps = sb("veps", [P, 3, TG])
        rstd = sb("rstd", [P, 3, TG])
        xin = sb("xin", [P, TG, D])
        y = sb("y", [P, TG, D])
        yT = sb("yT", [P, C, GT])
        d = sb("d", [P, TG * 512])
        above = sb("above", [P, TG * 512], BF16)
        top = d[:, 0:HR * TOP].rearrange("p (r k) -> p r k", k=TOP)
        ratio = above[:, 0:2 * HR * TOP].bitcast(F32).rearrange("p (r k) -> p r k", k=TOP)
        tau = sb("tau", [P, HR])
        cnt = sb("cnt", [P, HR])
        exc = sb("exc", [P, HR])
        rcnt = sb("rcnt", [P, HR])
        tot = sb("tot", [P, 2])
        moved = sb("moved", [P, 32])
        movedT = sb("movedT", [P, 32])
        flag = sb("flag", [P, 1])
        flagi = sb("flagi", [P, 1], I32)

        bdh = sb("bdh", [P, TG, 2, P])
        aT = sb("aT", [P, 2, 512])
        hoT = sb("hoT", [P, 2, P])
        o = sb("o_buf", [P, TG, D])

        smax = sb("smax", [P, 2])
        nmax = sb("nmax", [P, 2])
        ssum = sb("ssum", [P, 2])
        rsum = sb("rsum", [P, 2])
        pT = aT
        dWv = d[:, 0:512].rearrange("p (c n) -> p c n", c=C)
        dWo = d[:, 512:1024].rearrange("p (c n) -> p c n", c=C)
        gn = y[:, 0:2, :]
        zm = y[:, 2, :].rearrange("p (m n) -> p m n", m=2)
        gT = yT[:, 0, :].rearrange("p (c m n) -> p c m n", c=C, m=2)
        slot = yT[0:NE, 1, 0:256]
        hid = yT[0:NE, 1, 256:512]
        lng = xin[0:NE, 0, :]
        lnb = xin[0:NE, 1, :]
        dbo = xin[0:NE, 2, :]
        b1 = xin[:, 3, 0:P]
        bg = xin[:, 3, P:2 * P]
        bT1 = y[:, 3, :].rearrange("p (e g j) -> p e g j", g=2, j=J)
        hT = sb("hT", [P, 2, NE])
        sstats = sb("sstats", [NE, 6])
        smv = sb("smv", [NE, 2])
        sveps = sb("sveps", [NE, 1])
        srstd = sb("srstd", [NE, 1])
        slotT = sb("slotT", [P, C, NB, NE])
        hidT = sb("hidT", [P, C, NB, NE])

        def over(at, n):
            return d[:, at:at + n]

        pre = over(0, 32).rearrange("p (g j b) -> p g j b", g=2, b=NB)
        gate = over(32, 32).rearrange("p (g j b) -> p g j b", g=2, b=NB)
        ug = over(352, 48).rearrange("p (q j b) -> p q j b", q=EB, b=NB)
        hcol = over(160, 192).rearrange("p (q c x) -> p q c x", q=EB, c=C)
        spare = above[:, :].bitcast(F32)
        ugT = (over(1024, 512), over(1536, 512), spare[:, 0:512])
        dn = spare[0:NB, 512:768]
        newT = over(96, 64).rearrange("p (c b e) -> p c b e", c=C, b=NB)
        cKT = over(160, 64).rearrange("p (m b e) -> p m b e", m=2, b=NB)
        cVT = over(224, 64).rearrange("p (m b e) -> p m b e", m=2, b=NB)
        cWqT = over(512, 512).rearrange("p (m c n) -> p m c n", m=2, c=C)
        cbK = over(1024, 512).rearrange("p (m b h e) -> p m b h e", m=2, b=NB, h=8)
        cbV = over(1536, 512).rearrange("p (m b h e) -> p m b h e", m=2, b=NB, h=8)
        Wc = scr1[:, 0:1024].rearrange("p (b c n) -> p b c n", b=NB, c=C)
        Vc = scr1[:, 1024:2048].rearrange("p (b m n) -> p b m n", b=NB, m=2)
        cin = work[:, 0:2048].rearrange("p (g c n) -> p g c n", g=2, c=C)
        prob = work[:, 2048:4096].rearrange("p (g t n) -> p g t n", g=2, t=TG)
        cpT = work[:, 4096:5120].rearrange("p (g n) -> p g n", g=2)
        co = work[:, 5120:7168].rearrange("p (g t n) -> p g t n", g=2, t=TG)
        cmax = work[:, 7168:7232]
        csum = work[:, 7232:7296]
        crs = work[:, 7296:7360]

        xs = A['L0_attn_query'].rearrange("b (p j) d -> p b j d", p=P)
        xt = A['L0_attn_query'].rearrange("b (t p) d -> p (b t) d", p=P)
        ot = out.rearrange("b (t p) d -> p (b t) d", p=P)
        w_in = sem("w_in")
        w_in2 = sem("w_in2")
        w_in3 = sem("w_in3")
        xin_in = sem("xin_in")
        x_in = sem("x_in")
        bd_ready = sem("bd_ready")
        h_ps = sem("h_ps")
        h_sb = sem("h_sb")
        consts = sem("consts")
        pe_part = sem("pe_part")
        dve_part = sem("dve_part")
        prep = sem("prep")
        stat = [sem(f"stat{k}") for k in range(3)]
        mean = [sem(f"mean{k}") for k in range(3)]
        vare = [sem(f"vare{k}") for k in range(3)]
        rst = [sem(f"rst{k}") for k in range(3)]
        y_ready = sem("y_ready")
        yT_ps = sem("yT_ps")
        yT_sb = sem("yT_sb")
        z_ps = sem("z_ps")
        z_sb = sem("z_sb")
        topped = sem("topped")
        cum = sem("cum")
        diff = sem("diff")
        relued = sem("relued")
        newton = sem("newton")
        fix = sem("fix")
        settled = sem("settled")
        a_ps = sem("a_ps")
        a_sb = sem("a_sb")
        o_ps = sem("o_ps")
        o_sb = sem("o_sb")
        o_norm = sem("o_norm")
        x_new = sem("x_new")
        yn_ready = sem("yn_ready")
        yn_copied = sem("yn_copied")
        ynT_ps = sem("ynT_ps")
        ynT_sb = sem("ynT_sb")
        s_ps = sem("s_ps")
        s_sb = sem("s_sb")
        maxed = sem("maxed")
        exped = sem("exped")
        pT_ps = sem("pT_ps")
        pT_sb = sem("pT_sb")
        g_ps = sem("g_ps")
        slots = sem("slots")
        smean = sem("smean")
        srst = sem("srst")
        e_in = [[sem(f"e_in{q}{k}") for k in range(3)] for q in range(EB)]
        up_ps = sem("up_ps")
        hbias = sem("hbias")
        ug_sb = sem("ug_sb")
        ugT_ps = sem("ugT_ps")
        pred = sem("pred")
        silued = sem("silued")
        hcol_ready = sem("hcol_ready")
        ug_ready = sem("ug_ready")
        down_ps = sem("down_ps")
        dn_sb = sem("dn_sb")
        dnT_ps = sem("dnT_ps")
        down_sb = sem("down_sb")
        c_in = sem("c_in")
        c_ps = sem("c_ps")
        c_max = sem("c_max")
        c_sub = sem("c_sub")
        c_exp = sem("c_exp")
        c_sum = sem("c_sum")
        c_rs = sem("c_rs")
        c_prob = sem("c_prob")
        c_pT_ps = sem("c_pT_ps")
        c_pT_sb = sem("c_pT_sb")
        co_ps = sem("co_ps")
        co_sb = sem("co_sb")
        c_stat = sem("c_stat")
        c_mean = sem("c_mean")
        c_vare = sem("c_vare")
        c_rst = sem("c_rst")
        c_norm = sem("c_norm")
        c_out = sem("c_out")
        stored = [sem(f"stored{q}") for q in range(2)]

        bT = bank[0:2]; bZ = bank[2:4]; bA = bank[4:6]
        psH = bank[6][:, 0:D]
        psO = bank[7][:, 0:D]
        N_W1, N_W2, N_W3 = 21, 7, 4
        (M_MISC, M_AQ, M_DK, M_KQ, M_WZ, M_ZB, M_V, M_WD) = range(1, 9)
        PREP = M_WD
        (D_GT, D_Z, D_H, D_SLOT, D_T) = range(1, 6)
        ND = D_T
        (S_G, S_GT, S_ZM, S_H, S_SLOT, S_T) = range(1, 7)
        MS = 6
        CP = PREP + 2 * ND
        CS = PREP + 2 * MS

        block = ctx.enter_context(nc.Block())

        @block.sync
        def _(sp):
            def load(i, b):
                sp.dma_start(xin[:, :, :], xs[:, b, bass.ds(i * TG - b * KT, TG), :]).then_inc(xin_in, 16)

            load(0, 0)
            sp.dma_start(x[:, :, :], xt).then_inc(x_in, 16)
            for b in range(NB):
                with sp.Fori(1 if b == 0 else GB, (b + 1) * GB) as i:
                    sp.wait_ge(y_ready, i * TG)
                    load(i, b)

            sp.wait_ge(settled, NG)
            for dst, src in ((lng, A['L0_ffn_e_ln_g']), (lnb, A['L0_ffn_e_ln_b']),
                             (dbo, A['L0_ffn_d_bo'].rearrange("(o d) -> o d", o=1).broadcast_to([NE, D])),
                             (dWv, A['L0_ffn_d_Wv'].rearrange("(p c) n -> p c n", c=C)),
                             (dWo, A['L0_ffn_d_Wo'].rearrange("(c p) n -> p c n", c=C)),
                             (b1, A['L0_ffn_e_b1'].rearrange("e (j p) -> (e j) p", p=P)),
                             (bg, A['L0_ffn_e_bg'].rearrange("e (j p) -> (e j) p", p=P))):
                sp.dma_start(dst, src).then_inc(w_in2, 16)

            def expert(e, q, k):
                dst = ring[q][:, k, :]
                if k == 2:
                    dst = dst.rearrange("p (j d) -> p j d", j=J)
                if k < 2:
                    src = A[('L0_ffn_e_W1', 'L0_ffn_e_Wg')[k]].rearrange("e (p c) f -> p e (c f)", c=C)[:, e, :]
                else:
                    src = A['L0_ffn_e_W2'].rearrange("e (j p) d -> p e j d", j=J)[:, e, :, :]
                sp.dma_start(dst, src).then_inc(e_in[q][k], 16)

            sp.wait_ge(a_ps, KT)
            for k in range(3):
                expert(0, 0, k)
            sp.wait_ge(a_ps, 2 * KT)
            for w, name, form in ((cWq, 'L0_ffn_c_Wq', "(p c) n -> p c n"), (cWk, 'L0_ffn_c_Wk', "(p c) n -> p c n"),
                                  (cWv, 'L0_ffn_c_Wv', "(p c) n -> p c n"), (cWo, 'L0_ffn_c_Wo', "(c p) n -> p c n")):
                sp.dma_start(w, A[name].rearrange(form, c=C)).then_inc(w_in3, 16)
            for k in range(3):
                expert(1, 1, k)
            sp.wait_ge(g_ps, 2 * (KT // 2))
            for k in range(3):
                expert(2, 2, k)

            def refill(it, q):
                for k in range(3):
                    if k < 2:
                        sp.wait_ge(up_ps, it * 6 + (2 * (q - 3) + k + 1))
                    else:
                        sp.wait_ge(down_ps, it * 3 + (q - 2))
                    expert(it * 3 + q, q, k)

            with sp.Fori(1, NE // EB) as it:
                for q in range(EB):
                    refill(it, q)
            for q in range(NE % EB):
                refill(NE // EB, q)

            def store(j, q):
                sp.wait_ge(c_out, j + 1)
                sp.dma_start(ot[:, bass.ds(j * TG, TG), :], co[:, q, :, :]).then_inc(stored[q], 16)

            with sp.Fori(0, NG // 2) as h:
                store(h * 2, 0)
                store(h * 2 + 1, 1)
            sp.wait_ge(stored[0], 16 * NG // 2)
            sp.wait_ge(stored[1], 16 * NG // 2)

        @block.gpsimd
        def _(pool):
            pool.memset(ident[:, :], 0.0).then_inc(consts, 1)
            pool.memset(mask[:, :], 1.0).then_inc(consts, 1)
            pool.memset(ones3[:, :], 1.0).then_inc(consts, 1)
            pool.memset(mhalf[:, :], -0.5).then_inc(consts, 1)
            pool.memset(moved[:, :], 0.0).then_inc(consts, 1)
            for k in range(TOP):
                pool.memset(rk[:, k:k + 1], 1.0 / (k + 1)).then_inc(consts, 1)
            pool.memset(jmask[:, :, :], 1.0).then_inc(consts, 1)
            pool.memset(ones1, 1.0).then_inc(consts, 1)
            n = 7 + TOP
            pool.wait_ge(consts, n)
            pool.affine_select(out=ident[:, :], in_=ident[:, :], compare_op=ALU.not_equal, fill=1.0, base=0,
                               pattern=[[-1, P]], channel_multiplier=1).then_inc(consts, 1)
            pool.affine_select(out=mask[:, :], in_=mask[:, :], compare_op=ALU.is_ge, fill=0.0, base=0,
                               pattern=[[-DH, 8]], channel_multiplier=1).then_inc(consts, 1)
            pool.wait_ge(consts, n + 2)
            pool.affine_select(out=mask[:, :], in_=mask[:, :], compare_op=ALU.is_ge, fill=0.0, base=DH - 1,
                               pattern=[[DH, 8]], channel_multiplier=-1).then_inc(consts, 1)
            pool.wait_ge(consts, n + 3)
            pool.tensor_scalar(masks[:, :], mask[:, :], SCALE, None, ALU.mult).then_inc(consts, 1)
            pool.affine_select(out=jmask[:, :, :], in_=jmask[:, :, :], compare_op=ALU.is_ge, fill=0.0, base=0,
                               pattern=[[P, 2], [-NS, 8]], channel_multiplier=1).then_inc(consts, 1)
            pool.wait_ge(consts, n + 5)
            pool.affine_select(out=jmask[:, :, :], in_=jmask[:, :, :], compare_op=ALU.is_ge, fill=0.0, base=NS - 1,
                               pattern=[[-P, 2], [NS, 8]], channel_multiplier=-1).then_inc(consts, 1)

            def hold(s, value):
                pool.wait_ge(s, value)
                pool.nop(nofuse=True)

            def root(k, i):
                hold(mean[k], i * TG + TG)
                pool.tensor_scalar(veps[:, k, :], mv[:, k, :, 1], EPS, None, ALU.add).then_inc(vare[k], 1)
                pool.wait_ge(vare[k], i + 1)
                pool.tensor_tensor(rstd[:, k, :], veps[:, k, :], mhalf[:, :], ALU.pow).then_inc(rst[k], 1)

            def outs(g, b):
                for t in range(TG):
                    if not (isinstance(g, int) and g == 0):
                        pool.wait_ge(h_ps, g * TG + (t + 1 - TG))
                    pool.tensor_tensor(bdh[:, t, :, :].rearrange("p a (j e) -> p (a j) e", e=DH),
                                       vrep[:, bass.ds(g * TG + (t - b * NH), 1), :].broadcast_to([P, 16, DH]),
                                       jmask[:, :, :].rearrange("p a j -> p (a j)").unsqueeze(2).broadcast_to([P, 16, DH]),
                                       ALU.mult).then_inc(bd_ready, 1)
                root(1, g)
                root(2, g)
                pool.wait_ge(yn_ready, g * TG + TG)
                pool.tensor_copy(yn[:, bass.ds(g * TG - b * KT, TG), :], o[:, :, :]).then_inc(yn_copied, 1)

            def slot_root(b):
                pool.wait_ge(smean, 2 * b + 2)
                pool.tensor_scalar(sveps[:, :], smv[:, 1:2], EPS, None, ALU.add).then_inc(srst, 1)
                pool.wait_ge(srst, 2 * b + 1)
                pool.tensor_tensor(srstd[:, :], sveps[:, :], mhalf[0:NE, 0:1], ALU.pow).then_inc(srst, 1)

            with pool.Fori(0, GB) as i:
                root(0, i)
            pool.wait_ge(dve_part, PREP)
            root(0, GB)
            root(0, GB + 1)
            outs(0, 0)
            with pool.Fori(1, GB - 1) as g:
                root(0, g + GB + 1)
                outs(g, 0)
            outs(GB - 1, 0)
            slot_root(0)
            with pool.Fori(GB, NG) as g:
                outs(g, 1)
            slot_root(1)

            def stage(j, b, q):
                pool.tensor_copy(cin[:, q, :, :], ynT[:, b, :, bass.ds(j * GT - b * L, GT)]).then_inc(c_in, 1)

            def weigh(j, q):
                pool.wait_ge(c_rs, j + 1)
                pv = prob[:, q, :, :].rearrange("p t (h e) -> p (t h) e", e=NE)
                pool.tensor_tensor(pv, pv, crs[:, :].unsqueeze(2).broadcast_to([P, HR, NE]), ALU.mult)\
                    .then_inc(c_prob, 1)

            def finish(j, q):
                hold(c_mean, j * TG + TG)
                pool.tensor_scalar(veps[:, 0, :], mv[:, 0, :, 1], EPS, None, ALU.add).then_inc(c_vare, 1)
                pool.wait_ge(c_vare, j + 1)
                pool.tensor_tensor(rstd[:, 0, :], veps[:, 0, :], mhalf[:, :], ALU.pow).then_inc(c_rst, 1)
                pool.wait_ge(c_norm, j * TG + TG)
                pool.tensor_tensor(co[:, q, :, :], co[:, q, :, :], x[:, bass.ds(j * TG, TG), :], ALU.add)\
                    .then_inc(c_out, 1)

            def lay_by(it, q, first=False):
                if not first:
                    pool.wait_ge(up_ps, it * 6 + 2 * (q - 2))
                pool.tensor_copy(hcol[:, q, :, 0:NB], hidT[:, :, :, bass.ds(it * 3 + q, 1)].rearrange("p c b o -> p c (b o)"))\
                    .then_inc(hcol_ready, 1)

            pool.wait_ge(dve_part, PREP + 2 * MS)
            pool.memset(hcol, 0.0).then_inc(consts, 1)
            pool.wait_ge(consts, 14 + TOP)
            for q in range(EB):
                lay_by(0, q, first=True)
            with pool.Fori(1, NE // EB) as it:
                for q in range(EB):
                    lay_by(it, q)
            for q in range(NE % EB):
                lay_by(NE // EB, q)

            pool.wait_ge(down_ps, NE - 1)
            stage(0, 0, 0)
            stage(1, 0, 1)
            weigh(0, 0)

            def combine(j, b, q, more=True):
                if more:
                    pool.wait_ge(c_ps, j * 2)
                    stage(j + 1, b, 1 - q)
                weigh(j, q)
                finish(j - 1, 1 - q)

            combine(1, 0, 1)
            combine(2, 0, 0)
            with pool.Fori(1, NG // 2 - 1) as h:
                combine(h * 2 + 1, 1, 1)
                combine(h * 2 + 2, 1, 0)
            combine(NG - 1, 1, 1, more=False)
            finish(NG - 1, 1)

        @block.scalar
        def _(act):
            first_lot = [
                (kp, A['L0_attn_key_param'][0]), (sq[:, :], A['L0_ffn_slot_query'][0]), (b2, A['L0_ffn_e_b2']),
                (bvrow, A['L0_attn_bv'].rearrange("(o d) -> o d", o=1))]
            for v, name in enumerate(('L0_attn_bq', 'L0_attn_bk', 'L0_attn_bv', 'L0_ffn_d_bq', 'L0_ffn_d_bk',
                                      'L0_ffn_d_bv', 'L0_ffn_c_bq', 'L0_ffn_c_bk', 'L0_ffn_c_bv')):
                first_lot.append((brow[2 * v:2 * v + 2, :], A[name].rearrange("(m p) -> m p", p=P)))
            for a, name in ((0, 'L0_attn_bo'), (1, 'L0_ffn_c_bo')):
                first_lot.append((bo3[:, a, :], A[name].rearrange("(o d) -> o d", o=1).broadcast_to([3, D])))
            for w, name, form in ((aWq, 'L0_attn_Wq', "(p c) n -> p c n"), (aWk, 'L0_attn_Wk', "(p c) n -> p c n"),
                                  (aWv, 'L0_attn_Wv', "(c p) n -> p c n"), (aWo[:, :, :], 'L0_attn_Wo', "(c p) n -> p c n"),
                                  (dWq, 'L0_ffn_d_Wq', "(p c) n -> p c n"), (dWk, 'L0_ffn_d_Wk', "(p c) n -> p c n")):
                first_lot.append((w, A[name].rearrange(form, c=C)))
            assert len(first_lot) == N_W1
            for dst, src in first_lot:
                act.dma_start(dst, src).then_inc(w_in, 16)

            def put_yT(i, guard=True):
                act.wait_ge(yT_ps, i + 1)
                if guard:
                    act.wait_ge(z_ps, i * TG)
                for c in range(C):
                    act.activation(yT[:, c, :], bT[c][:, :], ACT.Copy).then_inc(yT_sb, 1)

            def put_scores(i, b):
                for t in range(TG):
                    act.wait_ge(z_ps, i * TG + (t + 1))
                    act.activation(scr[b][:, :, bass.ds(i * TG + (t - b * KT), 1), :].rearrange("p h o s -> p (h o) s"),
                                   bZ[t % 2][:, :].rearrange("p (h s) -> p h s", h=NH), ACT.Copy).then_inc(z_sb, 1)

            def clamp(i):
                act.wait_ge(diff, i + 1)
                act.activation(d[:, :], d[:, :], ACT.Relu).then_inc(relued, 1)

            def put_heads(g, first=False):
                for t in range(TG + 2):
                    if t < TG:
                        act.wait_ge(a_ps, g * TG + (t + 1))
                        if not (first and t < 2):
                            act.wait_ge(h_ps, g * TG + (t - 1))
                        act.activation(aT[:, t % 2, :], bA[t % 2][:, :], ACT.Relu).then_inc(a_sb, 1)
                    if 1 <= t < TG + 1:
                        act.wait_ge(h_ps, g * TG + t)
                        if not (first and t == 1):
                            act.wait_ge(o_ps, g * TG + (t - 1))
                        act.activation(hoT[:, :, :].rearrange("p m n -> p (m n)"), psH, ACT.Copy).then_inc(h_sb, 1)
                    if t >= 2:
                        act.wait_ge(o_ps, g * TG + (t - 1))
                        if t == 2 and not first:
                            act.wait_ge(yn_copied, g)
                            act.wait_ge(ynT_ps, g)
                        act.activation(o[:, t - 2, :], psO, ACT.Copy).then_inc(o_sb, 1)

            def put_norm(g, b):
                act.wait_ge(ynT_ps, g + 1)
                for c in range(C):
                    act.activation(ynT[:, b, c, bass.ds(g * GT - b * L, GT)], bT[c][:, :], ACT.Copy).then_inc(ynT_sb, 1)
                for m in range(2):
                    act.wait_ge(s_ps, g * 2 + (m + 1))
                    act.activation(s_all[:, m, bass.ds(g * GT - b * L, GT)], bA[m][:, :], ACT.Identity,
                                   bias=dconst[:, m:m + 1]).then_inc(s_sb, 1)

            def dispatch(b):
                for m in range(2):
                    act.wait_ge(maxed, 4 * b + 4)
                    act.activation(s_all[:, m, :], s_all[:, m, :], ACT.Exp, bias=nmax[:, m:m + 1],
                                   accum_out=ssum[:, m:m + 1]).then_inc(exped, 1)
                for k in range(KT // 2):
                    n = b * (KT // 2) + k
                    act.wait_ge(pT_ps, n + 1)
                    if n >= 2:
                        act.wait_ge(g_ps, n - 1)
                    act.activation(pT[:, k % 2, :], bA[k % 2][:, :], ACT.Copy).then_inc(pT_sb, 1)

            put_yT(0, guard=False)
            with act.Fori(0, GB) as i:
                put_scores(i, 0)
                put_yT(i + 1)
                clamp(i)
            put_scores(GB, 1)
            put_heads(0, first=True)
            put_yT(GB + 1)
            clamp(GB)
            put_norm(0, 0)
            with act.Fori(GB + 1, NG - 1) as i:
                put_scores(i, 1)
                put_heads(i - GB)
                put_yT(i + 1)
                clamp(i)
                put_norm(i - GB, 0)
            put_scores(NG - 1, 1)
            put_heads(GB - 1)
            clamp(NG - 1)
            put_norm(GB - 1, 0)
            dispatch(0)
            with act.Fori(GB, NG) as g:
                put_heads(g)
                put_norm(g, 1)
            dispatch(1)

            with act.Fori(0, NE) as e:
                act.wait_ge(pred, e + 1)
                act.activation(gate, pre, ACT.Silu).then_inc(silued, 1)

            def exps(j, q):
                act.wait_ge(c_sub, j * 2 + 2)
                act.activation(prob[:, q, :, :], prob[:, q, :, :], ACT.Exp).then_inc(c_exp, 1)

            def outs(j, q, guard=True):
                for u in range(2):
                    act.wait_ge(c_pT_ps, j * 2 + (u + 1))
                    act.activation(cpT[:, u, :], bA[u][:, :], ACT.Copy).then_inc(c_pT_sb, 1)
                for u in range(2):
                    act.wait_ge(co_ps, j * 2 + (u + 1))
                    if guard and u == 0:
                        act.wait_ge(stored[q], (j - q) * 8)
                    act.activation(co[:, q, 2 * u:2 * u + 2, :], bank[6 + u][:, :], ACT.Copy).then_inc(co_sb, 1)

            exps(0, 0)
            exps(1, 1)
            outs(0, 0, guard=False)
            exps(2, 0)
            outs(1, 1, guard=False)
            with act.Fori(1, NG // 2 - 1) as h:
                exps(h * 2 + 1, 1)
                outs(h * 2, 0)
                exps(h * 2 + 2, 0)
                outs(h * 2 + 1, 1)
            exps(NG - 1, 1)
            outs(NG - 2, 0)
            outs(NG - 1, 1)

        @block.tensor
        def _(pe):
            pe.wait_ge(consts, 13 + TOP)
            pe.wait_ge(w_in, 16 * N_W1)
            for c in range(C):
                pe.transpose(bank[0][:, c * NS:(c + 1) * NS], kp[:, c::C], ident[0:NS, 0:NS])
                pe.transpose(bank[0][:, 64 + c * NE:64 + (c + 1) * NE], sq[:, c::C], ident[0:NE, 0:NE])
                pe.transpose(bank[0][:, 96 + c * NE:96 + (c + 1) * NE], b2[:, c::C], ident[0:NE, 0:NE])
            pe.transpose(bank[0][:, 128:146], brow, ident[0:18, 0:18]).then_inc(pe_part, 1)
            for w, bk in ((aWq, 1), (dWk, 2)):
                for m in range(2):
                    for c in range(C):
                        mm = pe.transpose(bank[bk][:, (m * 2 + c) * P:(m * 2 + c + 1) * P], w[:, c, m * P:(m + 1) * P],
                                          ident[:, :])
                mm.then_inc(pe_part, 1)
            pe.wait_ge(dve_part, M_MISC)
            for m in range(2):
                for c in range(C):
                    pe.matmul(bank[4][:, m * NS:(m + 1) * NS], aWk[:, c, m * P:(m + 1) * P], kpT[:, c, :],
                              start=(c == 0), stop=(c == 1))
            for m in range(2):
                for c in range(C):
                    mm = pe.matmul(bank[4][:, 64 + m * NE:64 + (m + 1) * NE], dWq[:, c, m * P:(m + 1) * P], sqT[:, c, :],
                                   start=(c == 0), stop=(c == 1))
            mm.then_inc(pe_part, 1)
            pe.wait_ge(dve_part, M_KQ)
            for c in range(C):
                for m in range(2):
                    mm = pe.matmul(bank[c][:, m * 256:(m + 1) * 256], aWqT[:, m, c, :], bdK[:, m, :, :],
                                   start=True, stop=True)
            mm.then_inc(pe_part, 1)
            for m in range(2):
                mm = pe.matmul(bank[6][0:3, m * 256:(m + 1) * 256], bq3[:, 0, m, :], bdK[:, m, :, :], start=True, stop=True)
            mm.then_inc(pe_part, 1)
            for m in range(2):
                pe.matmul(bank[5][:, 0:D], aKT4[:, m, :], aWv[:, m, :], start=(m == 0), stop=False)
            pe.matmul(bank[5][:, 0:D], ones1, bvrow, start=False, stop=True).then_inc(pe_part, 1)
            for c in range(C):
                for m in range(2):
                    pe.matmul(bank[4][:, c * D + m * P:c * D + (m + 1) * P], dWkT[:, m, c, :], bdQ[:, m, :, :],
                              start=True, stop=True)
            for m in range(2):
                mm = pe.matmul(bank[7][:, m:m + 1], bdQ[:, m, :, :], bcol[:, DBK, m:m + 1], start=True, stop=True)
            mm.then_inc(pe_part, 1)

            def turn_y(i):
                pe.wait_ge(y_ready, i * TG + TG)
                if i > GB + 1:
                    pe.wait_ge(ynT_sb, 2 * (i - GB - 1))
                elif i > 0:
                    pe.wait_ge(yT_sb, 2 * i)
                for t in range(TG):
                    for c in range(C):
                        mm = pe.transpose(bT[c][:, t * P:(t + 1) * P], y[:, t, c::C], ident[:, :])
                mm.then_inc(yT_ps, 1)

            def scores_of(i):
                pe.wait_ge(yT_sb, i * 2 + 2)
                for t in range(TG):
                    n = i * TG + t
                    if n >= 2:
                        pe.wait_ge(topped, n - 1)
                    pe.matmul(bZ[t % 2][:, :], ones3[:, :], zb3[:, :], start=True, stop=False)
                    for c in range(C):
                        mm = pe.matmul(bZ[t % 2][:, :], yT[:, c, t * P:(t + 1) * P], Wz[:, c, :],
                                       start=False, stop=(c == C - 1))
                    mm.then_inc(z_ps, 1)

            def heads_of(g):
                b = g // GB
                pe.wait_ge(settled, GB * (b + 1))
                if g > 0:
                    pe.wait_ge(s_sb, 2 * g)
                w = scr[b].rearrange("p h j s -> p h (j s)")
                for t in range(TG + 2):
                    n = g * TG + t
                    if t < TG:
                        if t >= 2:
                            pe.wait_ge(a_sb, n - 1)
                        for k in range(4):
                            mm = pe.transpose(bA[t % 2][:, k * P:(k + 1) * P], w[:, n - b * NH, k * P:(k + 1) * P], ident[:, :])
                        mm.then_inc(a_ps, 1)
                    if 1 <= t < TG + 1:
                        pe.wait_ge(a_sb, n)
                        pe.wait_ge(bd_ready, n)
                        if n >= 2:
                            pe.wait_ge(h_sb, n - 1)
                        for m in range(2):
                            for half in range(2):
                                mm = pe.matmul(psH[:, m * P:(m + 1) * P], bdh[:, t - 1, half, :],
                                               aT[:, (t - 1) % 2, (2 * m + half) * P:(2 * m + half + 1) * P],
                                               start=(half == 0), stop=(half == 1))
                        mm.then_inc(h_ps, 1)
                    if t >= 2:
                        pe.wait_ge(h_sb, n - 1)
                        if n >= 3:
                            pe.wait_ge(o_sb, n - 2)
                        pe.matmul(psO, ones3[:, :], ab3[:, 0:D], start=True, stop=False)
                        for m in range(2):
                            mm = pe.matmul(psO, hoT[:, m, :], aWo[:, m, :], start=False, stop=(m == 1))
                        mm.then_inc(o_ps, 1)

            def norm_of(g):
                pe.wait_ge(yn_ready, (g + 1) * TG)
                if g < GB - 1:
                    pe.wait_ge(yT_sb, 2 * (g + GB + 2))
                elif g == GB - 1:
                    pe.wait_ge(yT_sb, 2 * NG)
                    pe.wait_ge(ynT_sb, 2 * g)
                else:
                    pe.wait_ge(ynT_sb, 2 * g)
                for t in range(TG):
                    for c in range(C):
                        mm = pe.transpose(bT[c][:, t * P:(t + 1) * P], o[:, t, c::C], ident[:, :])
                mm.then_inc(ynT_ps, 1)
                b = g // GB
                pe.wait_ge(ynT_sb, 2 * (g + 1))
                for m in range(2):
                    for c in range(C):
                        mm = pe.matmul(bA[m][:, :], Wd[:, c, m * P:(m + 1) * P], ynT[:, b, c, (g % GB) * GT:(g % GB + 1) * GT],
                                       start=(c == 0), stop=(c == C - 1))
                    mm.then_inc(s_ps, 1)

            def dispatch(b):
                pe.wait_ge(s_sb, 2 * GB * (b + 1))
                pe.wait_ge(o_sb, KT * (b + 1))
                pe.wait_ge(yn_copied, GB * (b + 1))
                pe.wait_ge(exped, 2 * b + 2)
                for k in range(KT // 2 + 1):
                    if k < KT // 2:
                        n = b * (KT // 2) + k
                        if k >= 2:
                            pe.wait_ge(pT_sb, n - 1)
                        for u in range(2):
                            for m in range(2):
                                mm = pe.transpose(bA[k % 2][:, (u * 2 + m) * P:(u * 2 + m + 1) * P],
                                                  s_all[:, m, (2 * k + u) * P:(2 * k + u + 1) * P], ident[:, :])
                        mm.then_inc(pT_ps, 1)
                    if k >= 1:
                        pe.wait_ge(pT_sb, b * (KT // 2) + k)
                        for u in range(2):
                            kt = 2 * (k - 1) + u
                            for m in range(2):
                                mm = pe.matmul(bank[6 + m][:, 0:D], pT[:, (k - 1) % 2, (u * 2 + m) * P:(u * 2 + m + 1) * P],
                                               yn[:, kt, :], start=(kt == 0), stop=(kt == KT - 1))
                        mm.then_inc(g_ps, 1)
                s0 = PREP + b * MS
                pe.wait_ge(dve_part, s0 + S_G)
                for c in range(C):
                    for m in range(2):
                        mm = pe.transpose(bA[0][:, (c * 2 + m) * P:(c * 2 + m + 1) * P], gn[:, m, c::C], ident[:, :])
                mm.then_inc(pe_part, 1)
                pe.wait_ge(dve_part, s0 + S_GT)
                for m in range(2):
                    for c in range(C):
                        mm = pe.matmul(bA[1][:, m * P:(m + 1) * P], gT[:, c, m, :], dWv[:, c, m * P:(m + 1) * P],
                                       start=(c == 0), stop=(c == C - 1))
                mm.then_inc(pe_part, 1)
                pe.wait_ge(dve_part, s0 + S_ZM)
                for m in range(2):
                    mm = pe.matmul(bA[0][:, m * NE:(m + 1) * NE], zm[:, m, :], sel[:, :], start=True, stop=True)
                mm.then_inc(pe_part, 1)
                pe.wait_ge(dve_part, s0 + S_H)
                for m in range(2):
                    mm = pe.matmul(bA[1][0:NE, 0:D], hT[:, m, :], dWo[:, m, :], start=(m == 0), stop=(m == 1))
                mm.then_inc(pe_part, 1)
                pe.wait_ge(dve_part, s0 + S_SLOT)
                for c in range(C):
                    pe.transpose(bA[0][:, c * NE:(c + 1) * NE], slot[:, c::C], ident[0:NE, 0:NE])
                    mm = pe.transpose(bA[0][:, 32 + c * NE:32 + (c + 1) * NE], hid[:, c::C], ident[0:NE, 0:NE])
                mm.then_inc(pe_part, 1)

            pe.wait_ge(dve_part, PREP)
            turn_y(0)
            for i in range(GB):
                scores_of(i)
                turn_y(i + 1)
            for i in range(GB, NG):
                scores_of(i)
                heads_of(i - GB)
                if i + 1 < NG:
                    turn_y(i + 1)
                norm_of(i - GB)
            pe.wait_ge(w_in2, 16 * N_W2)
            dispatch(0)
            pe.wait_ge(dve_part, PREP + MS)
            for g in range(GB, NG):
                heads_of(g)
                norm_of(g)
            dispatch(1)

            pe.wait_ge(w_in3, 16 * N_W3)
            for m in range(2):
                for c in range(C):
                    mm = pe.transpose(bank[6][:, (m * 2 + c) * P:(m * 2 + c + 1) * P], cWq[:, c, m * P:(m + 1) * P], ident[:, :])
            for g, rows_ in ((0, b1), (1, bg)):
                mm = pe.transpose(bank[7][:, g * P:(g + 1) * P], rows_, ident[:, :])
            mm.then_inc(pe_part, 1)

            pe.wait_ge(dve_part, PREP + 2 * MS)

            def grow(e, it, q, g, recent=True):
                if g == 0:
                    pe.wait_ge(hcol_ready, e + 1)
                    if recent:
                        pe.wait_ge(ug_sb, e - 2)
                pe.wait_ge(e_in[q][g], it * 16 + 16)
                for c in range(C):
                    for half in range(2):
                        k = 2 * g + half
                        mm = pe.matmul(bank[q][32 * k:32 * k + 32, :], hcol[:, q, c, :],
                                       ring[q][:, g, c * FF + half * 512:c * FF + (half + 1) * 512],
                                       start=(c == 0), stop=(c == C - 1))
                mm.then_inc(up_ps, 1)

            def turn_up(e, q):
                pe.wait_ge(ug_sb, e + 1)
                for j in range(4):
                    mm = pe.transpose(bank[3 + q][:, j * P:(j + 1) * P], ugT[q][:, j * P:(j + 1) * P], ident[:, :])
                mm.then_inc(ugT_ps, 1)

            def turn_down(e, first=False):
                pe.wait_ge(dn_sb, e + 1)
                if not first:
                    pe.wait_ge(down_sb, e)
                pe.nop(nofuse=True)
                for c in range(C):
                    mm = pe.transpose(bank[7][:, c * NB:(c + 1) * NB], dn[:, c::C], ident[0:NB, 0:NB])
                mm.then_inc(dnT_ps, 1)

            def shrink(e, it, q):
                pe.wait_ge(e_in[q][2], it * 16 + 16)
                pe.wait_ge(ug_ready, e + 1)
                for j in range(J):
                    mm = pe.matmul(bank[6][0:NB, 0:D], ug[:, q, j, :], ring[q][:, 2, j * D:(j + 1) * D],
                                   start=(j == 0), stop=(j == J - 1))
                mm.then_inc(down_ps, 1)

            def expert(h, k, first=False, last=False, recent=True):
                e, q, n = h * 3 + k, k % 3, (k + 1) % 3
                if not last:
                    grow(e + 1, h + (k + 1) // 3, n, 0, recent)
                turn_up(e, q)
                if not first:
                    turn_down(e - 1, first=recent is False and k == 1)
                if not last:
                    grow(e + 1, h + (k + 1) // 3, n, 1, recent)
                shrink(e, h + k // 3, q)

            pe.wait_ge(hbias, 1)
            grow(0, 0, 0, 0, recent=False)
            grow(0, 0, 0, 1, recent=False)
            expert(0, 0, first=True, recent=False)
            expert(0, 1, recent=False)
            with pe.Fori(0, 4) as h:
                for k in range(2, 5):
                    expert(h, k)
            expert(4, 2)
            expert(4, 3, last=True)
            turn_down(NE - 1)

            pe.wait_ge(down_sb, NE)
            for w, at in ((cWk, 0), (cWv, 64)):
                for m in range(2):
                    for c in range(C):
                        mm = pe.matmul(bank[0][:, at + m * 32:at + (m + 1) * 32], w[:, c, m * P:(m + 1) * P],
                                       newT[:, c, :, :], start=(c == 0), stop=(c == C - 1))
            mm.then_inc(pe_part, 1)
            pe.wait_ge(dve_part, CS + 1)
            for b in range(NB):
                for c in range(C):
                    for m in range(2):
                        pe.matmul(bank[1 + b][:, c * D + m * P:c * D + (m + 1) * P], cWqT[:, m, c, :], cbK[:, m, b, :, :],
                                  start=True, stop=True)
                for m in range(2):
                    pe.matmul(bank[3 + b][:, m * D:(m + 1) * D], cbV[:, m, b, :, :], cWo[:, m, :], start=True, stop=True)
                for m in range(2):
                    mm = pe.matmul(bank[5][0:3, b * D + m * P:b * D + (m + 1) * P], bq3[:, 1, m, :], cbK[:, m, b, :, :],
                                   start=True, stop=True)
            mm.then_inc(pe_part, 1)
            pe.wait_ge(dve_part, CS + 2)

            def scores(j, q, b, first=False):
                pe.wait_ge(c_in, j + 1)
                for t in range(TG):
                    u = t // 2
                    if t % 2 == 0 and not first:
                        pe.wait_ge(c_sub, j * 2 + (u - 1))
                    ps = bank[u][:, (t % 2) * D:(t % 2 + 1) * D]
                    pe.matmul(ps, ones3[:, :], cb3[:, b * D:(b + 1) * D], start=True, stop=False)
                    for c in range(C):
                        mm = pe.matmul(ps, cin[:, q, c, t * P:(t + 1) * P], Wc[:, b, c, :], start=False, stop=(c == C - 1))
                    if t % 2:
                        mm.then_inc(c_ps, 1)

            def outputs(j, q, b, first=False):
                pe.wait_ge(c_prob, j + 1)
                for u in range(2):
                    if not first:
                        pe.wait_ge(c_pT_sb, j * 2 + (u - 1))
                    for v in range(2):
                        for m in range(2):
                            mm = pe.transpose(bA[u][:, (v * 2 + m) * P:(v * 2 + m + 1) * P],
                                              prob[:, q, 2 * u + v, m * P:(m + 1) * P], ident[:, :])
                    mm.then_inc(c_pT_ps, 1)
                for u in range(2):
                    pe.wait_ge(c_pT_sb, j * 2 + (u + 1))
                    if not first:
                        pe.wait_ge(co_sb, j * 2 + (u - 1))
                    for v in range(2):
                        ps = bank[6 + u][:, v * D:(v + 1) * D]
                        pe.matmul(ps, ones3[:, :], ab3[:, D:2 * D], start=True, stop=False)
                        for m in range(2):
                            mm = pe.matmul(ps, cpT[:, u, (v * 2 + m) * P:(v * 2 + m + 1) * P], Vc[:, b, m, :],
                                           start=False, stop=(m == 1))
                    mm.then_inc(co_ps, 1)

            scores(0, 0, 0, first=True)
            scores(1, 1, 0)
            outputs(0, 0, 0, first=True)
            scores(2, 0, 0)
            outputs(1, 1, 0)
            scores(3, 1, 0)
            outputs(2, 0, 0)
            scores(4, 0, 1)
            outputs(3, 1, 0)
            with pe.Fori(2, NG // 2 - 1) as h:
                scores(h * 2 + 1, 1, 1)
                outputs(h * 2, 0, 1)
                scores(h * 2 + 2, 0, 1)
                outputs(h * 2 + 1, 1, 1)
            scores(NG - 1, 1, 1)
            outputs(NG - 2, 0, 1)
            outputs(NG - 1, 1, 1)

        @block.vector
        def _(v):
            steps = [0]

            def hold(s, value):
                v.wait_ge(s, value)
                v.nop(nofuse=True)

            def own(ins, wait=True):
                steps[0] += 1
                ins.then_inc(prep, 1)
                if wait:
                    v.wait_ge(prep, steps[0])

            def split3(dst, src):
                h = aT[0:3, :, :].rearrange("p a n -> p (a n)").bitcast(BF16)
                hs = [h[:, 512 * k:512 * (k + 1)] for k in range(3)]
                r = o[0:3, :, :].rearrange("p t n -> p (t n)")
                r1, r2 = r[:, 0:512], r[:, 512:1024]
                t0 = y[0:3, :, :].rearrange("p t n -> p (t n)")[:, 0:512]
                t1 = y[0:3, :, :].rearrange("p t n -> p (t n)")[:, 512:1024]
                own(v.tensor_copy(hs[0], src))
                own(v.tensor_tensor(r1, src, hs[0], ALU.subtract))
                own(v.tensor_copy(hs[1], r1))
                own(v.tensor_tensor(r2, r1, hs[1], ALU.subtract))
                own(v.tensor_copy(hs[2], r2))
                own(v.tensor_scalar(t0, hs[0], ident[0:3, 0:1], None, ALU.mult))
                own(v.scalar_tensor_tensor(out=t1, in0=hs[1], scalar=ident[0:3, 1:2], in1=t0, op0=ALU.mult, op1=ALU.add))
                return v.scalar_tensor_tensor(out=dst, in0=hs[2], scalar=ident[0:3, 2:3], in1=t1, op0=ALU.mult, op1=ALU.add)

            def spread(dst, src, m):
                n = src.shape[1]
                return v.tensor_tensor(dst, src.unsqueeze(1).broadcast_to([P, 8, n]),
                                       m[:, :].unsqueeze(2).broadcast_to([P, 8, n]), ALU.mult)

            v.wait_ge(consts, 13 + TOP)
            own(v.tensor_reduce(sel[:, :], ident[:, :].rearrange("p (h e) -> p e h", e=NE), AX_X, ALU.add))
            v.wait_ge(pe_part, M_MISC)
            v.tensor_copy(miscT[:, :], bank[0][:, 0:146]).then_inc(dve_part, 1)
            v.wait_ge(pe_part, M_AQ)
            v.tensor_copy(aWqT.rearrange("p m c q -> p (m c q)"), bank[1][:, :]).then_inc(dve_part, 1)
            v.wait_ge(pe_part, M_DK)
            v.tensor_copy(dWkT.rearrange("p m c q -> p (m c q)"), bank[2][:, :]).then_inc(dve_part, 1)
            v.wait_ge(dve_part, M_DK)
            v.wait_ge(pe_part, M_KQ)
            for a, k in ((0, ABQ), (1, CBQ)):
                for m in range(2):
                    own(v.tensor_copy(bq3[:, a, m, :], bcol[:, k, m:m + 1].broadcast_to([P, 3])), wait=False)
            for m in range(2):
                own(v.tensor_scalar(aKT[:, m, :], bank[4][:, m * NS:(m + 1) * NS], bcol[:, ABK, m:m + 1], None, ALU.add), wait=False)
                own(v.tensor_scalar(dQT[:, m, :], bank[4][:, 64 + m * NE:64 + (m + 1) * NE], bcol[:, DBQ, m:m + 1], None, ALU.add))
            for m in range(2):
                own(v.tensor_copy(aKT4[:, m, :].rearrange("p (j s) -> p j s", j=4),
                                  aKT[:, m, :].unsqueeze(1).broadcast_to([P, 4, NS])), wait=False)
                own(spread(bdK[:, m, :, :], aKT[:, m, :], masks), wait=False)
            own(spread(bdQ[:, 0, :, :], dQT[:, 0, :], masks), wait=False)
            spread(bdQ[:, 1, :, :], dQT[:, 1, :], masks).then_inc(dve_part, 1)
            v.wait_ge(pe_part, M_WZ)
            own(v.tensor_copy(Wz[:, 0, :], bank[0][:, :]), wait=False)
            v.tensor_copy(Wz[:, 1, :], bank[1][:, :]).then_inc(dve_part, 1)
            v.wait_ge(pe_part, M_ZB)
            split3(zb3[:, :], bank[6][0:3, :]).then_inc(dve_part, 1)
            v.wait_ge(dve_part, M_ZB)
            own(split3(ab3[:, :], bo3.rearrange("p a d -> p (a d)")))
            v.wait_ge(pe_part, M_V)
            v.tensor_copy(vrep[:, :, :].rearrange("p h e -> p (h e)"), bank[5][:, 0:D]).then_inc(dve_part, 1)
            v.wait_ge(pe_part, M_WD)
            own(v.tensor_copy(Wd[:, :, :].rearrange("p c n -> p (c n)"), bank[4][:, :]), wait=False)
            v.tensor_copy(dconst[:, :], bank[7][:, 0:2]).then_inc(dve_part, 1)

            def statistics(k, i, src):
                for t in range(TG):
                    v.bn_stats(stats[:, k, t, :], src(t)).then_inc(stat[k], 1)
                hold(stat[k], i * TG + TG)
                for t in range(TG):
                    v.bn_aggr(mv[:, k, t, :], stats[:, k, t, :]).then_inc(mean[k], 1)

            def xtile(i, t):
                return x[:, bass.ds(i * TG + t, 1), :].rearrange("p o d -> p (o d)")

            def norm_y(i, guard=True):
                v.wait_ge(rst[0], i + 1)
                if guard:
                    v.wait_ge(yT_ps, i)
                for t in range(TG):
                    v.tensor_scalar(y[:, t, :], xin[:, t, :], mv[:, 0, t, 0:1], rstd[:, 0, t:t + 1],
                                    ALU.subtract, ALU.mult).then_inc(y_ready, 1)

            rows = [P, NH, TG, NS]
            d3 = d[:, :].rearrange("p (h t s) -> p h t s", h=NH, t=TG)
            a3 = above[:, :].rearrange("p (h t s) -> p h t s", h=NH, t=TG)
            tau3 = tau[:, :].rearrange("p (h t) -> p h t", h=NH).unsqueeze(3).broadcast_to(rows)
            rcnt3 = rcnt[:, :].rearrange("p (h t) -> p h t", h=NH).unsqueeze(3).broadcast_to(rows)

            def first_statistics(i):
                hold(xin_in, i * 16 + 16)
                statistics(0, i, lambda t: xin[:, t, :])

            def sort_top(i):
                for t in range(TG):
                    hold(z_sb, i * TG + (t + 1))
                    for h in range(NH):
                        mx = v.max(top[:, h * TG + t, :], bZ[t % 2][:, h * NS:(h + 1) * NS])
                    mx.then_inc(topped, 1)

            def threshold(i, b):
                v.wait_ge(topped, i * TG + TG)
                for k in range(1, TOP):
                    v.tensor_tensor(top[:, :, k], top[:, :, k], top[:, :, k - 1], ALU.add).then_inc(cum, 1)
                    v.wait_ge(cum, i * 9 + k)
                v.scalar_tensor_tensor(out=ratio[:, :, :], in0=top, scalar=-1.0,
                                       in1=rk[:, :].unsqueeze(1).broadcast_to([P, HR, TOP]),
                                       op0=ALU.add, op1=ALU.mult).then_inc(cum, 1)
                v.wait_ge(cum, i * 9 + 8)
                v.tensor_reduce(tau[:, :], ratio[:, :, :], AX_X, ALU.max).then_inc(cum, 1)
                v.wait_ge(cum, i * 9 + 9)
                v.tensor_tensor(d3, scores_at(i, b), tau3, ALU.subtract).then_inc(diff, 1)

            def scores_at(i, b):
                return scr[b][:, :, bass.ds(i * TG - b * KT, TG), :]

            def count(i):
                v.wait_ge(relued, i + 1)
                v.tensor_scalar(above[:, :], d[:, :], 0.0, None, ALU.is_gt).then_inc(newton, 1)
                v.tensor_reduce(exc[:, :], d3, AX_X, ALU.add).then_inc(newton, 1)
                v.wait_ge(newton, i * NW + 1)
                v.tensor_reduce(cnt[:, :], a3, AX_X, ALU.add).then_inc(newton, 1)

            def settle(i, b):
                z3 = scores_at(i, b)
                v.wait_ge(newton, i * NW + 3)
                v.tensor_scalar(cnt[:, :], cnt[:, :], 1.0, None, ALU.max).then_inc(newton, 1)
                v.wait_ge(newton, i * NW + 4)
                v.tensor_reduce(tot[:, 0:1], cnt[:, :], AX_X, ALU.add).then_inc(newton, 1)
                v.reciprocal(rcnt[:, :], cnt[:, :]).then_inc(newton, 1)
                v.wait_ge(newton, i * NW + 6)
                v.scalar_tensor_tensor(out=rcnt[:, :], in0=exc[:, :], scalar=-1.0, in1=rcnt[:, :],
                                       op0=ALU.add, op1=ALU.mult).then_inc(newton, 1)
                v.wait_ge(newton, i * NW + 7)
                v.tensor_tensor(tau[:, :], tau[:, :], rcnt[:, :], ALU.add).then_inc(newton, 1)
                v.wait_ge(newton, i * NW + 8)
                v.tensor_tensor(z3, z3, tau3, ALU.subtract).then_inc(newton, 1)
                v.wait_ge(newton, i * NW + 9)
                v.tensor_scalar(a3, z3, 0.0, 0.0, ALU.is_gt, ALU.add, accum_out=tot[:, 1:2]).then_inc(newton, 1)
                v.wait_ge(newton, i * NW + 10)
                v.tensor_tensor(moved[:, 0:1], tot[:, 0:1], tot[:, 1:2], ALU.not_equal).then_inc(newton, 1)
                v.wait_ge(newton, i * NW + 11)
                v.transpose(movedT[:, :], moved[:, :]).then_inc(newton, 1)
                v.wait_ge(newton, i * NW + 12)
                v.tensor_reduce(flagi[:, :], movedT[:, :], AX_X, ALU.max).then_inc(newton, 1)
                hold(newton, i * NW + 13)
                parts = [v.value_load(flagi[32 * k:32 * k + 1, 0:1]) for k in range(4)]
                with v.If(parts[0] + parts[1] + parts[2] + parts[3] > 0):
                    with v.Fori(0, FIXES) as s:
                        at = i * (FIXES * 8) + s * 8
                        v.tensor_scalar(a3, z3, 0.0, None, ALU.is_gt).then_inc(fix, 1)
                        v.tensor_scalar(d3, z3, 0.0, None, ALU.max).then_inc(fix, 1)
                        v.wait_ge(fix, at + 2)
                        v.tensor_reduce(cnt[:, :], a3, AX_X, ALU.add).then_inc(fix, 1)
                        v.tensor_reduce(exc[:, :], d3, AX_X, ALU.add).then_inc(fix, 1)
                        v.wait_ge(fix, at + 4)
                        v.tensor_scalar(cnt[:, :], cnt[:, :], 1.0, None, ALU.max).then_inc(fix, 1)
                        v.wait_ge(fix, at + 5)
                        v.reciprocal(rcnt[:, :], cnt[:, :]).then_inc(fix, 1)
                        v.wait_ge(fix, at + 6)
                        v.scalar_tensor_tensor(out=rcnt[:, :], in0=exc[:, :], scalar=-1.0, in1=rcnt[:, :],
                                               op0=ALU.add, op1=ALU.mult).then_inc(fix, 1)
                        v.wait_ge(fix, at + 7)
                        v.tensor_tensor(z3, z3, rcnt3, ALU.subtract).then_inc(fix, 1)
                        v.wait_ge(fix, at + 8)
                with v.Else():
                    v.sem_inc(fix, FIXES * 8)
                v.tensor_copy(flag[:, :], moved[:, 0:1]).then_inc(settled, 1)

            def output_statistics(g):
                for t in range(TG):
                    hold(o_sb, g * TG + (t + 1))
                    v.bn_stats(stats[:, 1, t, :], o[:, t, :]).then_inc(stat[1], 1)
                hold(stat[1], g * TG + TG)
                for t in range(TG):
                    v.bn_aggr(mv[:, 1, t, :], stats[:, 1, t, :]).then_inc(mean[1], 1)

            def join(g):
                v.wait_ge(rst[1], g + 1)
                for t in range(TG):
                    v.tensor_scalar(o[:, t, :], o[:, t, :], mv[:, 1, t, 0:1], rstd[:, 1, t:t + 1],
                                    ALU.subtract, ALU.mult).then_inc(o_norm, 1)
                for t in range(TG):
                    v.wait_ge(o_norm, g * TG + (t + 1))
                    v.tensor_tensor(xtile(g, t), xtile(g, t), o[:, t, :], ALU.add).then_inc(x_new, 1)
                hold(x_new, g * TG + TG)
                statistics(2, g, lambda t: xtile(g, t))

            def second_norm(g):
                v.wait_ge(rst[2], g + 1)
                for t in range(TG):
                    v.tensor_scalar(o[:, t, :], xtile(g, t), mv[:, 2, t, 0:1], rstd[:, 2, t:t + 1],
                                    ALU.subtract, ALU.mult).then_inc(yn_ready, 1)

            def dispatch(b):
                v.wait_ge(s_sb, 2 * GB * (b + 1))
                for m in range(2):
                    v.tensor_reduce(smax[:, m:m + 1], s_all[:, m, :], AX_X, ALU.max).then_inc(maxed, 1)
                v.wait_ge(maxed, 4 * b + 2)
                for m in range(2):
                    v.tensor_scalar(nmax[:, m:m + 1], smax[:, m:m + 1], -1.0, None, ALU.mult).then_inc(maxed, 1)
                s0, p0 = PREP + b * MS, PREP + b * ND
                v.wait_ge(exped, 2 * b + 2)
                v.reciprocal(rsum[:, :], ssum[:, :]).then_inc(slots, 1)
                v.wait_ge(slots, b * NSL + 1)
                v.wait_ge(g_ps, (b + 1) * (KT // 2))
                v.tensor_scalar(gn[:, 0, :], bank[6][:, 0:D], rsum[:, 0:1], None, ALU.mult).then_inc(slots, 1)
                v.tensor_scalar(gn[:, 1, :], bank[7][:, 0:D], rsum[:, 1:2], None, ALU.mult).then_inc(dve_part, 1)
                v.wait_ge(pe_part, p0 + D_GT)
                v.tensor_copy(gT.rearrange("p c m n -> p (c m n)"), bA[0][:, :]).then_inc(dve_part, 1)
                v.wait_ge(pe_part, p0 + D_Z)
                for m in range(2):
                    z_ = v.tensor_tensor(zm[:, m, :].rearrange("p (h j) -> p h j", h=8),
                                         bA[1][:, m * P:(m + 1) * P].rearrange("p (h j) -> p h j", h=8),
                                         mask[:, :].unsqueeze(2).broadcast_to([P, 8, DH]), ALU.mult)
                    z_.then_inc((slots, dve_part)[m], 1)
                v.wait_ge(pe_part, p0 + D_H)
                for m in range(2):
                    h_ = v.tensor_scalar(hT[:, m, :], bA[0][:, m * NE:(m + 1) * NE], bcol[:, DBV, m:m + 1], None, ALU.add)
                    h_.then_inc((slots, dve_part)[m], 1)
                v.wait_ge(pe_part, p0 + D_SLOT)
                v.tensor_tensor(slot, bA[1][0:NE, 0:D], sq[:, :], ALU.add).then_inc(slots, 1)
                v.wait_ge(slots, b * NSL + 5)
                v.bn_stats(sstats[:, :], slot).then_inc(smean, 1)
                v.wait_ge(smean, 2 * b + 1)
                v.bn_aggr(smv[:, :], sstats[:, :]).then_inc(smean, 1)
                v.wait_ge(smean, 2 * b + 2)
                v.wait_ge(srst, 2 * b + 2)
                v.tensor_scalar(hid, slot, smv[:, 0:1], srstd[:, 0:1], ALU.subtract, ALU.mult).then_inc(slots, 1)
                v.wait_ge(slots, b * NSL + 6)
                v.tensor_tensor(hid, hid, lng, ALU.mult).then_inc(slots, 1)
                v.wait_ge(slots, b * NSL + 7)
                v.tensor_tensor(hid, hid, lnb, ALU.add).then_inc(dve_part, 1)
                v.wait_ge(pe_part, p0 + D_T)
                v.tensor_copy(slotT[:, :, b, :], bA[0][:, 0:32].rearrange("p (c e) -> p c e", c=C)).then_inc(slots, 1)
                v.tensor_copy(hidT[:, :, b, :], bA[0][:, 32:64].rearrange("p (c e) -> p c e", c=C)).then_inc(dve_part, 1)
                v.wait_ge(slots, b * NSL + NSL)

            NW = 13
            NSL = 8
            first_statistics(0)
            norm_y(0, guard=False)
            with v.Fori(0, GB) as i:
                first_statistics(i + 1)
                sort_top(i)
                norm_y(i + 1)
                threshold(i, 0)
                count(i)
                settle(i, 0)
            v.wait_ge(x_in, 16)
            with v.Fori(GB, NG - 1) as i:
                first_statistics(i + 1)
                sort_top(i)
                norm_y(i + 1)
                output_statistics(i - GB)
                threshold(i, 1)
                join(i - GB)
                count(i)
                second_norm(i - GB)
                settle(i, 1)
            sort_top(NG - 1)
            output_statistics(GB - 1)
            threshold(NG - 1, 1)
            join(GB - 1)
            count(NG - 1)
            second_norm(GB - 1)
            settle(NG - 1, 1)
            v.wait_ge(w_in2, 16 * N_W2)
            own(v.tensor_tensor(sq[:, :], sq[:, :], dbo, ALU.add))
            dispatch(0)
            with v.Fori(GB, NG) as g:
                output_statistics(g)
                join(g)
                second_norm(g)
            dispatch(1)

            v.wait_ge(pe_part, CP + 1)
            own(v.tensor_copy(cWqT.rearrange("p m c q -> p (m c q)"), bank[6][:, :]), wait=False)
            v.tensor_copy(bT1.rearrange("p e g j -> p g e j"), bank[7][:, 0:2 * P].rearrange("p (g e j) -> p g e j", g=2, j=J))\
                .then_inc(hbias, 1)
            v.wait_ge(hbias, 1)
            for b in range(NB):
                own(v.tensor_tensor(slotT[:, :, b, :], slotT[:, :, b, :], b2T, ALU.add), wait=b == NB - 1)

            def keep_down(e):
                v.wait_ge(down_ps, e + 1)
                v.tensor_copy(dn, bank[6][0:NB, 0:D]).then_inc(dn_sb, 1)

            def add_down(e):
                v.wait_ge(dnT_ps, e + 1)
                v.tensor_tensor(newT[:, :, :, bass.ds(e, 1)].rearrange("p c b o -> p c (b o)"),
                                bank[7][:, 0:C * NB].rearrange("p (c b) -> p c b", c=C),
                                slotT[:, :, :, bass.ds(e, 1)].rearrange("p c b o -> p c (b o)"), ALU.add).then_inc(down_sb, 1)

            def expert(h, k, first=False):
                e, q = h * 3 + k, k % 3
                v.wait_ge(up_ps, e * 2 + 2)
                v.tensor_copy(ugT[q], bank[q][:, :]).then_inc(ug_sb, 1)
                if not first:
                    keep_down(e - 1)
                v.wait_ge(ugT_ps, e + 1)
                v.tensor_tensor(pre.rearrange("p g (a j) b -> p (g a) j b", a=2),
                                bank[3 + q][:, :].rearrange("p (j k x) -> p k j x", j=4, k=4)[:, :, :, 0:NB],
                                bT1[:, bass.ds(e, 1), :, :].rearrange("p o g (a j) -> p (o g a) j", a=2).unsqueeze(3)
                                .broadcast_to([P, 4, 4, NB]), ALU.add).then_inc(pred, 1)
                v.wait_ge(silued, e + 1)
                v.tensor_tensor(ug[:, q, :, :], gate[:, 0, :, :], gate[:, 1, :, :], ALU.mult).then_inc(ug_ready, 1)
                if not first:
                    add_down(e - 1)

            expert(0, 0, first=True)
            with v.Fori(0, 5) as h:
                for k in range(1, 4):
                    expert(h, k)
            keep_down(NE - 1)
            add_down(NE - 1)

            v.wait_ge(pe_part, CP + 2)
            for m in range(2):
                own(v.tensor_scalar(cKT[:, m, :, :], bank[0][:, m * 32:(m + 1) * 32].rearrange("p (b e) -> p b e", b=NB),
                                    bcol[:, CBK, m:m + 1], None, ALU.add), wait=False)
                own(v.tensor_scalar(cVT[:, m, :, :], bank[0][:, 64 + m * 32:64 + (m + 1) * 32].rearrange("p (b e) -> p b e", b=NB),
                                    bcol[:, CBV, m:m + 1], None, ALU.add))
            for m in range(2):
                for b in range(NB):
                    own(spread(cbK[:, m, b, :, :], cKT[:, m, b, :], masks), wait=False)
                    last = spread(cbV[:, m, b, :, :], cVT[:, m, b, :], mask)
                    if m == 0 or b == 0:
                        own(last, wait=False)
            last.then_inc(dve_part, 1)
            v.wait_ge(pe_part, CP + 3)
            for b in range(NB):
                own(v.tensor_copy(Wc[:, b, :, :].rearrange("p c n -> p (c n)"), bank[1 + b][:, :]), wait=False)
                own(v.tensor_copy(Vc[:, b, :, :].rearrange("p m n -> p (m n)"), bank[3 + b][:, :]), wait=False)
            split3(cb3[:, :], bank[5][0:3, :]).then_inc(dve_part, 1)

            def soften(j, q):
                for u in range(2):
                    v.wait_ge(c_ps, j * 2 + (u + 1))
                    ps = bank[u][:, :].rearrange("p (r e) -> p r e", e=NE)
                    cm = cmax[:, u * 32:(u + 1) * 32]
                    v.tensor_reduce(cm, ps, AX_X, ALU.max).then_inc(c_max, 1)
                    v.wait_ge(c_max, j * 2 + (u + 1))
                    v.tensor_tensor(prob[:, q, 2 * u:2 * u + 2, :].rearrange("p t (h e) -> p (t h) e", e=NE), ps,
                                    cm.unsqueeze(2).broadcast_to([P, 32, NE]), ALU.subtract).then_inc(c_sub, 1)

            def total(j, q, first=False):
                v.wait_ge(c_exp, j + 1)
                v.tensor_reduce(csum, prob[:, q, :, :].rearrange("p t (h e) -> p (t h) e", e=NE), AX_X, ALU.add)\
                    .then_inc(c_sum, 1)
                v.wait_ge(c_sum, j + 1)
                if not first:
                    v.wait_ge(c_prob, j)
                v.reciprocal(crs, csum).then_inc(c_rs, 1)

            def norm_out(j, q):
                for t in range(TG):
                    hold(co_sb, j * 2 + (t // 2 + 1))
                    v.bn_stats(stats[:, 0, t, :], co[:, q, t, :]).then_inc(c_stat, 1)
                hold(c_stat, j * TG + TG)
                for t in range(TG):
                    v.bn_aggr(mv[:, 0, t, :], stats[:, 0, t, :]).then_inc(c_mean, 1)

            def apply_out(j, q):
                v.wait_ge(c_rst, j + 1)
                for t in range(TG):
                    v.tensor_scalar(co[:, q, t, :], co[:, q, t, :], mv[:, 0, t, 0:1], rstd[:, 0, t:t + 1],
                                    ALU.subtract, ALU.mult).then_inc(c_norm, 1)

            def combine(j, q, second=False):
                soften(j, q)
                if not second:
                    apply_out(j - 2, q)
                total(j, q)
                norm_out(j - 1, 1 - q)

            v.wait_ge(c_in, 2)
            soften(0, 0)
            total(0, 0, first=True)
            combine(1, 1, second=True)
            with v.Fori(1, NG // 2) as h:
                combine(h * 2, 0)
                combine(h * 2 + 1, 1)
            apply_out(NG - 2, 0)
            norm_out(NG - 1, 1)
            apply_out(NG - 1, 1)


_INS = ['L0_attn_query', 'L0_attn_key_param', 'L0_attn_Wq', 'L0_attn_bq', 'L0_attn_Wk', 'L0_attn_bk', 'L0_attn_Wv',
        'L0_attn_bv', 'L0_attn_Wo', 'L0_attn_bo', 'L0_ffn_slot_query', 'L0_ffn_d_Wq', 'L0_ffn_d_Wk', 'L0_ffn_d_Wv',
        'L0_ffn_d_Wo', 'L0_ffn_d_bq', 'L0_ffn_d_bk', 'L0_ffn_d_bv', 'L0_ffn_d_bo', 'L0_ffn_c_Wq', 'L0_ffn_c_Wk',
        'L0_ffn_c_Wv', 'L0_ffn_c_Wo', 'L0_ffn_c_bq', 'L0_ffn_c_bk', 'L0_ffn_c_bv', 'L0_ffn_c_bo', 'L0_ffn_e_ln_g',
        'L0_ffn_e_ln_b', 'L0_ffn_e_W1', 'L0_ffn_e_b1', 'L0_ffn_e_Wg', 'L0_ffn_e_bg', 'L0_ffn_e_W2', 'L0_ffn_e_b2']
_OUTS = [((2, 2048, 256), 'float32')]


def kernel(**inputs):
    import numpy as _np
    import concourse.bacc as _bacc
    from concourse import mybir as _mybir
    from concourse.bass_utils import run_bass_kernel_spmd as _run

    nc = _bacc.Bacc("TRN2", target_bir_lowering=False, num_devices=1)
    arrays, args = {}, {}
    for name in _INS:
        a = _np.ascontiguousarray(inputs[name])
        arrays[f"in_{name}_dram"] = a
        args[name] = nc.dram_tensor(f"in_{name}_dram", a.shape, _mybir.dt.from_np(a.dtype), kind="ExternalInput").ap()
    shape, dtype = _OUTS[0]
    out = nc.dram_tensor("out_0_dram", shape, _mybir.dt.from_np(_np.dtype(dtype)), kind="ExternalOutput").ap()
    build(nc, args, out)
    r = _run(nc, [arrays], core_ids=[0])
    return r.results[0]["out_0_dram"]
```

```python
from contextlib import ExitStack

import concourse.bass as bass
from concourse import mybir

ALU = mybir.AluOpType
ACT = mybir.ActivationFunctionType
F32 = mybir.dt.float32
BF16 = mybir.dt.bfloat16
I32 = mybir.dt.int32
AX_X = mybir.AxisListType.X

P = 128
D = 256
C = D // P
NB, L = 2, 2048
NH, DH = 16, 16
NS = 32
NE, FF = 16, 1024
J = FF // P
TG = 4
GT = TG * P
NG = NB * L // GT
GB = L // GT
KT = L // P
HR = TG * NH
TOP = 8
EPS = 1e-5
FIXES = NS - TOP
EB = 3
SCALE = DH ** -0.5


def build(nc, A, out):
    with ExitStack() as ctx:
        def sb(name, shape, dt=F32):
            return ctx.enter_context(nc.sbuf_tensor(name, shape, dt))

        def sem(name):
            return ctx.enter_context(nc.semaphore(name))

        bank = [ctx.enter_context(nc.psum_tensor(f"bank{i}", [P, 512], F32)) for i in range(8)]

        x = sb("x", [P, NB * KT, D])
        arena = sb("arena", [P, 14336])
        ynT = arena[:, 0:8192].rearrange("p (b c l) -> p b c l", b=NB, c=C)
        ring0 = arena[:, 8192:14336].rearrange("p (k n) -> p k n", k=3)
        work = sb("work", [P, 8192])
        s_all = work[:, 0:4096].rearrange("p (m k) -> p m k", m=2)
        yn = work[:, 4096:8192].rearrange("p (t d) -> p t d", d=D)
        scr1 = sb("scr1", [P, KT * 512])
        ring = (ring0, scr1[:, 0:6144].rearrange("p (k n) -> p k n", k=3), work[:, 0:6144].rearrange("p (k n) -> p k n", k=3))
        scr = tuple(a.rearrange("p (h j s) -> p h j s", h=NH, j=KT) for a in (arena[:, 4096:12288], scr1[:, :]))

        aWq, aWk, aWv, dWq, dWk = (
            work[:, 512 * i:512 * i + 512].rearrange("p (c d) -> p c d", c=C) for i in range(5))
        kp = work[0:NS, 2560:2816]
        b2 = work[0:NE, 2816:3072]
        aWo = sb("aWo", [P, C, D])
        sq = sb("sq", [NE, D])
        cWq, cWk, cWv, cWo = (scr1[:, 6144 + 512 * i:6656 + 512 * i].rearrange("p (c d) -> p c d", c=C) for i in range(4))

        def fold(at, n, parts=P):
            return work[0:parts, 4096 + at:4096 + at + n]

        aWqT = fold(0, 512).rearrange("p (m c q) -> p m c q", m=2, c=C)
        dWkT = fold(512, 512).rearrange("p (m c q) -> p m c q", m=2, c=C)
        bdK = fold(1024, 512).rearrange("p (m h s) -> p m h s", m=2, h=8)
        bdQ = fold(2048, 256).rearrange("p (m h s) -> p m h s", m=2, h=8)
        aKT = fold(2304, 64).rearrange("p (m s) -> p m s", m=2)
        aKT4 = fold(3488, 256).rearrange("p (m s) -> p m s", m=2)
        dQT = fold(2432, 32).rearrange("p (m s) -> p m s", m=2)
        brow = fold(2464, P, 18)
        bo3 = fold(2592, 512, 3).rearrange("p (a d) -> p a d", a=2)
        bvrow = fold(3104, D, 1)
        ones1 = fold(3360, P, 1)

        ident = sb("ident", [P, P])
        mask = sb("mask", [P, 8])
        masks = sb("masks", [P, 8])
        sel = sb("sel", [P, NE])
        ones3 = sb("ones3", [3, P], BF16)
        mhalf = sb("mhalf", [P, TG])
        tiny = sb("tiny", [P, 1])
        rk = sb("rk", [P, TOP])
        miscT = sb("miscT", [P, 146])
        kpT = miscT[:, 0:64].rearrange("p (c s) -> p c s", c=C)
        sqT = miscT[:, 64:96].rearrange("p (c s) -> p c s", c=C)
        b2T = miscT[:, 96:128].rearrange("p (c s) -> p c s", c=C)
        bcol = miscT[:, 128:146].rearrange("p (v m) -> p v m", m=2)
        ABQ, ABK, ABV, DBQ, DBK, DBV, CBQ, CBK, CBV = range(9)
        bq3 = sb("bq3", [P, 2, 2, 3])
        Wz = sb("Wz", [P, C, 512])
        Wd = sb("Wd", [P, C, D])
        vrep = sb("vrep", [P, NH, DH])
        jmask = sb("jmask", [P, 2, 8])
        dconst = sb("dconst", [P, 2])
        zb3 = sb("zb3", [3, 512], BF16)
        ab3 = sb("ab3", [3, 512], BF16)
        cb3 = sb("cb3", [3, 512], BF16)

        stats = sb("stats", [P, 3, TG, 6])
        mv = sb("mv", [P, 3, TG, 2])
        veps = sb("veps", [P, 3, TG])
        rstd = sb("rstd", [P, 3, TG])
        shift = sb("shift", [P, 3, TG])
        xin = sb("xin", [P, TG, D])
        y = sb("y", [P, TG, D])
        yT = sb("yT", [P, C, GT])
        d = sb("d", [P, TG * 512])
        above = sb("above", [P, TG * 512], BF16)
        top = sb("top", [P, HR, TOP])
        tau = sb("tau", [P, HR])
        cnt = sb("cnt", [P, HR])
        exc = sb("exc", [P, HR])
        rcnt = sb("rcnt", [P, HR])
        tauf = sb("tauf", [P, HR])
        tot = sb("tot", [P, 2, GB])
        ahead = sb("ahead", [P, NG])
        moved = sb("moved", [P, 32])
        movedT = sb("movedT", [P, 32])
        flag = sb("flag", [P, 1])
        flagi = sb("flagi", [P, 1], I32)

        bdh = sb("bdh", [P, TG, 2, P])
        aT = sb("aT", [P, 2, 512])
        hoT = sb("hoT", [P, 2, P])
        o = arena[:, 12288:14336].rearrange("p (q t d) -> p q t d", q=2, t=TG)

        pmax = sb("pmax", [P, 2, GB])
        smax = sb("smax", [P, 2])
        nmax = sb("nmax", [P, 2])
        ssum = sb("ssum", [P, 2])
        rsum = sb("rsum", [P, 2])
        pT = aT
        dWv = d[:, 0:512].rearrange("p (c n) -> p c n", c=C)
        dWo = d[:, 512:1024].rearrange("p (c n) -> p c n", c=C)
        gn = y[:, 0:2, :]
        zm = y[:, 2, :].rearrange("p (m n) -> p m n", m=2)
        gT = yT[:, 0, :].rearrange("p (c m n) -> p c m n", c=C, m=2)
        slot = yT[0:NE, 1, 0:256]
        hid = yT[0:NE, 1, 256:512]
        lng = xin[0:NE, 0, :]
        lnb = xin[0:NE, 1, :]
        dbo = xin[0:NE, 2, :]
        b1 = xin[:, 3, 0:P]
        bg = xin[:, 3, P:2 * P]
        bT1 = y[:, 3, :].rearrange("p (e g j) -> p e g j", g=2, j=J)
        hT = sb("hT", [P, 2, NE])
        sstats = sb("sstats", [NE, 6])
        smv = sb("smv", [NE, 2])
        sveps = sb("sveps", [NE, 1])
        srstd = sb("srstd", [NE, 1])
        slotT = sb("slotT", [P, C, NB, NE])
        hidT = sb("hidT", [P, C, NB, NE])

        def over(at, n):
            return d[:, at:at + n]

        pre = over(0, 32).rearrange("p (g j b) -> p g j b", g=2, b=NB)
        gate = over(32, 32).rearrange("p (g j b) -> p g j b", g=2, b=NB)
        ug = over(352, 48).rearrange("p (q j b) -> p q j b", q=EB, b=NB)
        hcol = over(160, 192).rearrange("p (q c x) -> p q c x", q=EB, c=C)
        spare = above[:, :].bitcast(F32)
        ugT = (over(1024, 512), over(1536, 512), spare[:, 0:512])
        dn = spare[0:NB, 512:768]
        newT = over(96, 64).rearrange("p (c b e) -> p c b e", c=C, b=NB)
        cKT = over(160, 64).rearrange("p (m b e) -> p m b e", m=2, b=NB)
        cVT = over(224, 64).rearrange("p (m b e) -> p m b e", m=2, b=NB)
        cWqT = over(512, 512).rearrange("p (m c n) -> p m c n", m=2, c=C)
        cbK = over(1024, 512).rearrange("p (m b h e) -> p m b h e", m=2, b=NB, h=8)
        cbV = over(1536, 512).rearrange("p (m b h e) -> p m b h e", m=2, b=NB, h=8)
        Wc = scr1[:, 0:1024].rearrange("p (b c n) -> p b c n", b=NB, c=C)
        Vc = scr1[:, 1024:2048].rearrange("p (b m n) -> p b m n", b=NB, m=2)
        cin = work[:, 0:2048].rearrange("p (g c n) -> p g c n", g=2, c=C)
        prob = work[:, 2048:4096].rearrange("p (g t n) -> p g t n", g=2, t=TG)
        cpT = work[:, 4096:5120].rearrange("p (g n) -> p g n", g=2)
        co = work[:, 5120:7168].rearrange("p (g t n) -> p g t n", g=2, t=TG)
        cmax = work[:, 7168:7232]
        csum = work[:, 7232:7296]
        crs = work[:, 7296:7360]

        xs = A['L0_attn_query'].rearrange("b (p j) d -> p b j d", p=P)
        xt = A['L0_attn_query'].rearrange("b (t p) d -> p (b t) d", p=P)
        ot = out.rearrange("b (t p) d -> p (b t) d", p=P)
        w_in = sem("w_in")
        w_in2 = sem("w_in2")
        w_in3 = sem("w_in3")
        xin_in = sem("xin_in")
        x_in = sem("x_in")
        bd_ready = sem("bd_ready")
        h_ps = sem("h_ps")
        h_sb = sem("h_sb")
        consts = sem("consts")
        pe_part = sem("pe_part")
        dve_part = sem("dve_part")
        prep = sem("prep")
        stat = [sem(f"stat{k}") for k in range(3)]
        mean = [sem(f"mean{k}") for k in range(3)]
        vare = [sem(f"vare{k}") for k in range(3)]
        root = [sem(f"root{k}") for k in range(3)]
        rst = [sem(f"rst{k}") for k in range(3)]
        y_ready = sem("y_ready")
        yT_ps = sem("yT_ps")
        yT_sb = sem("yT_sb")
        z_ps = sem("z_ps")
        z_sb = sem("z_sb")
        topped = sem("topped")
        cum = sem("cum")
        diff = sem("diff")
        relued = sem("relued")
        newton = sem("newton")
        checked = sem("checked")
        fix = sem("fix")
        tau_ready = sem("tau_ready")
        lowered = sem("lowered")
        signed = sem("signed")
        settled = sem("settled")
        a_ps = sem("a_ps")
        a_sb = sem("a_sb")
        o_ps = sem("o_ps")
        o_sb = sem("o_sb")
        o_norm = sem("o_norm")
        x_new = sem("x_new")
        yn_ready = sem("yn_ready")
        ynT_ps = sem("ynT_ps")
        ynT_sb = sem("ynT_sb")
        s_ps = sem("s_ps")
        s_sb = sem("s_sb")
        maxed = sem("maxed")
        exped = sem("exped")
        pT_ps = sem("pT_ps")
        pT_sb = sem("pT_sb")
        g_ps = sem("g_ps")
        slots = sem("slots")
        smean = sem("smean")
        srst = sem("srst")
        e_in = [[sem(f"e_in{q}{k}") for k in range(3)] for q in range(EB)]
        up_ps = sem("up_ps")
        hbias = sem("hbias")
        ug_sb = sem("ug_sb")
        ugT_ps = sem("ugT_ps")
        pred = sem("pred")
        silued = sem("silued")
        hcol_ready = sem("hcol_ready")
        ug_ready = sem("ug_ready")
        down_ps = sem("down_ps")
        dn_sb = sem("dn_sb")
        dnT_ps = sem("dnT_ps")
        down_sb = sem("down_sb")
        c_in = sem("c_in")
        c_ps = sem("c_ps")
        c_max = sem("c_max")
        c_sub = sem("c_sub")
        c_exp = sem("c_exp")
        c_sum = sem("c_sum")
        c_rs = sem("c_rs")
        c_prob = sem("c_prob")
        c_pT_ps = sem("c_pT_ps")
        c_pT_sb = sem("c_pT_sb")
        co_ps = sem("co_ps")
        co_sb = sem("co_sb")
        c_stat = sem("c_stat")
        c_mean = sem("c_mean")
        c_vare = sem("c_vare")
        c_rst = sem("c_rst")
        c_norm = sem("c_norm")
        c_out = sem("c_out")
        stored = [sem(f"stored{q}") for q in range(2)]

        bT = bank[0:2]; bZ = bank[2:4]; bA = bank[4:6]
        psH = bank[6][:, 0:D]
        psO = bank[7][:, 0:D]
        N_W1, N_W2, N_W3 = 21, 7, 4
        (M_MISC, M_AQ, M_DK, M_KQ, M_WZ, M_ZB, M_V, M_WD) = range(1, 9)
        PREP = M_WD
        (D_GT, D_Z, D_H, D_SLOT, D_T) = range(1, 6)
        ND = D_T
        (S_G, S_GT, S_ZM, S_H, S_SLOT, S_T) = range(1, 7)
        MS = 6
        NMX = 2 * GB + 2
        CP = PREP + 2 * ND
        CS = PREP + 2 * MS

        block = ctx.enter_context(nc.Block())

        @block.sync
        def _(sp):
            def load(i, b):
                sp.dma_start(xin[:, :, :], xs[:, b, bass.ds(i * TG - b * KT, TG), :]).then_inc(xin_in, 16)

            load(0, 0)
            sp.dma_start(x[:, :, :], xt).then_inc(x_in, 16)
            for b in range(NB):
                with sp.Fori(1 if b == 0 else GB, (b + 1) * GB) as i:
                    sp.wait_ge(y_ready, i * TG)
                    load(i, b)

            sp.wait_ge(settled, NB)
            for dst, src in ((lng, A['L0_ffn_e_ln_g']), (lnb, A['L0_ffn_e_ln_b']),
                             (dbo, A['L0_ffn_d_bo'].rearrange("(o d) -> o d", o=1).broadcast_to([NE, D])),
                             (dWv, A['L0_ffn_d_Wv'].rearrange("(p c) n -> p c n", c=C)),
                             (dWo, A['L0_ffn_d_Wo'].rearrange("(c p) n -> p c n", c=C)),
                             (b1, A['L0_ffn_e_b1'].rearrange("e (j p) -> (e j) p", p=P)),
                             (bg, A['L0_ffn_e_bg'].rearrange("e (j p) -> (e j) p", p=P))):
                sp.dma_start(dst, src).then_inc(w_in2, 16)

            def expert(e, q, k):
                dst = ring[q][:, k, :]
                if k == 2:
                    dst = dst.rearrange("p (j d) -> p j d", j=J)
                if k < 2:
                    src = A[('L0_ffn_e_W1', 'L0_ffn_e_Wg')[k]].rearrange("e (p c) f -> p e (c f)", c=C)[:, e, :]
                else:
                    src = A['L0_ffn_e_W2'].rearrange("e (j p) d -> p e j d", j=J)[:, e, :, :]
                sp.dma_start(dst, src).then_inc(e_in[q][k], 16)

            sp.wait_ge(a_ps, KT)
            for k in range(2):
                expert(0, 0, k)
            sp.wait_ge(a_ps, 2 * KT)
            for w, name, form in ((cWq, 'L0_ffn_c_Wq', "(p c) n -> p c n"), (cWk, 'L0_ffn_c_Wk', "(p c) n -> p c n"),
                                  (cWv, 'L0_ffn_c_Wv', "(p c) n -> p c n"), (cWo, 'L0_ffn_c_Wo', "(c p) n -> p c n")):
                sp.dma_start(w, A[name].rearrange(form, c=C)).then_inc(w_in3, 16)
            for k in range(3):
                expert(1, 1, k)
            sp.wait_ge(x_new, NG)
            expert(0, 0, 2)
            sp.wait_ge(g_ps, 2 * (KT // 2))
            for k in range(3):
                expert(2, 2, k)

            def refill(it, q):
                for k in range(3):
                    if k < 2:
                        sp.wait_ge(up_ps, it * 6 + (2 * (q - 3) + k + 1))
                    else:
                        sp.wait_ge(down_ps, it * 3 + (q - 2))
                    expert(it * 3 + q, q, k)

            with sp.Fori(1, NE // EB) as it:
                for q in range(EB):
                    refill(it, q)
            for q in range(NE % EB):
                refill(NE // EB, q)

            def store(j, q):
                sp.wait_ge(c_out, j + 1)
                sp.dma_start(ot[:, bass.ds(j * TG, TG), :], co[:, q, :, :]).then_inc(stored[q], 16)

            with sp.Fori(0, NG // 2) as h:
                store(h * 2, 0)
                store(h * 2 + 1, 1)
            sp.wait_ge(stored[0], 16 * NG // 2)
            sp.wait_ge(stored[1], 16 * NG // 2)

        @block.gpsimd
        def _(pool):
            pool.memset(ident[:, :], 0.0).then_inc(consts, 1)
            pool.memset(mask[:, :], 1.0).then_inc(consts, 1)
            pool.memset(ones3[:, :], 1.0).then_inc(consts, 1)
            pool.memset(mhalf[:, :], -0.5).then_inc(consts, 1)
            pool.memset(tiny[:, :], -1e-30).then_inc(consts, 1)
            pool.memset(moved[:, :], 0.0).then_inc(consts, 1)
            for k in range(TOP):
                pool.memset(rk[:, k:k + 1], 1.0 / (k + 1)).then_inc(consts, 1)
            pool.memset(jmask[:, :, :], 1.0).then_inc(consts, 1)
            pool.memset(ones1, 1.0).then_inc(consts, 1)
            n = 8 + TOP
            pool.wait_ge(consts, n)
            pool.affine_select(out=ident[:, :], in_=ident[:, :], compare_op=ALU.not_equal, fill=1.0, base=0,
                               pattern=[[-1, P]], channel_multiplier=1).then_inc(consts, 1)
            pool.affine_select(out=mask[:, :], in_=mask[:, :], compare_op=ALU.is_ge, fill=0.0, base=0,
                               pattern=[[-DH, 8]], channel_multiplier=1).then_inc(consts, 1)
            pool.wait_ge(consts, n + 2)
            pool.affine_select(out=mask[:, :], in_=mask[:, :], compare_op=ALU.is_ge, fill=0.0, base=DH - 1,
                               pattern=[[DH, 8]], channel_multiplier=-1).then_inc(consts, 1)
            pool.wait_ge(consts, n + 3)
            pool.tensor_scalar(masks[:, :], mask[:, :], SCALE, None, ALU.mult).then_inc(consts, 1)
            pool.affine_select(out=jmask[:, :, :], in_=jmask[:, :, :], compare_op=ALU.is_ge, fill=0.0, base=0,
                               pattern=[[P, 2], [-NS, 8]], channel_multiplier=1).then_inc(consts, 1)
            pool.wait_ge(consts, n + 5)
            pool.affine_select(out=jmask[:, :, :], in_=jmask[:, :, :], compare_op=ALU.is_ge, fill=0.0, base=NS - 1,
                               pattern=[[-P, 2], [NS, 8]], channel_multiplier=-1).then_inc(consts, 1)

            def hold(s, value):
                pool.wait_ge(s, value)
                pool.nop(nofuse=True)

            def roots(k, i):
                if k == 2 and not (isinstance(i, int) and i == 0):
                    hold(yn_ready, i * TG)
                hold(mean[k], i * TG + TG)
                pool.tensor_scalar(veps[:, k, :], mv[:, k, :, 1], EPS, None, ALU.add).then_inc(vare[k], 1)
                pool.tensor_scalar(shift[:, k, :], mv[:, k, :, 0], -1.0, None, ALU.mult).then_inc(vare[k], 1)
                pool.wait_ge(vare[k], i * 2 + 2)
                pool.tensor_tensor(rstd[:, k, :], veps[:, k, :], mhalf[:, :], ALU.pow).then_inc(root[k], 1)
                pool.wait_ge(root[k], i + 1)
                pool.tensor_tensor(shift[:, k, :], shift[:, k, :], rstd[:, k, :], ALU.mult).then_inc(rst[k], 1)

            def values(g):
                b = g // GB
                for t in range(TG):
                    if g > 0:
                        pool.wait_ge(h_ps, g * TG + (t + 1 - TG))
                    pool.tensor_tensor(bdh[:, t, :, :].rearrange("p a (j e) -> p (a j) e", e=DH),
                                       vrep[:, g * TG + t - b * NH, :].unsqueeze(1).broadcast_to([P, 16, DH]),
                                       jmask[:, :, :].rearrange("p a j -> p (a j)").unsqueeze(2).broadcast_to([P, 16, DH]),
                                       ALU.mult).then_inc(bd_ready, 1)

            def lower(i, b):
                pool.wait_ge(tau_ready, i + 1)
                z3 = scr[b][:, :, bass.ds(i * TG - b * KT, TG), :]
                pool.tensor_tensor(z3, z3, tauf[:, :].rearrange("p (h t) -> p h t", h=NH).unsqueeze(3)
                                   .broadcast_to([P, NH, TG, NS]), ALU.subtract).then_inc(lowered, 1)

            def slot_root(b):
                pool.wait_ge(smean, 2 * b + 2)
                pool.tensor_scalar(sveps[:, :], smv[:, 1:2], EPS, None, ALU.add).then_inc(srst, 1)
                pool.wait_ge(srst, 2 * b + 1)
                pool.tensor_tensor(srstd[:, :], sveps[:, :], mhalf[0:NE, 0:1], ALU.pow).then_inc(srst, 1)

            roots(0, 0)
            roots(0, 1)
            with pool.Fori(0, GB) as i:
                roots(0, i + 2)
                lower(i, 0)
            pool.wait_ge(dve_part, PREP)
            for i in range(GB, NG):
                g = i - GB
                values(g)
                if g > 0:
                    roots(1, g - 1)
                if i + 2 < NG:
                    roots(0, i + 2)
                if g > 0:
                    roots(2, g - 1)
                lower(i, 1)
            for g in range(GB, NG + 1):
                if g < NG:
                    values(g)
                roots(1, g - 1)
                roots(2, g - 1)
            slot_root(0)
            slot_root(1)

            def stage(j, b, q):
                pool.tensor_copy(cin[:, q, :, :], ynT[:, b, :, bass.ds(j * GT - b * L, GT)]).then_inc(c_in, 1)

            def weigh(j, q):
                pool.wait_ge(c_rs, j + 1)
                pv = prob[:, q, :, :].rearrange("p t (h e) -> p (t h) e", e=NE)
                pool.tensor_tensor(pv, pv, crs[:, :].unsqueeze(2).broadcast_to([P, HR, NE]), ALU.mult)\
                    .then_inc(c_prob, 1)

            def finish(j, q):
                hold(c_mean, j * TG + TG)
                pool.tensor_scalar(veps[:, 0, :], mv[:, 0, :, 1], EPS, None, ALU.add).then_inc(c_vare, 1)
                pool.wait_ge(c_vare, j + 1)
                pool.tensor_tensor(rstd[:, 0, :], veps[:, 0, :], mhalf[:, :], ALU.pow).then_inc(c_rst, 1)
                pool.wait_ge(c_norm, j * TG + TG)
                pool.tensor_tensor(co[:, q, :, :], co[:, q, :, :], x[:, bass.ds(j * TG, TG), :], ALU.add)\
                    .then_inc(c_out, 1)

            def lay_by(it, q, first=False):
                if not first:
                    pool.wait_ge(up_ps, it * 6 + 2 * (q - 2))
                pool.tensor_copy(hcol[:, q, :, 0:NB], hidT[:, :, :, bass.ds(it * 3 + q, 1)].rearrange("p c b o -> p c (b o)"))\
                    .then_inc(hcol_ready, 1)

            pool.wait_ge(dve_part, PREP + 2 * MS)
            pool.memset(hcol, 0.0).then_inc(consts, 1)
            pool.wait_ge(consts, 15 + TOP)
            for q in range(EB):
                lay_by(0, q, first=True)
            with pool.Fori(1, NE // EB) as it:
                for q in range(EB):
                    lay_by(it, q)
            for q in range(NE % EB):
                lay_by(NE // EB, q)

            pool.wait_ge(down_ps, NE - 1)
            stage(0, 0, 0)
            stage(1, 0, 1)
            weigh(0, 0)

            def combine(j, b, q, more=True):
                if more:
                    pool.wait_ge(c_ps, j * 2)
                    stage(j + 1, b, 1 - q)
                weigh(j, q)
                finish(j - 1, 1 - q)

            combine(1, 0, 1)
            combine(2, 0, 0)
            with pool.Fori(1, NG // 2 - 1) as h:
                combine(h * 2 + 1, 1, 1)
                combine(h * 2 + 2, 1, 0)
            combine(NG - 1, 1, 1, more=False)
            finish(NG - 1, 1)

        @block.scalar
        def _(act):
            first_lot = [
                (kp, A['L0_attn_key_param'][0]), (sq[:, :], A['L0_ffn_slot_query'][0]), (b2, A['L0_ffn_e_b2']),
                (bvrow, A['L0_attn_bv'].rearrange("(o d) -> o d", o=1))]
            for v, name in enumerate(('L0_attn_bq', 'L0_attn_bk', 'L0_attn_bv', 'L0_ffn_d_bq', 'L0_ffn_d_bk',
                                      'L0_ffn_d_bv', 'L0_ffn_c_bq', 'L0_ffn_c_bk', 'L0_ffn_c_bv')):
                first_lot.append((brow[2 * v:2 * v + 2, :], A[name].rearrange("(m p) -> m p", p=P)))
            for a, name in ((0, 'L0_attn_bo'), (1, 'L0_ffn_c_bo')):
                first_lot.append((bo3[:, a, :], A[name].rearrange("(o d) -> o d", o=1).broadcast_to([3, D])))
            for w, name, form in ((aWq, 'L0_attn_Wq', "(p c) n -> p c n"), (aWk, 'L0_attn_Wk', "(p c) n -> p c n"),
                                  (aWv, 'L0_attn_Wv', "(c p) n -> p c n"), (aWo[:, :, :], 'L0_attn_Wo', "(c p) n -> p c n"),
                                  (dWq, 'L0_ffn_d_Wq', "(p c) n -> p c n"), (dWk, 'L0_ffn_d_Wk', "(p c) n -> p c n")):
                first_lot.append((w, A[name].rearrange(form, c=C)))
            assert len(first_lot) == N_W1
            for dst, src in first_lot:
                act.dma_start(dst, src).then_inc(w_in, 16)

            def scaled(k, t, dst, src):
                return act.activation(dst, src, ACT.Identity, bias=shift[:, k, t:t + 1], scale=rstd[:, k, t:t + 1])

            def norm_y(i, guard=True):
                act.wait_ge(rst[0], i + 1)
                if guard:
                    act.wait_ge(yT_ps, i)
                for t in range(TG):
                    scaled(0, t, y[:, t, :], xin[:, t, :]).then_inc(y_ready, 1)

            def put_yT(i, guard=True):
                act.wait_ge(yT_ps, i + 1)
                if guard:
                    act.wait_ge(z_ps, i * TG)
                for c in range(C):
                    act.activation(yT[:, c, :], bT[c][:, :], ACT.Copy).then_inc(yT_sb, 1)

            def put_scores(i, b, tiles):
                for t in tiles:
                    act.wait_ge(z_ps, i * TG + (t + 1))
                    act.activation(scr[b][:, :, bass.ds(i * TG + (t - b * KT), 1), :].rearrange("p h o s -> p (h o) s"),
                                   bZ[t % 2][:, :].rearrange("p (h s) -> p h s", h=NH), ACT.Copy).then_inc(z_sb, 1)

            def clamp(i):
                act.wait_ge(diff, i + 1)
                act.activation(d[:, :], d[:, :], ACT.Relu).then_inc(relued, 1)

            def signs(i, b):
                act.wait_ge(lowered, i + 1)
                act.activation(above[:, :].rearrange("p (h t s) -> p h t s", h=NH, t=TG),
                               scr[b][:, :, bass.ds(i * TG - b * KT, TG), :], ACT.Sign, bias=tiny[:, 0:1],
                               accum_out=ahead[:, bass.ds(i, 1)]).then_inc(signed, 1)

            def put_heads(g, steps=range(TG + 2)):
                for t in steps:
                    n = g * TG + t
                    if t < TG:
                        act.wait_ge(a_ps, n + 1)
                        if n >= 2:
                            act.wait_ge(h_ps, n - 1)
                        act.activation(aT[:, t % 2, :], bA[t % 2][:, :], ACT.Relu).then_inc(a_sb, 1)
                    if 1 <= t < TG + 1:
                        act.wait_ge(h_ps, n)
                        if n >= 2:
                            act.wait_ge(o_ps, n - 1)
                        act.activation(hoT[:, :, :].rearrange("p m n -> p (m n)"), psH, ACT.Copy).then_inc(h_sb, 1)
                    if t >= 2:
                        act.wait_ge(o_ps, n - 1)
                        if t == 2 and g >= 2:
                            act.wait_ge(x_new, g - 1)
                        act.activation(o[:, g % 2, t - 2, :], psO, ACT.Copy).then_inc(o_sb, 1)

            def norm_o(g):
                act.wait_ge(rst[1], g + 1)
                for t in range(TG):
                    scaled(1, t, o[:, g % 2, t, :], o[:, g % 2, t, :]).then_inc(o_norm, 1)

            def second_norm(g):
                act.wait_ge(rst[2], g + 1)
                if g == GB:
                    act.wait_ge(g_ps, KT // 2)
                for t in range(TG):
                    scaled(2, t, yn[:, (g % GB) * TG + t, :], x[:, g * TG + t, :]).then_inc(yn_ready, 1)

            def put_norm(g):
                b, at = g // GB, (g % GB) * GT
                act.wait_ge(ynT_ps, g + 1)
                for c in range(C):
                    act.activation(ynT[:, b, c, at:at + GT], bT[c][:, :], ACT.Copy).then_inc(ynT_sb, 1)
                for m in range(2):
                    act.wait_ge(s_ps, g * 2 + (m + 1))
                    act.activation(s_all[:, m, at:at + GT], bA[m][:, :], ACT.Identity,
                                   bias=dconst[:, m:m + 1]).then_inc(s_sb, 1)

            def exponentials(b):
                for m in range(2):
                    act.wait_ge(maxed, NMX * (b + 1))
                    act.activation(s_all[:, m, :], s_all[:, m, :], ACT.Exp, bias=nmax[:, m:m + 1],
                                   accum_out=ssum[:, m:m + 1]).then_inc(exped, 1)

            def put_probabilities(b):
                for k in range(KT // 2):
                    n = b * (KT // 2) + k
                    act.wait_ge(pT_ps, n + 1)
                    if n >= 2:
                        act.wait_ge(g_ps, n - 1)
                    act.activation(pT[:, k % 2, :], bA[k % 2][:, :], ACT.Copy).then_inc(pT_sb, 1)

            norm_y(0, guard=False)
            put_yT(0, guard=False)
            norm_y(1)
            put_scores(0, 0, range(TG))
            put_yT(1)
            put_scores(1, 0, range(2))
            with act.Fori(0, GB - 2) as i:
                clamp(i)
                norm_y(i + 2)
                put_scores(i + 1, 0, range(2, TG))
                put_yT(i + 2)
                put_scores(i + 2, 0, range(2))
                signs(i, 0)
            for i in range(GB - 2, NG):
                g = i - GB
                b1_, b2_ = (i + 1) // GB, (i + 2) // GB
                clamp(i)
                if g > 0:
                    norm_o(g - 1)
                if i + 2 < NG:
                    norm_y(i + 2)
                if g >= 0:
                    put_heads(g, range(3))
                if i + 1 < NG:
                    put_scores(i + 1, b1_, range(2, TG))
                if g > 0:
                    second_norm(g - 1)
                if g >= 0:
                    put_heads(g, range(3, TG + 2))
                if i + 2 < NG:
                    put_yT(i + 2)
                if g > 0:
                    put_norm(g - 1)
                if i + 2 < NG:
                    put_scores(i + 2, b2_, range(2))
                signs(i, i // GB)
            for g in range(GB, NG):
                norm_o(g - 1)
                if g == GB + 1:
                    put_heads(g)
                    exponentials(0)
                    put_probabilities(0)
                second_norm(g - 1)
                if g != GB + 1:
                    put_heads(g)
                put_norm(g - 1)
            norm_o(NG - 1)
            second_norm(NG - 1)
            put_norm(NG - 1)
            exponentials(1)
            put_probabilities(1)

            with act.Fori(0, NE) as e:
                act.wait_ge(pred, e + 1)
                act.activation(gate, pre, ACT.Silu).then_inc(silued, 1)

            def exps(j, q):
                act.wait_ge(c_sub, j * 2 + 2)
                act.activation(prob[:, q, :, :], prob[:, q, :, :], ACT.Exp).then_inc(c_exp, 1)

            def outs(j, q, guard=True):
                for u in range(2):
                    act.wait_ge(c_pT_ps, j * 2 + (u + 1))
                    act.activation(cpT[:, u, :], bA[u][:, :], ACT.Copy).then_inc(c_pT_sb, 1)
                for u in range(2):
                    act.wait_ge(co_ps, j * 2 + (u + 1))
                    if guard and u == 0:
                        act.wait_ge(stored[q], (j - q) * 8)
                    act.activation(co[:, q, 2 * u:2 * u + 2, :], bank[6 + u][:, :], ACT.Copy).then_inc(co_sb, 1)

            exps(0, 0)
            exps(1, 1)
            outs(0, 0, guard=False)
            exps(2, 0)
            outs(1, 1, guard=False)
            with act.Fori(1, NG // 2 - 1) as h:
                exps(h * 2 + 1, 1)
                outs(h * 2, 0)
                exps(h * 2 + 2, 0)
                outs(h * 2 + 1, 1)
            exps(NG - 1, 1)
            outs(NG - 2, 0)
            outs(NG - 1, 1)

        @block.tensor
        def _(pe):
            pe.wait_ge(consts, 14 + TOP)
            pe.wait_ge(w_in, 16 * N_W1)
            for c in range(C):
                pe.transpose(bank[0][:, c * NS:(c + 1) * NS], kp[:, c::C], ident[0:NS, 0:NS])
                pe.transpose(bank[0][:, 64 + c * NE:64 + (c + 1) * NE], sq[:, c::C], ident[0:NE, 0:NE])
                pe.transpose(bank[0][:, 96 + c * NE:96 + (c + 1) * NE], b2[:, c::C], ident[0:NE, 0:NE])
            pe.transpose(bank[0][:, 128:146], brow, ident[0:18, 0:18]).then_inc(pe_part, 1)
            for w, bk in ((aWq, 1), (dWk, 2)):
                for m in range(2):
                    for c in range(C):
                        mm = pe.transpose(bank[bk][:, (m * 2 + c) * P:(m * 2 + c + 1) * P], w[:, c, m * P:(m + 1) * P],
                                          ident[:, :])
                mm.then_inc(pe_part, 1)
            pe.wait_ge(dve_part, M_MISC)
            for m in range(2):
                for c in range(C):
                    pe.matmul(bank[4][:, m * NS:(m + 1) * NS], aWk[:, c, m * P:(m + 1) * P], kpT[:, c, :],
                              start=(c == 0), stop=(c == 1))
            for m in range(2):
                for c in range(C):
                    mm = pe.matmul(bank[4][:, 64 + m * NE:64 + (m + 1) * NE], dWq[:, c, m * P:(m + 1) * P], sqT[:, c, :],
                                   start=(c == 0), stop=(c == 1))
            mm.then_inc(pe_part, 1)
            pe.wait_ge(dve_part, M_KQ)
            for c in range(C):
                for m in range(2):
                    mm = pe.matmul(bank[c][:, m * 256:(m + 1) * 256], aWqT[:, m, c, :], bdK[:, m, :, :],
                                   start=True, stop=True)
            mm.then_inc(pe_part, 1)
            for m in range(2):
                mm = pe.matmul(bank[6][0:3, m * 256:(m + 1) * 256], bq3[:, 0, m, :], bdK[:, m, :, :], start=True, stop=True)
            mm.then_inc(pe_part, 1)
            for m in range(2):
                pe.matmul(bank[5][:, 0:D], aKT4[:, m, :], aWv[:, m, :], start=(m == 0), stop=False)
            pe.matmul(bank[5][:, 0:D], ones1, bvrow, start=False, stop=True).then_inc(pe_part, 1)
            for c in range(C):
                for m in range(2):
                    pe.matmul(bank[4][:, c * D + m * P:c * D + (m + 1) * P], dWkT[:, m, c, :], bdQ[:, m, :, :],
                              start=True, stop=True)
            for m in range(2):
                mm = pe.matmul(bank[7][:, m:m + 1], bdQ[:, m, :, :], bcol[:, DBK, m:m + 1], start=True, stop=True)
            mm.then_inc(pe_part, 1)

            def turn_y(i):
                pe.wait_ge(y_ready, i * TG + TG)
                if i > 0:
                    pe.wait_ge(yT_sb, 2 * i)
                for t in range(TG):
                    for c in range(C):
                        mm = pe.transpose(bT[c][:, t * P:(t + 1) * P], y[:, t, c::C], ident[:, :])
                mm.then_inc(yT_ps, 1)

            def scores_of(i, tiles):
                pe.wait_ge(yT_sb, i * 2 + 2)
                for t in tiles:
                    n = i * TG + t
                    if n >= 2:
                        pe.wait_ge(topped, n - 1)
                    pe.matmul(bZ[t % 2][:, :], ones3[:, :], zb3[:, :], start=True, stop=False)
                    for c in range(C):
                        mm = pe.matmul(bZ[t % 2][:, :], yT[:, c, t * P:(t + 1) * P], Wz[:, c, :],
                                       start=False, stop=(c == C - 1))
                    mm.then_inc(z_ps, 1)

            def heads_of(g, steps=range(TG + 2)):
                b = g // GB
                pe.wait_ge(settled, b + 1)
                if g >= 2:
                    pe.wait_ge(s_sb, 2 * (g - 1))
                w = scr[b].rearrange("p h j s -> p h (j s)")
                for t in steps:
                    n = g * TG + t
                    if t < TG:
                        if n >= 2:
                            pe.wait_ge(a_sb, n - 1)
                        for k in range(4):
                            mm = pe.transpose(bA[t % 2][:, k * P:(k + 1) * P], w[:, n - b * NH, k * P:(k + 1) * P], ident[:, :])
                        mm.then_inc(a_ps, 1)
                    if 1 <= t < TG + 1:
                        pe.wait_ge(a_sb, n)
                        pe.wait_ge(bd_ready, n)
                        if n >= 2:
                            pe.wait_ge(h_sb, n - 1)
                        for m in range(2):
                            for half in range(2):
                                mm = pe.matmul(psH[:, m * P:(m + 1) * P], bdh[:, t - 1, half, :],
                                               aT[:, (t - 1) % 2, (2 * m + half) * P:(2 * m + half + 1) * P],
                                               start=(half == 0), stop=(half == 1))
                        mm.then_inc(h_ps, 1)
                    if t >= 2:
                        pe.wait_ge(h_sb, n - 1)
                        if n >= 3:
                            pe.wait_ge(o_sb, n - 2)
                        pe.matmul(psO, ones3[:, :], ab3[:, 0:D], start=True, stop=False)
                        for m in range(2):
                            mm = pe.matmul(psO, hoT[:, m, :], aWo[:, m, :], start=False, stop=(m == 1))
                        mm.then_inc(o_ps, 1)

            def norm_of(g):
                b, gb = g // GB, g % GB
                pe.wait_ge(yn_ready, (g + 1) * TG)
                if g == 0:
                    pe.wait_ge(yT_sb, 2 * NG)
                else:
                    pe.wait_ge(ynT_sb, 2 * g)
                for t in range(TG):
                    for c in range(C):
                        mm = pe.transpose(bT[c][:, t * P:(t + 1) * P], yn[:, gb * TG + t, c::C], ident[:, :])
                mm.then_inc(ynT_ps, 1)
                pe.wait_ge(ynT_sb, 2 * (g + 1))
                for m in range(2):
                    if g > 0:
                        pe.wait_ge(s_sb, 2 * g)
                    for c in range(C):
                        mm = pe.matmul(bA[m][:, :], Wd[:, c, m * P:(m + 1) * P], ynT[:, b, c, gb * GT:(gb + 1) * GT],
                                       start=(c == 0), stop=(c == C - 1))
                    mm.then_inc(s_ps, 1)

            def sums(b):
                pe.wait_ge(s_sb, 2 * GB * (b + 1))
                pe.wait_ge(exped, 2 * b + 2)
                for k in range(KT // 2 + 1):
                    if k < KT // 2:
                        n = b * (KT // 2) + k
                        if n >= 2:
                            pe.wait_ge(pT_sb, n - 1)
                        for u in range(2):
                            for m in range(2):
                                mm = pe.transpose(bA[k % 2][:, (u * 2 + m) * P:(u * 2 + m + 1) * P],
                                                  s_all[:, m, (2 * k + u) * P:(2 * k + u + 1) * P], ident[:, :])
                        mm.then_inc(pT_ps, 1)
                    if k >= 1:
                        pe.wait_ge(pT_sb, b * (KT // 2) + k)
                        for u in range(2):
                            kt = 2 * (k - 1) + u
                            for m in range(2):
                                mm = pe.matmul(bZ[m][:, 0:D], pT[:, (k - 1) % 2, (u * 2 + m) * P:(u * 2 + m + 1) * P],
                                               yn[:, kt, :], start=(kt == 0), stop=(kt == KT - 1))
                        mm.then_inc(g_ps, 1)

            def to_slots(b, step):
                pe.wait_ge(dve_part, PREP + b * MS + (S_G, S_GT, S_ZM, S_H, S_SLOT)[step])
                if step == 0:
                    for c in range(C):
                        for m in range(2):
                            mm = pe.transpose(bZ[0][:, (c * 2 + m) * P:(c * 2 + m + 1) * P], gn[:, m, c::C], ident[:, :])
                elif step == 1:
                    for m in range(2):
                        for c in range(C):
                            mm = pe.matmul(bZ[1][:, m * P:(m + 1) * P], gT[:, c, m, :], dWv[:, c, m * P:(m + 1) * P],
                                           start=(c == 0), stop=(c == C - 1))
                elif step == 2:
                    for m in range(2):
                        mm = pe.matmul(bZ[0][:, m * NE:(m + 1) * NE], zm[:, m, :], sel[:, :], start=True, stop=True)
                elif step == 3:
                    for m in range(2):
                        mm = pe.matmul(bZ[1][0:NE, 0:D], hT[:, m, :], dWo[:, m, :], start=(m == 0), stop=(m == 1))
                else:
                    for c in range(C):
                        pe.transpose(bZ[0][:, c * NE:(c + 1) * NE], slot[:, c::C], ident[0:NE, 0:NE])
                        mm = pe.transpose(bZ[0][:, 32 + c * NE:32 + (c + 1) * NE], hid[:, c::C], ident[0:NE, 0:NE])
                mm.then_inc(pe_part, 1)

            pe.wait_ge(dve_part, PREP)
            turn_y(0)
            scores_of(0, range(2))
            turn_y(1)
            scores_of(0, range(2, TG))
            scores_of(1, range(2))
            for i in range(NG):
                g = i - GB
                if g >= 0:
                    heads_of(g, range(3))
                if i + 1 < NG:
                    scores_of(i + 1, range(2, TG))
                if g >= 0:
                    heads_of(g, range(3, TG + 2))
                if i + 2 < NG:
                    turn_y(i + 2)
                if g > 0:
                    norm_of(g - 1)
                if i + 2 < NG:
                    scores_of(i + 2, range(2))
            heads_of(4)
            norm_of(3)
            heads_of(5)
            pe.wait_ge(w_in2, 16 * N_W2)
            sums(0)
            norm_of(4)
            to_slots(0, 0)
            heads_of(6)
            to_slots(0, 1)
            norm_of(5)
            to_slots(0, 2)
            heads_of(7)
            to_slots(0, 3)
            norm_of(6)
            to_slots(0, 4)
            norm_of(7)
            pe.wait_ge(dve_part, PREP + MS)
            sums(1)
            for step in range(5):
                to_slots(1, step)

            pe.wait_ge(w_in3, 16 * N_W3)
            for m in range(2):
                for c in range(C):
                    mm = pe.transpose(bank[6][:, (m * 2 + c) * P:(m * 2 + c + 1) * P], cWq[:, c, m * P:(m + 1) * P], ident[:, :])
            for g, rows_ in ((0, b1), (1, bg)):
                mm = pe.transpose(bank[7][:, g * P:(g + 1) * P], rows_, ident[:, :])
            mm.then_inc(pe_part, 1)

            pe.wait_ge(dve_part, PREP + 2 * MS)

            def grow(e, it, q, g, recent=True):
                if g == 0:
                    pe.wait_ge(hcol_ready, e + 1)
                    if recent:
                        pe.wait_ge(ug_sb, e - 2)
                pe.wait_ge(e_in[q][g], it * 16 + 16)
                for c in range(C):
                    for half in range(2):
                        k = 2 * g + half
                        mm = pe.matmul(bank[q][32 * k:32 * k + 32, :], hcol[:, q, c, :],
                                       ring[q][:, g, c * FF + half * 512:c * FF + (half + 1) * 512],
                                       start=(c == 0), stop=(c == C - 1))
                mm.then_inc(up_ps, 1)

            def turn_up(e, q):
                pe.wait_ge(ug_sb, e + 1)
                for j in range(4):
                    mm = pe.transpose(bank[3 + q][:, j * P:(j + 1) * P], ugT[q][:, j * P:(j + 1) * P], ident[:, :])
                mm.then_inc(ugT_ps, 1)

            def turn_down(e, first=False):
                pe.wait_ge(dn_sb, e + 1)
                if not first:
                    pe.wait_ge(down_sb, e)
                pe.nop(nofuse=True)
                for c in range(C):
                    mm = pe.transpose(bank[7][:, c * NB:(c + 1) * NB], dn[:, c::C], ident[0:NB, 0:NB])
                mm.then_inc(dnT_ps, 1)

            def shrink(e, it, q):
                pe.wait_ge(e_in[q][2], it * 16 + 16)
                pe.wait_ge(ug_ready, e + 1)
                for j in range(J):
                    mm = pe.matmul(bank[6][0:NB, 0:D], ug[:, q, j, :], ring[q][:, 2, j * D:(j + 1) * D],
                                   start=(j == 0), stop=(j == J - 1))
                mm.then_inc(down_ps, 1)

            def expert(h, k, first=False, last=False, recent=True):
                e, q, n = h * 3 + k, k % 3, (k + 1) % 3
                if not last:
                    grow(e + 1, h + (k + 1) // 3, n, 0, recent)
                turn_up(e, q)
                if not first:
                    turn_down(e - 1, first=recent is False and k == 1)
                if not last:
                    grow(e + 1, h + (k + 1) // 3, n, 1, recent)
                shrink(e, h + k // 3, q)

            pe.wait_ge(hbias, 1)
            grow(0, 0, 0, 0, recent=False)
            grow(0, 0, 0, 1, recent=False)
            expert(0, 0, first=True, recent=False)
            expert(0, 1, recent=False)
            with pe.Fori(0, 4) as h:
                for k in range(2, 5):
                    expert(h, k)
            expert(4, 2)
            expert(4, 3, last=True)
            turn_down(NE - 1)

            pe.wait_ge(down_sb, NE)
            for w, at in ((cWk, 0), (cWv, 64)):
                for m in range(2):
                    for c in range(C):
                        mm = pe.matmul(bank[0][:, at + m * 32:at + (m + 1) * 32], w[:, c, m * P:(m + 1) * P],
                                       newT[:, c, :, :], start=(c == 0), stop=(c == C - 1))
            mm.then_inc(pe_part, 1)
            pe.wait_ge(dve_part, CS + 1)
            for b in range(NB):
                for c in range(C):
                    for m in range(2):
                        pe.matmul(bank[1 + b][:, c * D + m * P:c * D + (m + 1) * P], cWqT[:, m, c, :], cbK[:, m, b, :, :],
                                  start=True, stop=True)
                for m in range(2):
                    pe.matmul(bank[3 + b][:, m * D:(m + 1) * D], cbV[:, m, b, :, :], cWo[:, m, :], start=True, stop=True)
                for m in range(2):
                    mm = pe.matmul(bank[5][0:3, b * D + m * P:b * D + (m + 1) * P], bq3[:, 1, m, :], cbK[:, m, b, :, :],
                                   start=True, stop=True)
            mm.then_inc(pe_part, 1)
            pe.wait_ge(dve_part, CS + 2)

            def scores(j, q, b, first=False):
                pe.wait_ge(c_in, j + 1)
                for t in range(TG):
                    u = t // 2
                    if t % 2 == 0 and not first:
                        pe.wait_ge(c_sub, j * 2 + (u - 1))
                    ps = bank[u][:, (t % 2) * D:(t % 2 + 1) * D]
                    pe.matmul(ps, ones3[:, :], cb3[:, b * D:(b + 1) * D], start=True, stop=False)
                    for c in range(C):
                        mm = pe.matmul(ps, cin[:, q, c, t * P:(t + 1) * P], Wc[:, b, c, :], start=False, stop=(c == C - 1))
                    if t % 2:
                        mm.then_inc(c_ps, 1)

            def outputs(j, q, b, first=False):
                pe.wait_ge(c_prob, j + 1)
                for u in range(2):
                    if not first:
                        pe.wait_ge(c_pT_sb, j * 2 + (u - 1))
                    for v in range(2):
                        for m in range(2):
                            mm = pe.transpose(bA[u][:, (v * 2 + m) * P:(v * 2 + m + 1) * P],
                                              prob[:, q, 2 * u + v, m * P:(m + 1) * P], ident[:, :])
                    mm.then_inc(c_pT_ps, 1)
                for u in range(2):
                    pe.wait_ge(c_pT_sb, j * 2 + (u + 1))
                    if not first:
                        pe.wait_ge(co_sb, j * 2 + (u - 1))
                    for v in range(2):
                        ps = bank[6 + u][:, v * D:(v + 1) * D]
                        pe.matmul(ps, ones3[:, :], ab3[:, D:2 * D], start=True, stop=False)
                        for m in range(2):
                            mm = pe.matmul(ps, cpT[:, u, (v * 2 + m) * P:(v * 2 + m + 1) * P], Vc[:, b, m, :],
                                           start=False, stop=(m == 1))
                    mm.then_inc(co_ps, 1)

            scores(0, 0, 0, first=True)
            scores(1, 1, 0)
            outputs(0, 0, 0, first=True)
            scores(2, 0, 0)
            outputs(1, 1, 0)
            scores(3, 1, 0)
            outputs(2, 0, 0)
            scores(4, 0, 1)
            outputs(3, 1, 0)
            with pe.Fori(2, NG // 2 - 1) as h:
                scores(h * 2 + 1, 1, 1)
                outputs(h * 2, 0, 1)
                scores(h * 2 + 2, 0, 1)
                outputs(h * 2 + 1, 1, 1)
            scores(NG - 1, 1, 1)
            outputs(NG - 2, 0, 1)
            outputs(NG - 1, 1, 1)

        @block.vector
        def _(v):
            steps = [0]

            def hold(s, value):
                v.wait_ge(s, value)
                v.nop(nofuse=True)

            def own(ins, wait=True):
                steps[0] += 1
                ins.then_inc(prep, 1)
                if wait:
                    v.wait_ge(prep, steps[0])

            def split3(dst, src):
                h = aT[0:3, :, :].rearrange("p a n -> p (a n)").bitcast(BF16)
                hs = [h[:, 512 * k:512 * (k + 1)] for k in range(3)]
                r = o[0:3, 0, :, :].rearrange("p t n -> p (t n)")
                r1, r2 = r[:, 0:512], r[:, 512:1024]
                t0 = y[0:3, :, :].rearrange("p t n -> p (t n)")[:, 0:512]
                t1 = y[0:3, :, :].rearrange("p t n -> p (t n)")[:, 512:1024]
                own(v.tensor_copy(hs[0], src))
                own(v.tensor_tensor(r1, src, hs[0], ALU.subtract))
                own(v.tensor_copy(hs[1], r1))
                own(v.tensor_tensor(r2, r1, hs[1], ALU.subtract))
                own(v.tensor_copy(hs[2], r2))
                own(v.tensor_scalar(t0, hs[0], ident[0:3, 0:1], None, ALU.mult))
                own(v.scalar_tensor_tensor(out=t1, in0=hs[1], scalar=ident[0:3, 1:2], in1=t0, op0=ALU.mult, op1=ALU.add))
                return v.scalar_tensor_tensor(out=dst, in0=hs[2], scalar=ident[0:3, 2:3], in1=t1, op0=ALU.mult, op1=ALU.add)

            def spread(dst, src, m):
                n = src.shape[1]
                return v.tensor_tensor(dst, src.unsqueeze(1).broadcast_to([P, 8, n]),
                                       m[:, :].unsqueeze(2).broadcast_to([P, 8, n]), ALU.mult)

            v.wait_ge(consts, 14 + TOP)
            own(v.tensor_reduce(sel[:, :], ident[:, :].rearrange("p (h e) -> p e h", e=NE), AX_X, ALU.add))
            v.wait_ge(pe_part, M_MISC)
            v.tensor_copy(miscT[:, :], bank[0][:, 0:146]).then_inc(dve_part, 1)
            v.wait_ge(pe_part, M_AQ)
            v.tensor_copy(aWqT.rearrange("p m c q -> p (m c q)"), bank[1][:, :]).then_inc(dve_part, 1)
            v.wait_ge(pe_part, M_DK)
            v.tensor_copy(dWkT.rearrange("p m c q -> p (m c q)"), bank[2][:, :]).then_inc(dve_part, 1)
            v.wait_ge(dve_part, M_DK)
            v.wait_ge(pe_part, M_KQ)
            for a, k in ((0, ABQ), (1, CBQ)):
                for m in range(2):
                    own(v.tensor_copy(bq3[:, a, m, :], bcol[:, k, m:m + 1].broadcast_to([P, 3])), wait=False)
            for m in range(2):
                own(v.tensor_scalar(aKT[:, m, :], bank[4][:, m * NS:(m + 1) * NS], bcol[:, ABK, m:m + 1], None, ALU.add), wait=False)
                own(v.tensor_scalar(dQT[:, m, :], bank[4][:, 64 + m * NE:64 + (m + 1) * NE], bcol[:, DBQ, m:m + 1], None, ALU.add))
            for m in range(2):
                own(v.tensor_copy(aKT4[:, m, :].rearrange("p (j s) -> p j s", j=4),
                                  aKT[:, m, :].unsqueeze(1).broadcast_to([P, 4, NS])), wait=False)
                own(spread(bdK[:, m, :, :], aKT[:, m, :], masks), wait=False)
            own(spread(bdQ[:, 0, :, :], dQT[:, 0, :], masks), wait=False)
            spread(bdQ[:, 1, :, :], dQT[:, 1, :], masks).then_inc(dve_part, 1)
            v.wait_ge(pe_part, M_WZ)
            own(v.tensor_copy(Wz[:, 0, :], bank[0][:, :]), wait=False)
            v.tensor_copy(Wz[:, 1, :], bank[1][:, :]).then_inc(dve_part, 1)
            v.wait_ge(pe_part, M_ZB)
            split3(zb3[:, :], bank[6][0:3, :]).then_inc(dve_part, 1)
            v.wait_ge(dve_part, M_ZB)
            own(split3(ab3[:, :], bo3.rearrange("p a d -> p (a d)")))
            v.wait_ge(pe_part, M_V)
            v.tensor_copy(vrep[:, :, :].rearrange("p h e -> p (h e)"), bank[5][:, 0:D]).then_inc(dve_part, 1)
            v.wait_ge(pe_part, M_WD)
            own(v.tensor_copy(Wd[:, :, :].rearrange("p c n -> p (c n)"), bank[4][:, :]), wait=False)
            v.tensor_copy(dconst[:, :], bank[7][:, 0:2]).then_inc(dve_part, 1)

            def statistics(k, i, src):
                for t in range(TG):
                    v.bn_stats(stats[:, k, t, :], src(t)).then_inc(stat[k], 1)
                hold(stat[k], i * TG + TG)
                for t in range(TG):
                    v.bn_aggr(mv[:, k, t, :], stats[:, k, t, :]).then_inc(mean[k], 1)

            def xtile(i, t):
                return x[:, bass.ds(i * TG + t, 1), :].rearrange("p o d -> p (o d)")

            rows = [P, NH, TG, NS]
            d3 = d[:, :].rearrange("p (h t s) -> p h t s", h=NH, t=TG)
            a3 = above[:, :].rearrange("p (h t s) -> p h t s", h=NH, t=TG)
            tau3 = tau[:, :].rearrange("p (h t) -> p h t", h=NH).unsqueeze(3).broadcast_to(rows)
            rcnt3 = rcnt[:, :].rearrange("p (h t) -> p h t", h=NH).unsqueeze(3).broadcast_to(rows)

            def first_statistics(i):
                hold(xin_in, i * 16 + 16)
                statistics(0, i, lambda t: xin[:, t, :])

            def sort_top(i, tiles):
                for t in tiles:
                    hold(z_sb, i * TG + (t + 1))
                    for h in range(NH):
                        mx = v.max(top[:, h * TG + t, :], bZ[t % 2][:, h * NS:(h + 1) * NS])
                    mx.then_inc(topped, 1)

            def threshold(i):
                v.wait_ge(topped, i * TG + TG)
                for k in range(1, TOP):
                    v.tensor_tensor(top[:, :, k], top[:, :, k], top[:, :, k - 1], ALU.add).then_inc(cum, 1)
                    v.wait_ge(cum, i * 9 + k)
                v.scalar_tensor_tensor(out=top[:, :, :], in0=top[:, :, :], scalar=-1.0,
                                       in1=rk[:, :].unsqueeze(1).broadcast_to([P, HR, TOP]),
                                       op0=ALU.add, op1=ALU.mult).then_inc(cum, 1)
                v.wait_ge(cum, i * 9 + 8)
                v.tensor_reduce(tau[:, :], top[:, :, :], AX_X, ALU.max).then_inc(cum, 1)

            def scores_at(i, b):
                return scr[b][:, :, bass.ds(i * TG - b * KT, TG), :]

            def subtract(i, b):
                v.wait_ge(cum, i * 9 + 9)
                v.tensor_tensor(d3, scores_at(i, b), tau3, ALU.subtract).then_inc(diff, 1)

            def count(i):
                v.wait_ge(relued, i + 1)
                if not (isinstance(i, int) and i == 0):
                    v.wait_ge(signed, i)
                v.tensor_scalar(above[:, :], d[:, :], 0.0, None, ALU.is_gt).then_inc(newton, 1)
                v.tensor_reduce(exc[:, :], d3, AX_X, ALU.add).then_inc(newton, 1)
                v.wait_ge(newton, i * NW + 1)
                v.tensor_reduce(cnt[:, :], a3, AX_X, ALU.add).then_inc(newton, 1)

            def settle(i, b):
                v.wait_ge(newton, i * NW + 3)
                v.tensor_scalar(cnt[:, :], cnt[:, :], 1.0, None, ALU.max).then_inc(newton, 1)
                v.wait_ge(newton, i * NW + 4)
                v.tensor_reduce(tot[:, 0, bass.ds(i - b * GB, 1)], cnt[:, :], AX_X, ALU.add).then_inc(newton, 1)
                v.reciprocal(rcnt[:, :], cnt[:, :]).then_inc(newton, 1)
                v.wait_ge(newton, i * NW + 6)
                v.scalar_tensor_tensor(out=rcnt[:, :], in0=exc[:, :], scalar=-1.0, in1=rcnt[:, :],
                                       op0=ALU.add, op1=ALU.mult).then_inc(newton, 1)
                if not (isinstance(i, int) and i == 0):
                    v.wait_ge(lowered, i)
                v.wait_ge(newton, i * NW + 7)
                v.tensor_tensor(tauf[:, :], tau[:, :], rcnt[:, :], ALU.add).then_inc(tau_ready, 1)

            def check(b):
                v.wait_ge(signed, GB * (b + 1))
                v.wait_ge(newton, GB * (b + 1) * NW)
                v.tensor_scalar(tot[:, 1, :], ahead[:, b * GB:(b + 1) * GB], float(HR * NS), 0.5, ALU.add, ALU.mult)\
                    .then_inc(checked, 1)
                v.wait_ge(checked, b * 5 + 1)
                v.tensor_tensor(tot[:, 1, :], tot[:, 1, :], tot[:, 0, :], ALU.not_equal).then_inc(checked, 1)
                v.wait_ge(checked, b * 5 + 2)
                v.tensor_reduce(moved[:, 0:1], tot[:, 1, :], AX_X, ALU.max).then_inc(checked, 1)
                v.wait_ge(checked, b * 5 + 3)
                v.transpose(movedT[:, :], moved[:, :]).then_inc(checked, 1)
                v.wait_ge(checked, b * 5 + 4)
                v.tensor_reduce(flagi[:, :], movedT[:, :], AX_X, ALU.max).then_inc(checked, 1)
                hold(checked, b * 5 + 5)
                parts = [v.value_load(flagi[32 * k:32 * k + 1, 0:1]) for k in range(4)]
                with v.If(parts[0] + parts[1] + parts[2] + parts[3] > 0):
                    with v.Fori(0, GB) as g:
                        z3 = scr[b][:, :, bass.ds(g * TG, TG), :]
                        with v.Fori(0, FIXES) as s:
                            at = g * (FIXES * 8) + s * 8 + b * (GB * FIXES * 8)
                            v.tensor_scalar(a3, z3, 0.0, None, ALU.is_gt).then_inc(fix, 1)
                            v.tensor_scalar(d3, z3, 0.0, None, ALU.max).then_inc(fix, 1)
                            v.wait_ge(fix, at + 2)
                            v.tensor_reduce(cnt[:, :], a3, AX_X, ALU.add).then_inc(fix, 1)
                            v.tensor_reduce(exc[:, :], d3, AX_X, ALU.add).then_inc(fix, 1)
                            v.wait_ge(fix, at + 4)
                            v.tensor_scalar(cnt[:, :], cnt[:, :], 1.0, None, ALU.max).then_inc(fix, 1)
                            v.wait_ge(fix, at + 5)
                            v.reciprocal(rcnt[:, :], cnt[:, :]).then_inc(fix, 1)
                            v.wait_ge(fix, at + 6)
                            v.scalar_tensor_tensor(out=rcnt[:, :], in0=exc[:, :], scalar=-1.0, in1=rcnt[:, :],
                                                   op0=ALU.add, op1=ALU.mult).then_inc(fix, 1)
                            v.wait_ge(fix, at + 7)
                            v.tensor_tensor(z3, z3, rcnt3, ALU.subtract).then_inc(fix, 1)
                            v.wait_ge(fix, at + 8)
                with v.Else():
                    v.sem_inc(fix, GB * FIXES * 8)
                v.tensor_copy(flag[:, :], moved[:, 0:1]).then_inc(settled, 1)

            def output_statistics(g):
                for t in range(TG):
                    v.wait_ge(o_sb, g * TG + (t + 1))
                    v.bn_stats(stats[:, 1, t, :], o[:, g % 2, t, :]).then_inc(stat[1], 1)
                v.wait_ge(stat[1], g * TG + TG)
                for t in range(TG):
                    v.bn_aggr(mv[:, 1, t, :], stats[:, 1, t, :]).then_inc(mean[1], 1)

            def join(g):
                v.wait_ge(o_norm, g * TG + TG)
                tiles = x[:, g * TG:(g + 1) * TG, :]
                v.tensor_tensor(tiles, tiles, o[:, g % 2, :, :], ALU.add).then_inc(x_new, 1)
                v.wait_ge(x_new, g + 1)
                if g > 0:
                    v.wait_ge(rst[2], g)
                statistics(2, g, lambda t: x[:, g * TG + t, :])

            def group_maximum(g):
                v.wait_ge(s_sb, 2 * g + 2)
                at = (g % GB) * GT
                for m in range(2):
                    v.tensor_reduce(pmax[:, m, g % GB:g % GB + 1], s_all[:, m, at:at + GT], AX_X, ALU.max).then_inc(maxed, 1)

            def batch_maximum(b):
                v.wait_ge(maxed, NMX * b + NMX - 2)
                v.tensor_reduce(smax[:, :], pmax[:, :, :], AX_X, ALU.max).then_inc(maxed, 1)
                v.wait_ge(maxed, NMX * b + NMX - 1)
                v.tensor_scalar(nmax[:, :], smax[:, :], -1.0, None, ALU.mult).then_inc(maxed, 1)

            def to_slots(b, step):
                p0, s0 = PREP + b * ND, b * NSL
                if step == 0:
                    v.wait_ge(exped, 2 * b + 2)
                    v.reciprocal(rsum[:, :], ssum[:, :]).then_inc(slots, 1)
                    v.wait_ge(slots, s0 + 1)
                    v.wait_ge(g_ps, (b + 1) * (KT // 2))
                    v.tensor_scalar(gn[:, 0, :], bZ[0][:, 0:D], rsum[:, 0:1], None, ALU.mult).then_inc(slots, 1)
                    v.tensor_scalar(gn[:, 1, :], bZ[1][:, 0:D], rsum[:, 1:2], None, ALU.mult).then_inc(dve_part, 1)
                elif step == 1:
                    v.wait_ge(pe_part, p0 + D_GT)
                    v.tensor_copy(gT.rearrange("p c m n -> p (c m n)"), bZ[0][:, :]).then_inc(dve_part, 1)
                elif step == 2:
                    v.wait_ge(pe_part, p0 + D_Z)
                    for m in range(2):
                        z_ = v.tensor_tensor(zm[:, m, :].rearrange("p (h j) -> p h j", h=8),
                                             bZ[1][:, m * P:(m + 1) * P].rearrange("p (h j) -> p h j", h=8),
                                             mask[:, :].unsqueeze(2).broadcast_to([P, 8, DH]), ALU.mult)
                        z_.then_inc((slots, dve_part)[m], 1)
                elif step == 3:
                    v.wait_ge(pe_part, p0 + D_H)
                    for m in range(2):
                        h_ = v.tensor_scalar(hT[:, m, :], bZ[0][:, m * NE:(m + 1) * NE], bcol[:, DBV, m:m + 1], None, ALU.add)
                        h_.then_inc((slots, dve_part)[m], 1)
                elif step == 4:
                    v.wait_ge(pe_part, p0 + D_SLOT)
                    v.tensor_tensor(slot, bZ[1][0:NE, 0:D], sq[:, :], ALU.add).then_inc(slots, 1)
                    v.wait_ge(slots, s0 + 5)
                    v.bn_stats(sstats[:, :], slot).then_inc(smean, 1)
                    v.wait_ge(smean, 2 * b + 1)
                    v.bn_aggr(smv[:, :], sstats[:, :]).then_inc(smean, 1)
                    v.wait_ge(smean, 2 * b + 2)
                    v.wait_ge(srst, 2 * b + 2)
                    v.tensor_scalar(hid, slot, smv[:, 0:1], srstd[:, 0:1], ALU.subtract, ALU.mult).then_inc(slots, 1)
                    v.wait_ge(slots, s0 + 6)
                    v.tensor_tensor(hid, hid, lng, ALU.mult).then_inc(slots, 1)
                    v.wait_ge(slots, s0 + 7)
                    v.tensor_tensor(hid, hid, lnb, ALU.add).then_inc(dve_part, 1)
                else:
                    v.wait_ge(pe_part, p0 + D_T)
                    v.tensor_copy(slotT[:, :, b, :], bZ[0][:, 0:32].rearrange("p (c e) -> p c e", c=C)).then_inc(slots, 1)
                    v.tensor_copy(hidT[:, :, b, :], bZ[0][:, 32:64].rearrange("p (c e) -> p c e", c=C)).then_inc(dve_part, 1)
                    v.wait_ge(slots, s0 + NSL)

            NW = 7
            NSL = 8
            first_statistics(0)
            first_statistics(1)
            sort_top(0, range(TG))
            threshold(0)

            def batch_of_scores(i, b):
                subtract(i, b)
                first_statistics(i + 2)
                sort_top(i + 1, range(2))
                count(i)
                sort_top(i + 1, range(2, TG))
                settle(i, b)
                threshold(i + 1)

            batch_of_scores(0, 0)
            with v.Fori(1, GB) as i:
                batch_of_scores(i, 0)
            check(0)
            v.wait_ge(x_in, 16)
            for i in range(GB, NG):
                g = i - GB
                subtract(i, 1)
                if g > 0:
                    output_statistics(g - 1)
                if i + 2 < NG:
                    first_statistics(i + 2)
                if i + 1 < NG:
                    sort_top(i + 1, range(2))
                if g > 0:
                    join(g - 1)
                count(i)
                if i + 1 < NG:
                    sort_top(i + 1, range(2, TG))
                settle(i, 1)
                if i + 1 < NG:
                    threshold(i + 1)
                if g > 1:
                    group_maximum(g - 2)
            output_statistics(3)
            join(3)
            check(1)
            group_maximum(2)
            output_statistics(4)
            join(4)
            group_maximum(3)
            batch_maximum(0)
            v.wait_ge(w_in2, 16 * N_W2)
            own(v.tensor_tensor(sq[:, :], sq[:, :], dbo, ALU.add))
            output_statistics(5)
            join(5)
            to_slots(0, 0)
            group_maximum(4)
            to_slots(0, 1)
            output_statistics(6)
            join(6)
            to_slots(0, 2)
            group_maximum(5)
            to_slots(0, 3)
            output_statistics(7)
            join(7)
            to_slots(0, 4)
            group_maximum(6)
            to_slots(0, 5)
            group_maximum(7)
            batch_maximum(1)
            for step in range(6):
                to_slots(1, step)

            v.wait_ge(pe_part, CP + 1)
            own(v.tensor_copy(cWqT.rearrange("p m c q -> p (m c q)"), bank[6][:, :]), wait=False)
            v.tensor_copy(bT1.rearrange("p e g j -> p g e j"), bank[7][:, 0:2 * P].rearrange("p (g e j) -> p g e j", g=2, j=J))\
                .then_inc(hbias, 1)
            v.wait_ge(hbias, 1)
            for b in range(NB):
                own(v.tensor_tensor(slotT[:, :, b, :], slotT[:, :, b, :], b2T, ALU.add), wait=b == NB - 1)

            def keep_down(e):
                v.wait_ge(down_ps, e + 1)
                v.tensor_copy(dn, bank[6][0:NB, 0:D]).then_inc(dn_sb, 1)

            def add_down(e):
                v.wait_ge(dnT_ps, e + 1)
                v.tensor_tensor(newT[:, :, :, bass.ds(e, 1)].rearrange("p c b o -> p c (b o)"),
                                bank[7][:, 0:C * NB].rearrange("p (c b) -> p c b", c=C),
                                slotT[:, :, :, bass.ds(e, 1)].rearrange("p c b o -> p c (b o)"), ALU.add).then_inc(down_sb, 1)

            def expert(h, k, first=False):
                e, q = h * 3 + k, k % 3
                v.wait_ge(up_ps, e * 2 + 2)
                v.tensor_copy(ugT[q], bank[q][:, :]).then_inc(ug_sb, 1)
                if not first:
                    keep_down(e - 1)
                v.wait_ge(ugT_ps, e + 1)
                v.tensor_tensor(pre.rearrange("p g (a j) b -> p (g a) j b", a=2),
                                bank[3 + q][:, :].rearrange("p (j k x) -> p k j x", j=4, k=4)[:, :, :, 0:NB],
                                bT1[:, bass.ds(e, 1), :, :].rearrange("p o g (a j) -> p (o g a) j", a=2).unsqueeze(3)
                                .broadcast_to([P, 4, 4, NB]), ALU.add).then_inc(pred, 1)
                v.wait_ge(silued, e + 1)
                v.tensor_tensor(ug[:, q, :, :], gate[:, 0, :, :], gate[:, 1, :, :], ALU.mult).then_inc(ug_ready, 1)
                if not first:
                    add_down(e - 1)

            expert(0, 0, first=True)
            with v.Fori(0, 5) as h:
                for k in range(1, 4):
                    expert(h, k)
            keep_down(NE - 1)
            add_down(NE - 1)

            v.wait_ge(pe_part, CP + 2)
            for m in range(2):
                own(v.tensor_scalar(cKT[:, m, :, :], bank[0][:, m * 32:(m + 1) * 32].rearrange("p (b e) -> p b e", b=NB),
                                    bcol[:, CBK, m:m + 1], None, ALU.add), wait=False)
                own(v.tensor_scalar(cVT[:, m, :, :], bank[0][:, 64 + m * 32:64 + (m + 1) * 32].rearrange("p (b e) -> p b e", b=NB),
                                    bcol[:, CBV, m:m + 1], None, ALU.add))
            for m in range(2):
                for b in range(NB):
                    own(spread(cbK[:, m, b, :, :], cKT[:, m, b, :], masks), wait=False)
                    last = spread(cbV[:, m, b, :, :], cVT[:, m, b, :], mask)
                    if m == 0 or b == 0:
                        own(last, wait=False)
            last.then_inc(dve_part, 1)
            v.wait_ge(pe_part, CP + 3)
            for b in range(NB):
                own(v.tensor_copy(Wc[:, b, :, :].rearrange("p c n -> p (c n)"), bank[1 + b][:, :]), wait=False)
                own(v.tensor_copy(Vc[:, b, :, :].rearrange("p m n -> p (m n)"), bank[3 + b][:, :]), wait=False)
            split3(cb3[:, :], bank[5][0:3, :]).then_inc(dve_part, 1)

            def soften(j, q):
                for u in range(2):
                    v.wait_ge(c_ps, j * 2 + (u + 1))
                    ps = bank[u][:, :].rearrange("p (r e) -> p r e", e=NE)
                    cm = cmax[:, u * 32:(u + 1) * 32]
                    v.tensor_reduce(cm, ps, AX_X, ALU.max).then_inc(c_max, 1)
                    v.wait_ge(c_max, j * 2 + (u + 1))
                    v.tensor_tensor(prob[:, q, 2 * u:2 * u + 2, :].rearrange("p t (h e) -> p (t h) e", e=NE), ps,
                                    cm.unsqueeze(2).broadcast_to([P, 32, NE]), ALU.subtract).then_inc(c_sub, 1)

            def total(j, q, first=False):
                v.wait_ge(c_exp, j + 1)
                v.tensor_reduce(csum, prob[:, q, :, :].rearrange("p t (h e) -> p (t h) e", e=NE), AX_X, ALU.add)\
                    .then_inc(c_sum, 1)
                v.wait_ge(c_sum, j + 1)
                if not first:
                    v.wait_ge(c_prob, j)
                v.reciprocal(crs, csum).then_inc(c_rs, 1)

            def norm_out(j, q):
                for t in range(TG):
                    hold(co_sb, j * 2 + (t // 2 + 1))
                    v.bn_stats(stats[:, 0, t, :], co[:, q, t, :]).then_inc(c_stat, 1)
                hold(c_stat, j * TG + TG)
                for t in range(TG):
                    v.bn_aggr(mv[:, 0, t, :], stats[:, 0, t, :]).then_inc(c_mean, 1)

            def apply_out(j, q):
                v.wait_ge(c_rst, j + 1)
                for t in range(TG):
                    v.tensor_scalar(co[:, q, t, :], co[:, q, t, :], mv[:, 0, t, 0:1], rstd[:, 0, t:t + 1],
                                    ALU.subtract, ALU.mult).then_inc(c_norm, 1)

            def combine(j, q, second=False):
                soften(j, q)
                if not second:
                    apply_out(j - 2, q)
                total(j, q)
                norm_out(j - 1, 1 - q)

            v.wait_ge(c_in, 2)
            soften(0, 0)
            total(0, 0, first=True)
            combine(1, 1, second=True)
            with v.Fori(1, NG // 2) as h:
                combine(h * 2, 0)
                combine(h * 2 + 1, 1)
            apply_out(NG - 2, 0)
            norm_out(NG - 1, 1)
            apply_out(NG - 1, 1)


_INS = ['L0_attn_query', 'L0_attn_key_param', 'L0_attn_Wq', 'L0_attn_bq', 'L0_attn_Wk', 'L0_attn_bk', 'L0_attn_Wv',
        'L0_attn_bv', 'L0_attn_Wo', 'L0_attn_bo', 'L0_ffn_slot_query', 'L0_ffn_d_Wq', 'L0_ffn_d_Wk', 'L0_ffn_d_Wv',
        'L0_ffn_d_Wo', 'L0_ffn_d_bq', 'L0_ffn_d_bk', 'L0_ffn_d_bv', 'L0_ffn_d_bo', 'L0_ffn_c_Wq', 'L0_ffn_c_Wk',
        'L0_ffn_c_Wv', 'L0_ffn_c_Wo', 'L0_ffn_c_bq', 'L0_ffn_c_bk', 'L0_ffn_c_bv', 'L0_ffn_c_bo', 'L0_ffn_e_ln_g',
        'L0_ffn_e_ln_b', 'L0_ffn_e_W1', 'L0_ffn_e_b1', 'L0_ffn_e_Wg', 'L0_ffn_e_bg', 'L0_ffn_e_W2', 'L0_ffn_e_b2']
_OUTS = [((2, 2048, 256), 'float32')]


def kernel(**inputs):
    import numpy as _np
    import concourse.bacc as _bacc
    from concourse import mybir as _mybir
    from concourse.bass_utils import run_bass_kernel_spmd as _run

    nc = _bacc.Bacc("TRN2", target_bir_lowering=False, num_devices=1)
    arrays, args = {}, {}
    for name in _INS:
        a = _np.ascontiguousarray(inputs[name])
        arrays[f"in_{name}_dram"] = a
        args[name] = nc.dram_tensor(f"in_{name}_dram", a.shape, _mybir.dt.from_np(a.dtype), kind="ExternalInput").ap()
    shape, dtype = _OUTS[0]
    out = nc.dram_tensor("out_0_dram", shape, _mybir.dt.from_np(_np.dtype(dtype)), kind="ExternalOutput").ap()
    build(nc, args, out)
    r = _run(nc, [arrays], core_ids=[0])
    return r.results[0]["out_0_dram"]
```

```python
from contextlib import ExitStack

import concourse.bass as bass
from concourse import mybir

ALU = mybir.AluOpType
ACT = mybir.ActivationFunctionType
F32 = mybir.dt.float32
BF16 = mybir.dt.bfloat16
I32 = mybir.dt.int32
AX_X = mybir.AxisListType.X

P = 128
D = 256
C = D // P
NB, L = 2, 2048
NH, DH = 16, 16
NS = 32
NE, FF = 16, 1024
J = FF // P
TG = 4
GT = TG * P
NG = NB * L // GT
GB = L // GT
KT = L // P
HR = TG * NH
TOP = 8
EPS = 1e-5
FIXES = NS - TOP
EB = 3
SCALE = DH ** -0.5


def build(nc, A, out):
    with ExitStack() as ctx:
        def sb(name, shape, dt=F32):
            return ctx.enter_context(nc.sbuf_tensor(name, shape, dt))

        def sem(name):
            return ctx.enter_context(nc.semaphore(name))

        bank = [ctx.enter_context(nc.psum_tensor(f"bank{i}", [P, 512], F32)) for i in range(8)]

        x = sb("x", [P, NB * KT, D])
        arena = sb("arena", [P, 14336])
        ynT = arena[:, 0:8192].rearrange("p (b c l) -> p b c l", b=NB, c=C)
        ring0 = arena[:, 8192:14336].rearrange("p (k n) -> p k n", k=3)
        work = sb("work", [P, 8192])
        s_all = work[:, 0:4096].rearrange("p (m k) -> p m k", m=2)
        yn = work[:, 4096:8192].rearrange("p (t d) -> p t d", d=D)
        scr1 = sb("scr1", [P, KT * 512])
        ring = (ring0, scr1[:, 0:6144].rearrange("p (k n) -> p k n", k=3), work[:, 0:6144].rearrange("p (k n) -> p k n", k=3))
        scr = tuple(a.rearrange("p (h j s) -> p h j s", h=NH, j=KT) for a in (arena[:, 4096:12288], scr1[:, :]))

        aWq, aWk, aWv, dWq, dWk = (
            work[:, 512 * i:512 * i + 512].rearrange("p (c d) -> p c d", c=C) for i in range(5))
        kp = work[0:NS, 2560:2816]
        b2 = work[0:NE, 2816:3072]
        aWo = sb("aWo", [P, C, D])
        sq = sb("sq", [NE, D])
        cWq, cWk, cWv, cWo = (scr1[:, 6144 + 512 * i:6656 + 512 * i].rearrange("p (c d) -> p c d", c=C) for i in range(4))

        def fold(at, n, parts=P):
            return work[0:parts, 4096 + at:4096 + at + n]

        aWqT = fold(0, 512).rearrange("p (m c q) -> p m c q", m=2, c=C)
        dWkT = fold(512, 512).rearrange("p (m c q) -> p m c q", m=2, c=C)
        bdK = fold(1024, 512).rearrange("p (m h s) -> p m h s", m=2, h=8)
        bdQ = fold(2048, 256).rearrange("p (m h s) -> p m h s", m=2, h=8)
        aKT = fold(2304, 64).rearrange("p (m s) -> p m s", m=2)
        aKT4 = fold(3488, 256).rearrange("p (m s) -> p m s", m=2)
        dQT = fold(2432, 32).rearrange("p (m s) -> p m s", m=2)
        brow = fold(2464, P, 18)
        bo3 = fold(2592, 512, 3).rearrange("p (a d) -> p a d", a=2)
        bvrow = fold(3104, D, 1)
        ones1 = fold(3360, P, 1)

        ident = sb("ident", [P, P])
        mask = sb("mask", [P, 8])
        masks = sb("masks", [P, 8])
        sel = sb("sel", [P, NE])
        ones3 = sb("ones3", [3, P], BF16)
        mhalf = sb("mhalf", [P, TG])
        tiny = sb("tiny", [P, 1])
        rk = sb("rk", [P, TOP])
        miscT = sb("miscT", [P, 146])
        kpT = miscT[:, 0:64].rearrange("p (c s) -> p c s", c=C)
        sqT = miscT[:, 64:96].rearrange("p (c s) -> p c s", c=C)
        b2T = miscT[:, 96:128].rearrange("p (c s) -> p c s", c=C)
        bcol = miscT[:, 128:146].rearrange("p (v m) -> p v m", m=2)
        ABQ, ABK, ABV, DBQ, DBK, DBV, CBQ, CBK, CBV = range(9)
        bq3 = sb("bq3", [P, 2, 2, 3])
        Wz = sb("Wz", [P, C, 512])
        Wd = sb("Wd", [P, C, D])
        vrep = sb("vrep", [P, NH, DH])
        jmask = sb("jmask", [P, 2, 8])
        dconst = sb("dconst", [P, 2])
        zb3 = sb("zb3", [3, 512], BF16)
        ab3 = sb("ab3", [3, 512], BF16)
        cb3 = sb("cb3", [3, 512], BF16)

        stats = sb("stats", [P, 3, TG, 6])
        mv = sb("mv", [P, 3, TG, 2])
        veps = sb("veps", [P, 3, TG])
        rstd = sb("rstd", [P, 3, TG])
        shift = sb("shift", [P, 3, TG])
        xin = sb("xin", [P, TG, D])
        y = sb("y", [P, TG, D])
        yT = sb("yT", [P, C, GT])
        d = sb("d", [P, TG * 512])
        above = sb("above", [P, TG * 512], BF16)
        top = sb("top", [P, HR, TOP])
        tau = sb("tau", [P, HR])
        cnt = sb("cnt", [P, HR])
        exc = sb("exc", [P, HR])
        rcnt = sb("rcnt", [P, HR])
        tauf = sb("tauf", [P, HR])
        tot = sb("tot", [P, 2, GB])
        ahead = sb("ahead", [P, NG])
        moved = sb("moved", [P, 32])
        movedT = sb("movedT", [P, 32])
        flag = sb("flag", [P, 1])
        flagi = sb("flagi", [P, 1], I32)

        bdh = sb("bdh", [P, TG, 2, P])
        aT = sb("aT", [P, 2, 512])
        hoT = sb("hoT", [P, 2, 2, P])
        o = arena[:, 12288:14336].rearrange("p (q t d) -> p q t d", q=2, t=TG)

        pmax = sb("pmax", [P, 2, GB])
        smax = sb("smax", [P, 2])
        nmax = sb("nmax", [P, 2])
        ssum = sb("ssum", [P, 2])
        rsum = sb("rsum", [P, 2])
        pT = aT
        dWv = d[:, 0:512].rearrange("p (c n) -> p c n", c=C)
        dWo = d[:, 512:1024].rearrange("p (c n) -> p c n", c=C)
        zm = y[:, 2, :].rearrange("p (m n) -> p m n", m=2)
        gT = yT[:, 0, :].rearrange("p (c m n) -> p c m n", c=C, m=2)
        slot = yT[0:NE, 1, 0:256]
        hid = yT[0:NE, 1, 256:512]
        lng = xin[0:NE, 0, :]
        lnb = xin[0:NE, 1, :]
        dbo = xin[0:NE, 2, :]
        b1 = xin[:, 3, 0:P]
        bg = xin[:, 3, P:2 * P]
        bT1 = y[:, 3, :].rearrange("p (e g j) -> p e g j", g=2, j=J)
        hT = sb("hT", [P, 2, NE])
        sstats = sb("sstats", [NE, 6])
        smv = sb("smv", [NE, 2])
        sveps = sb("sveps", [NE, 1])
        srstd = sb("srstd", [NE, 1])
        slotT = sb("slotT", [P, C, NB, NE])
        hidT = sb("hidT", [P, C, NB, NE])

        def over(at, n):
            return d[:, at:at + n]

        pre = over(0, 32).rearrange("p (g j b) -> p g j b", g=2, b=NB)
        gate = over(32, 32).rearrange("p (g j b) -> p g j b", g=2, b=NB)
        ug = over(352, 48).rearrange("p (q j b) -> p q j b", q=EB, b=NB)
        hcol = over(160, 192).rearrange("p (q c x) -> p q c x", q=EB, c=C)
        spare = above[:, :].bitcast(F32)
        ugT = (over(1024, 512), over(1536, 512), spare[:, 0:512])
        dn = spare[0:NB, 512:768]
        newT = over(96, 64).rearrange("p (c b e) -> p c b e", c=C, b=NB)
        cKT = over(160, 64).rearrange("p (m b e) -> p m b e", m=2, b=NB)
        cVT = over(224, 64).rearrange("p (m b e) -> p m b e", m=2, b=NB)
        cWqT = over(512, 512).rearrange("p (m c n) -> p m c n", m=2, c=C)
        cbK = over(1024, 512).rearrange("p (m b h e) -> p m b h e", m=2, b=NB, h=8)
        cbV = over(1536, 512).rearrange("p (m b h e) -> p m b h e", m=2, b=NB, h=8)
        Wc = scr1[:, 0:1024].rearrange("p (b c n) -> p b c n", b=NB, c=C)
        Vc = scr1[:, 1024:2048].rearrange("p (b m n) -> p b m n", b=NB, m=2)
        prob = work[:, 2048:4096].rearrange("p (g t n) -> p g t n", g=2, t=TG)
        cpT = work[:, 4096:5120].rearrange("p (g n) -> p g n", g=2)
        co = work[:, 5120:7168].rearrange("p (g t n) -> p g t n", g=2, t=TG)
        cmax = work[:, 7168:7232]
        csum = work[:, 7232:7296]
        crs = work[:, 7296:7360]

        xs = A['L0_attn_query'].rearrange("b (p j) d -> p b j d", p=P)
        xt = A['L0_attn_query'].rearrange("b (t p) d -> p (b t) d", p=P)
        ot = out.rearrange("b (t p) d -> p (b t) d", p=P)
        w_in = sem("w_in")
        w_in1 = sem("w_in1")
        bo_in = sem("bo_in")
        w_in2 = sem("w_in2")
        w_in3 = sem("w_in3")
        xin_in = sem("xin_in")
        x_in = sem("x_in")
        bd_ready = sem("bd_ready")
        h_ps = sem("h_ps")
        h_sb = sem("h_sb")
        consts = sem("consts")
        pe_part = sem("pe_part")
        dve_part = sem("dve_part")
        prep = sem("prep")
        stat = [sem(f"stat{k}") for k in range(3)]
        mean = [sem(f"mean{k}") for k in range(3)]
        vare = [sem(f"vare{k}") for k in range(3)]
        root = [sem(f"root{k}") for k in range(3)]
        rst = [sem(f"rst{k}") for k in range(3)]
        y_ready = sem("y_ready")
        yT_ps = sem("yT_ps")
        yT_sb = sem("yT_sb")
        z_ps = sem("z_ps")
        z_sb = sem("z_sb")
        topped = sem("topped")
        cum = sem("cum")
        diff = sem("diff")
        relued = sem("relued")
        newton = sem("newton")
        checked = sem("checked")
        fix = sem("fix")
        tau_ready = sem("tau_ready")
        lowered = sem("lowered")
        signed = sem("signed")
        settled = sem("settled")
        a_ps = sem("a_ps")
        a_sb = sem("a_sb")
        o_ps = sem("o_ps")
        o_sb = sem("o_sb")
        o_norm = sem("o_norm")
        x_new = sem("x_new")
        yn_ready = sem("yn_ready")
        ynT_ps = sem("ynT_ps")
        ynT_sb = sem("ynT_sb")
        s_ps = sem("s_ps")
        s_sb = sem("s_sb")
        maxed = sem("maxed")
        exped = sem("exped")
        pT_ps = sem("pT_ps")
        pT_sb = sem("pT_sb")
        g_ps = sem("g_ps")
        slots = sem("slots")
        smean = sem("smean")
        srst = sem("srst")
        e_in = [[sem(f"e_in{q}{k}") for k in range(3)] for q in range(EB)]
        up_ps = sem("up_ps")
        hbias = sem("hbias")
        ug_sb = sem("ug_sb")
        ugT_ps = sem("ugT_ps")
        pred = sem("pred")
        silued = sem("silued")
        hcol_ready = sem("hcol_ready")
        ug_ready = sem("ug_ready")
        down_ps = sem("down_ps")
        dn_sb = sem("dn_sb")
        dnT_ps = sem("dnT_ps")
        down_sb = sem("down_sb")
        laid = sem("laid")
        c_ps = sem("c_ps")
        c_max = sem("c_max")
        c_sub = sem("c_sub")
        c_exp = sem("c_exp")
        c_sum = sem("c_sum")
        c_rs = sem("c_rs")
        c_prob = sem("c_prob")
        c_pT_ps = sem("c_pT_ps")
        c_pT_sb = sem("c_pT_sb")
        co_ps = sem("co_ps")
        co_sb = sem("co_sb")
        c_stat = sem("c_stat")
        c_mean = sem("c_mean")
        c_vare = sem("c_vare")
        c_root = sem("c_root")
        c_rst = sem("c_rst")
        c_norm = sem("c_norm")
        c_out = sem("c_out")
        stored = [sem(f"stored{q}") for q in range(2)]

        bT = bank[0:2]; bZ = bank[2:4]; bA = bank[4:6]
        psH = bank[6][:, 0:D]
        psO = bank[7][:, 0:D]
        N_W2, N_W3 = 7, 4
        (M_MISC, M_AQ, M_KQ, M_WZ, M_ZB, M_DK, M_DQ, M_V, M_WD) = range(1, 10)
        PREP = M_WD
        (D_Z, D_H, D_SLOT, D_T) = range(1, 5)
        ND = D_T
        (S_GT, S_ZM, S_H, S_SLOT, S_T) = range(1, 6)
        MS = S_T
        NMX = 2 * GB + 2
        CP = PREP + 2 * ND
        CS = PREP + 2 * MS

        def biases(names):
            return [(brow[2 * v:2 * v + 2, :], A[name].rearrange("(m p) -> m p", p=P), w_in) for v, name in names]

        def weight(w, name, form, s):
            return w, A[name].rearrange(form, c=C), s

        rows_of = list(enumerate(('L0_attn_bq', 'L0_attn_bk', 'L0_attn_bv', 'L0_ffn_d_bq', 'L0_ffn_d_bk',
                                  'L0_ffn_d_bv', 'L0_ffn_c_bq', 'L0_ffn_c_bk', 'L0_ffn_c_bv')))
        first_by_sync = [weight(aWk, 'L0_attn_Wk', "(p c) n -> p c n", w_in), weight(aWq, 'L0_attn_Wq', "(p c) n -> p c n", w_in),
                         (kp, A['L0_attn_key_param'][0], w_in)] + biases(rows_of[:6])
        first_by_scalar = [(sq[:, :], A['L0_ffn_slot_query'][0], w_in), (b2, A['L0_ffn_e_b2'], w_in)] + biases(rows_of[6:]) + [
            (bo3[:, a, :], A[name].rearrange("(o d) -> o d", o=1).broadcast_to([3, D]), bo_in)
            for a, name in ((0, 'L0_attn_bo'), (1, 'L0_ffn_c_bo'))] + [
            weight(dWk, 'L0_ffn_d_Wk', "(p c) n -> p c n", w_in1), weight(dWq, 'L0_ffn_d_Wq', "(p c) n -> p c n", w_in1),
            (bvrow, A['L0_attn_bv'].rearrange("(o d) -> o d", o=1), w_in1),
            weight(aWv, 'L0_attn_Wv', "(c p) n -> p c n", w_in1), weight(aWo[:, :, :], 'L0_attn_Wo', "(c p) n -> p c n", w_in1)]
        N_W0, N_W1 = (sum(s is which for _, _, s in first_by_sync + first_by_scalar) for which in (w_in, w_in1))

        block = ctx.enter_context(nc.Block())

        @block.sync
        def _(sp):
            def load(i, b):
                sp.dma_start(xin[:, :, :], xs[:, b, bass.ds(i * TG - b * KT, TG), :]).then_inc(xin_in, 16)

            load(0, 0)
            for dst, src, s in first_by_sync:
                sp.dma_start(dst, src).then_inc(s, 16)

            def next_load(i, b):
                sp.wait_ge(y_ready, i * TG)
                load(i, b)

            next_load(1, 0)
            next_load(2, 0)
            sp.dma_start(x[:, :, :], xt).then_inc(x_in, 16)
            next_load(3, 0)
            with sp.Fori(GB, NG) as i:
                next_load(i, 1)

            sp.wait_ge(settled, NB)
            for dst, src in ((lng, A['L0_ffn_e_ln_g']), (lnb, A['L0_ffn_e_ln_b']),
                             (dbo, A['L0_ffn_d_bo'].rearrange("(o d) -> o d", o=1).broadcast_to([NE, D])),
                             (dWv, A['L0_ffn_d_Wv'].rearrange("(p c) n -> p c n", c=C)),
                             (dWo, A['L0_ffn_d_Wo'].rearrange("(c p) n -> p c n", c=C)),
                             (b1, A['L0_ffn_e_b1'].rearrange("e (j p) -> (e j) p", p=P)),
                             (bg, A['L0_ffn_e_bg'].rearrange("e (j p) -> (e j) p", p=P))):
                sp.dma_start(dst, src).then_inc(w_in2, 16)

            def expert(e, q, k):
                dst = ring[q][:, k, :]
                if k == 2:
                    dst = dst.rearrange("p (j d) -> p j d", j=J)
                if k < 2:
                    src = A[('L0_ffn_e_W1', 'L0_ffn_e_Wg')[k]].rearrange("e (p c) f -> p e (c f)", c=C)[:, e, :]
                else:
                    src = A['L0_ffn_e_W2'].rearrange("e (j p) d -> p e j d", j=J)[:, e, :, :]
                sp.dma_start(dst, src).then_inc(e_in[q][k], 16)

            sp.wait_ge(a_ps, KT)
            for k in range(2):
                expert(0, 0, k)
            sp.wait_ge(a_ps, 2 * KT)
            for w, name, form in ((cWq, 'L0_ffn_c_Wq', "(p c) n -> p c n"), (cWk, 'L0_ffn_c_Wk', "(p c) n -> p c n"),
                                  (cWv, 'L0_ffn_c_Wv', "(p c) n -> p c n"), (cWo, 'L0_ffn_c_Wo', "(c p) n -> p c n")):
                sp.dma_start(w, A[name].rearrange(form, c=C)).then_inc(w_in3, 16)
            for k in range(3):
                expert(1, 1, k)
            sp.wait_ge(x_new, NG)
            expert(0, 0, 2)
            sp.wait_ge(g_ps, KT // 2 + KT // 4)
            expert(2, 2, 2)
            sp.wait_ge(g_ps, 2 * (KT // 2))
            for k in range(2):
                expert(2, 2, k)

            def refill(it, q):
                for k in range(3):
                    if k < 2:
                        sp.wait_ge(up_ps, it * 6 + (2 * (q - 3) + k + 1))
                    else:
                        sp.wait_ge(down_ps, it * 3 + (q - 2))
                    expert(it * 3 + q, q, k)

            with sp.Fori(1, NE // EB) as it:
                for q in range(EB):
                    refill(it, q)
            for q in range(NE % EB):
                refill(NE // EB, q)

            def store(j, q):
                sp.wait_ge(c_out, j + 1)
                sp.dma_start(ot[:, bass.ds(j * TG, TG), :], co[:, q, :, :]).then_inc(stored[q], 16)

            with sp.Fori(0, NG // 2) as h:
                store(h * 2, 0)
                store(h * 2 + 1, 1)
            sp.wait_ge(stored[0], 16 * NG // 2)
            sp.wait_ge(stored[1], 16 * NG // 2)

        @block.gpsimd
        def _(pool):
            pool.memset(ident[:, :], 0.0).then_inc(consts, 1)
            pool.memset(mask[:, :], 1.0).then_inc(consts, 1)
            pool.memset(ones3[:, :], 1.0).then_inc(consts, 1)
            pool.memset(mhalf[:, :], -0.5).then_inc(consts, 1)
            pool.memset(tiny[:, :], -1e-30).then_inc(consts, 1)
            pool.memset(moved[:, :], 0.0).then_inc(consts, 1)
            for k in range(TOP):
                pool.memset(rk[:, k:k + 1], 1.0 / (k + 1)).then_inc(consts, 1)
            pool.memset(jmask[:, :, :], 1.0).then_inc(consts, 1)
            pool.memset(ones1, 1.0).then_inc(consts, 1)
            n = 8 + TOP
            pool.wait_ge(consts, n)
            pool.affine_select(out=ident[:, :], in_=ident[:, :], compare_op=ALU.not_equal, fill=1.0, base=0,
                               pattern=[[-1, P]], channel_multiplier=1).then_inc(consts, 1)
            pool.affine_select(out=mask[:, :], in_=mask[:, :], compare_op=ALU.is_ge, fill=0.0, base=0,
                               pattern=[[-DH, 8]], channel_multiplier=1).then_inc(consts, 1)
            pool.wait_ge(consts, n + 2)
            pool.affine_select(out=mask[:, :], in_=mask[:, :], compare_op=ALU.is_ge, fill=0.0, base=DH - 1,
                               pattern=[[DH, 8]], channel_multiplier=-1).then_inc(consts, 1)
            pool.wait_ge(consts, n + 3)
            pool.tensor_scalar(masks[:, :], mask[:, :], SCALE, None, ALU.mult).then_inc(consts, 1)
            pool.affine_select(out=jmask[:, :, :], in_=jmask[:, :, :], compare_op=ALU.is_ge, fill=0.0, base=0,
                               pattern=[[P, 2], [-NS, 8]], channel_multiplier=1).then_inc(consts, 1)
            pool.wait_ge(consts, n + 5)
            pool.affine_select(out=jmask[:, :, :], in_=jmask[:, :, :], compare_op=ALU.is_ge, fill=0.0, base=NS - 1,
                               pattern=[[-P, 2], [NS, 8]], channel_multiplier=-1).then_inc(consts, 1)

            def hold(s, value):
                pool.wait_ge(s, value)
                pool.nop(nofuse=True)

            def roots(k, i):
                if k == 2 and not (isinstance(i, int) and i == 0):
                    hold(yn_ready, i * TG)
                hold(mean[k], i * TG + TG)
                pool.tensor_scalar(veps[:, k, :], mv[:, k, :, 1], EPS, None, ALU.add).then_inc(vare[k], 1)
                pool.tensor_scalar(shift[:, k, :], mv[:, k, :, 0], -1.0, None, ALU.mult).then_inc(vare[k], 1)
                pool.wait_ge(vare[k], i * 2 + 2)
                pool.tensor_tensor(rstd[:, k, :], veps[:, k, :], mhalf[:, :], ALU.pow).then_inc(root[k], 1)
                pool.wait_ge(root[k], i + 1)
                pool.tensor_tensor(shift[:, k, :], shift[:, k, :], rstd[:, k, :], ALU.mult).then_inc(rst[k], 1)

            def values(g):
                b = g // GB
                for t in range(TG):
                    if g > 0:
                        pool.wait_ge(h_ps, g * TG + (t + 1 - TG))
                    pool.tensor_tensor(bdh[:, t, :, :].rearrange("p a (j e) -> p (a j) e", e=DH),
                                       vrep[:, g * TG + t - b * NH, :].unsqueeze(1).broadcast_to([P, 16, DH]),
                                       jmask[:, :, :].rearrange("p a j -> p (a j)").unsqueeze(2).broadcast_to([P, 16, DH]),
                                       ALU.mult).then_inc(bd_ready, 1)

            def lower(i, b):
                pool.wait_ge(tau_ready, i + 1)
                z3 = scr[b][:, :, bass.ds(i * TG - b * KT, TG), :]
                pool.tensor_tensor(z3, z3, tauf[:, :].rearrange("p (h t) -> p h t", h=NH).unsqueeze(3)
                                   .broadcast_to([P, NH, TG, NS]), ALU.subtract).then_inc(lowered, 1)

            def slot_root(b):
                pool.wait_ge(smean, 2 * b + 2)
                pool.tensor_scalar(sveps[:, :], smv[:, 1:2], EPS, None, ALU.add).then_inc(srst, 1)
                pool.wait_ge(srst, 2 * b + 1)
                pool.tensor_tensor(srstd[:, :], sveps[:, :], mhalf[0:NE, 0:1], ALU.pow).then_inc(srst, 1)

            roots(0, 0)
            roots(0, 1)
            with pool.Fori(0, GB - 1) as i:
                roots(0, i + 2)
                lower(i, 0)
            roots(0, GB + 1)
            pool.wait_ge(dve_part, PREP)
            for i in range(GB, NG):
                g = i - GB
                values(g)
                if g > 0:
                    roots(1, g - 1)
                if i + 2 < NG:
                    roots(0, i + 2)
                if g > 0:
                    roots(2, g - 1)
                if i < NG - 1:
                    lower(i, 1)
            for g in range(GB, NG + 1):
                if g < NG:
                    values(g)
                roots(1, g - 1)
                roots(2, g - 1)
            slot_root(0)
            slot_root(1)

            def lay_by(it, q, first=False):
                if not first:
                    pool.wait_ge(up_ps, it * 6 + 2 * (q - 2))
                pool.tensor_copy(hcol[:, q, :, 0:NB], hidT[:, :, :, bass.ds(it * 3 + q, 1)].rearrange("p c b o -> p c (b o)"))\
                    .then_inc(hcol_ready, 1)

            pool.wait_ge(dve_part, PREP + 2 * MS)
            pool.memset(hcol, 0.0).then_inc(consts, 1)
            pool.wait_ge(consts, 15 + TOP)
            for q in range(EB):
                lay_by(0, q, first=True)
            with pool.Fori(1, NE // EB) as it:
                for q in range(EB):
                    lay_by(it, q)
            for q in range(NE % EB):
                lay_by(NE // EB, q)

            def weigh(j, q):
                for u in range(2):
                    pool.wait_ge(c_rs, j * 2 + (u + 1))
                    pv = prob[:, q, 2 * u:2 * u + 2, :].rearrange("p t (h e) -> p (t h) e", e=NE)
                    pool.tensor_tensor(pv, pv, crs[:, u * 32:(u + 1) * 32].unsqueeze(2).broadcast_to([P, 32, NE]), ALU.mult)\
                        .then_inc(c_prob, 1)

            def out_roots(j):
                hold(c_mean, j * TG + TG)
                pool.tensor_scalar(veps[:, 0, :], mv[:, 0, :, 1], EPS, None, ALU.add).then_inc(c_vare, 1)
                pool.tensor_scalar(shift[:, 0, :], mv[:, 0, :, 0], -1.0, None, ALU.mult).then_inc(c_vare, 1)
                pool.wait_ge(c_vare, j * 2 + 2)
                pool.tensor_tensor(rstd[:, 0, :], veps[:, 0, :], mhalf[:, :], ALU.pow).then_inc(c_root, 1)
                pool.wait_ge(c_root, j + 1)
                pool.tensor_tensor(shift[:, 0, :], shift[:, 0, :], rstd[:, 0, :], ALU.mult).then_inc(c_rst, 1)

            def combine(j, q):
                weigh(j, q)
                pool.wait_ge(c_norm, (j - 1) * TG)
                out_roots(j - 1)

            weigh(0, 0)
            weigh(1, 1)
            out_roots(0)
            with pool.Fori(1, NG // 2) as h:
                combine(h * 2, 0)
                combine(h * 2 + 1, 1)
            pool.wait_ge(c_norm, (NG - 1) * TG)
            out_roots(NG - 1)

        @block.scalar
        def _(act):
            for dst, src, s in first_by_scalar[:-5]:
                act.dma_start(dst, src).then_inc(s, 16)

            def scaled(k, t, dst, src):
                return act.activation(dst, src, ACT.Identity, bias=shift[:, k, t:t + 1], scale=rstd[:, k, t:t + 1])

            def norm_y(i, guard=True):
                act.wait_ge(rst[0], i + 1)
                if guard:
                    act.wait_ge(yT_ps, i)
                for t in range(TG):
                    scaled(0, t, y[:, t, :], xin[:, t, :]).then_inc(y_ready, 1)

            def put_yT(i, guard=True):
                act.wait_ge(yT_ps, i + 1)
                if guard:
                    act.wait_ge(z_ps, i * TG)
                for c in range(C):
                    act.activation(yT[:, c, :], bT[c][:, :], ACT.Copy).then_inc(yT_sb, 1)

            def put_scores(i, b, tiles):
                for t in tiles:
                    act.wait_ge(z_ps, i * TG + (t + 1))
                    act.activation(scr[b][:, :, bass.ds(i * TG + (t - b * KT), 1), :].rearrange("p h o s -> p (h o) s"),
                                   bZ[t % 2][:, :].rearrange("p (h s) -> p h s", h=NH), ACT.Copy).then_inc(z_sb, 1)

            def clamp(i):
                act.wait_ge(diff, i + 1)
                act.activation(d[:, :], d[:, :], ACT.Relu).then_inc(relued, 1)

            def signs(i, b):
                act.wait_ge(lowered, i + 1)
                act.activation(above[:, :].rearrange("p (h t s) -> p h t s", h=NH, t=TG),
                               scr[b][:, :, bass.ds(i * TG - b * KT, TG), :], ACT.Sign, bias=tiny[:, 0:1],
                               accum_out=ahead[:, bass.ds(i, 1)]).then_inc(signed, 1)

            def put_heads(g, steps=range(TG + 2)):
                for t in steps:
                    n = g * TG + t
                    if t < TG:
                        act.wait_ge(a_ps, n + 1)
                        if n >= 2:
                            act.wait_ge(h_ps, n - 1)
                        act.activation(aT[:, t % 2, :], bA[t % 2][:, :], ACT.Relu).then_inc(a_sb, 1)
                    if 1 <= t < TG + 1:
                        act.wait_ge(h_ps, n)
                        if n >= 3:
                            act.wait_ge(o_ps, n - 2)
                        act.activation(hoT[:, n % 2, :, :].rearrange("p m n -> p (m n)"), psH, ACT.Copy).then_inc(h_sb, 1)
                    if t >= 2:
                        act.wait_ge(o_ps, n - 1)
                        if t == 2 and g >= 2:
                            act.wait_ge(x_new, g - 1)
                        act.activation(o[:, g % 2, t - 2, :], psO, ACT.Copy).then_inc(o_sb, 1)

            def norm_o(g):
                act.wait_ge(rst[1], g + 1)
                for t in range(TG):
                    scaled(1, t, o[:, g % 2, t, :], o[:, g % 2, t, :]).then_inc(o_norm, 1)

            def second_norm(g):
                act.wait_ge(rst[2], g + 1)
                if g == GB:
                    act.wait_ge(g_ps, KT // 2)
                for t in range(TG):
                    scaled(2, t, yn[:, (g % GB) * TG + t, :], x[:, g * TG + t, :]).then_inc(yn_ready, 1)

            def put_norm(g):
                b, at = g // GB, (g % GB) * GT
                act.wait_ge(ynT_ps, g + 1)
                for c in range(C):
                    act.activation(ynT[:, b, c, at:at + GT], bT[c][:, :], ACT.Copy).then_inc(ynT_sb, 1)

            def put_slot_scores(g):
                at = (g % GB) * GT
                for m in range(2):
                    act.wait_ge(s_ps, g * 2 + (m + 1))
                    act.activation(s_all[:, m, at:at + GT], bT[m][:, :], ACT.Identity,
                                   bias=dconst[:, m:m + 1]).then_inc(s_sb, 1)

            def exponentials(b):
                for m in range(2):
                    act.wait_ge(maxed, NMX * (b + 1))
                    act.activation(s_all[:, m, :], s_all[:, m, :], ACT.Exp, bias=nmax[:, m:m + 1],
                                   accum_out=ssum[:, m:m + 1]).then_inc(exped, 1)

            def put_probabilities(b):
                for k in range(KT // 2):
                    n = b * (KT // 2) + k
                    act.wait_ge(pT_ps, n + 1)
                    if n >= 2:
                        act.wait_ge(g_ps, n - 1)
                    act.activation(pT[:, k % 2, :], bA[k % 2][:, :], ACT.Copy).then_inc(pT_sb, 1)

            norm_y(0, guard=False)
            for dst, src, s in first_by_scalar[-5:]:
                act.dma_start(dst, src).then_inc(s, 16)
            put_yT(0, guard=False)
            norm_y(1)
            put_scores(0, 0, range(TG))
            put_yT(1)
            put_scores(1, 0, range(2))
            with act.Fori(0, GB - 2) as i:
                clamp(i)
                norm_y(i + 2)
                put_scores(i + 1, 0, range(2, TG))
                put_yT(i + 2)
                put_scores(i + 2, 0, range(2))
                signs(i, 0)
            for i in range(GB - 2, NG):
                g = i - GB
                if g >= 0:
                    put_heads(g, range(1))
                clamp(i)
                if g >= 0:
                    put_heads(g, range(1, 2))
                if g > 0:
                    norm_o(g - 1)
                if g >= 0:
                    put_heads(g, range(2, 3))
                if i + 1 < NG:
                    put_scores(i + 1, (i + 1) // GB, range(2, TG))
                if i + 2 < NG:
                    norm_y(i + 2)
                if g > 0:
                    second_norm(g - 1)
                if g >= 0:
                    put_heads(g, range(3, TG + 2))
                if i + 2 < NG:
                    put_yT(i + 2)
                if i == NG - 1:
                    signs(i, 1)
                if g > 0:
                    put_norm(g - 1)
                    put_slot_scores(g - 1)
                if i + 2 < NG:
                    put_scores(i + 2, (i + 2) // GB, range(2))
                if i < NG - 1:
                    signs(i, i // GB)
            norm_o(3)
            put_heads(4, range(3))
            second_norm(3)
            put_heads(4, range(3, TG + 2))
            norm_o(4)
            put_norm(3)
            put_heads(5, range(2))
            put_slot_scores(3)
            put_heads(5, range(2, TG + 2))
            exponentials(0)
            norm_o(5)
            put_probabilities(0)
            second_norm(4)
            put_heads(6, range(2))
            put_norm(4)
            put_heads(6, range(2, 4))
            put_slot_scores(4)
            put_heads(6, range(4, TG + 2))
            second_norm(5)
            put_norm(5)
            norm_o(6)
            put_heads(7, range(2))
            put_slot_scores(5)
            put_heads(7, range(2, TG + 2))
            second_norm(6)
            norm_o(7)
            put_norm(6)
            put_slot_scores(6)
            second_norm(7)
            put_norm(7)
            put_slot_scores(7)
            exponentials(1)
            put_probabilities(1)

            with act.Fori(0, NE) as e:
                act.wait_ge(pred, e + 1)
                act.activation(gate, pre, ACT.Silu).then_inc(silued, 1)

            def exps(j, q):
                for u in range(2):
                    act.wait_ge(c_sub, j * 2 + (u + 1))
                    pair = prob[:, q, 2 * u:2 * u + 2, :]
                    act.activation(pair, pair, ACT.Exp).then_inc(c_exp, 1)

            def outs(j, q, guard=True):
                for u in range(2):
                    act.wait_ge(c_pT_ps, j * 2 + (u + 1))
                    act.activation(cpT[:, u, :], bA[u][:, :], ACT.Copy).then_inc(c_pT_sb, 1)
                for u in range(2):
                    act.wait_ge(co_ps, j * 2 + (u + 1))
                    if guard and u == 0:
                        act.wait_ge(stored[q], (j - q) * 8)
                    act.activation(co[:, q, 2 * u:2 * u + 2, :], bank[6 + u][:, :], ACT.Copy).then_inc(co_sb, 1)

            def apply_out(j, q):
                act.wait_ge(c_rst, j + 1)
                for t in range(TG):
                    scaled(0, t, co[:, q, t, :], co[:, q, t, :]).then_inc(c_norm, 1)

            def combine(j, q):
                outs(j - 1, 1 - q)
                apply_out(j - 2, q)
                exps(j + 1, 1 - q)

            for part, dst, b in ((4, Vc, 0), (5, Wc, 1), (6, Vc, 1)):
                act.wait_ge(pe_part, CP + part)
                act.activation(dst[:, b, :, :].rearrange("p a n -> p (a n)"), bank[4 + b if dst is Vc else 2][:, :],
                               ACT.Copy).then_inc(laid, 1)
            exps(0, 0)
            exps(1, 1)
            outs(0, 0, guard=False)
            exps(2, 0)
            outs(1, 1, guard=False)
            apply_out(0, 0)
            exps(3, 1)
            with act.Fori(1, NG // 2 - 1) as h:
                combine(h * 2 + 1, 1)
                combine(h * 2 + 2, 0)
            outs(NG - 2, 0)
            apply_out(NG - 3, 1)
            outs(NG - 1, 1)
            apply_out(NG - 2, 0)
            apply_out(NG - 1, 1)

        @block.tensor
        def _(pe):
            def turn_y(i):
                pe.wait_ge(y_ready, i * TG + TG)
                if i > 0:
                    pe.wait_ge(yT_sb, 2 * i)
                for t in range(TG):
                    for c in range(C):
                        mm = pe.transpose(bT[c][:, t * P:(t + 1) * P], y[:, t, c::C], ident[:, :])
                mm.then_inc(yT_ps, 1)

            def scores_of(i, tiles):
                pe.wait_ge(yT_sb, i * 2 + 2)
                for t in tiles:
                    n = i * TG + t
                    if n >= 2:
                        pe.wait_ge(topped, n - 1)
                    pe.matmul(bZ[t % 2][:, :], ones3[:, :], zb3[:, :], start=True, stop=False)
                    for c in range(C):
                        mm = pe.matmul(bZ[t % 2][:, :], yT[:, c, t * P:(t + 1) * P], Wz[:, c, :],
                                       start=False, stop=(c == C - 1))
                    mm.then_inc(z_ps, 1)

            def heads_of(g, steps=range(TG + 2)):
                b = g // GB
                pe.wait_ge(settled, b + 1)
                if g == 6:
                    pe.wait_ge(pT_sb, KT // 2)
                w = scr[b].rearrange("p h j s -> p h (j s)")
                for t in steps:
                    n = g * TG + t
                    if t < TG:
                        if n >= 2:
                            pe.wait_ge(a_sb, n - 1)
                        for k in range(4):
                            mm = pe.transpose(bA[t % 2][:, k * P:(k + 1) * P], w[:, n - b * NH, k * P:(k + 1) * P], ident[:, :])
                        mm.then_inc(a_ps, 1)
                    if 1 <= t < TG + 1:
                        pe.wait_ge(a_sb, n)
                        pe.wait_ge(bd_ready, n)
                        if n >= 2:
                            pe.wait_ge(h_sb, n - 1)
                        for m in range(2):
                            for half in range(2):
                                mm = pe.matmul(psH[:, m * P:(m + 1) * P], bdh[:, t - 1, half, :],
                                               aT[:, (t - 1) % 2, (2 * m + half) * P:(2 * m + half + 1) * P],
                                               start=(half == 0), stop=(half == 1))
                        mm.then_inc(h_ps, 1)
                    if t >= 2:
                        pe.wait_ge(h_sb, n - 1)
                        if n >= 3:
                            pe.wait_ge(o_sb, n - 2)
                        pe.matmul(psO, ones3[:, :], ab3[:, 0:D], start=True, stop=False)
                        for m in range(2):
                            mm = pe.matmul(psO, hoT[:, (n - 1) % 2, m, :], aWo[:, m, :], start=False, stop=(m == 1))
                        mm.then_inc(o_ps, 1)

            def turn_norm(g):
                gb = g % GB
                pe.wait_ge(yn_ready, (g + 1) * TG)
                if g == 0:
                    pe.wait_ge(yT_sb, 2 * NG)
                else:
                    pe.wait_ge(s_sb, 2 * g)
                for t in range(TG):
                    for c in range(C):
                        mm = pe.transpose(bT[c][:, t * P:(t + 1) * P], yn[:, gb * TG + t, c::C], ident[:, :])
                mm.then_inc(ynT_ps, 1)

            def slot_scores(g):
                b, gb = g // GB, g % GB
                pe.wait_ge(ynT_sb, 2 * (g + 1))
                for m in range(2):
                    for c in range(C):
                        mm = pe.matmul(bT[m][:, :], Wd[:, c, m * P:(m + 1) * P], ynT[:, b, c, gb * GT:(gb + 1) * GT],
                                       start=(c == 0), stop=(c == C - 1))
                    mm.then_inc(s_ps, 1)

            def sums(b):
                pe.wait_ge(s_sb, 2 * GB * (b + 1))
                pe.wait_ge(exped, 2 * b + 2)
                for k in range(KT // 2 + 1):
                    if k < KT // 2:
                        n = b * (KT // 2) + k
                        if n >= 2:
                            pe.wait_ge(pT_sb, n - 1)
                        for u in range(2):
                            for m in range(2):
                                mm = pe.transpose(bA[k % 2][:, (u * 2 + m) * P:(u * 2 + m + 1) * P],
                                                  s_all[:, m, (2 * k + u) * P:(2 * k + u + 1) * P], ident[:, :])
                        mm.then_inc(pT_ps, 1)
                    if k >= 1:
                        pe.wait_ge(pT_sb, b * (KT // 2) + k)
                        for u in range(2):
                            kt = 2 * (k - 1) + u
                            for c in range(C):
                                mm = pe.matmul(bZ[c][:, 0:2 * P], yn[:, kt, c::C],
                                               pT[:, (k - 1) % 2, u * 2 * P:(u + 1) * 2 * P],
                                               start=(kt == 0), stop=(kt == KT - 1))
                        mm.then_inc(g_ps, 1)

            def to_slots(b, step):
                pe.wait_ge(dve_part, PREP + b * MS + (S_GT, S_ZM, S_H, S_SLOT)[step])
                if step == 0:
                    for m in range(2):
                        for c in range(C):
                            mm = pe.matmul(bZ[0][:, m * P:(m + 1) * P], gT[:, c, m, :], dWv[:, c, m * P:(m + 1) * P],
                                           start=(c == 0), stop=(c == C - 1))
                elif step == 1:
                    for m in range(2):
                        mm = pe.matmul(bZ[1][:, m * NE:(m + 1) * NE], zm[:, m, :], sel[:, :], start=True, stop=True)
                elif step == 2:
                    for m in range(2):
                        mm = pe.matmul(bZ[0][0:NE, 0:D], hT[:, m, :], dWo[:, m, :], start=(m == 0), stop=(m == 1))
                else:
                    for c in range(C):
                        pe.transpose(bZ[1][:, c * NE:(c + 1) * NE], slot[:, c::C], ident[0:NE, 0:NE])
                        mm = pe.transpose(bZ[1][:, 32 + c * NE:32 + (c + 1) * NE], hid[:, c::C], ident[0:NE, 0:NE])
                mm.then_inc(pe_part, 1)

            pe.wait_ge(consts, 14 + TOP)
            pe.wait_ge(w_in, 16 * N_W0)
            for c in range(C):
                pe.transpose(bank[7][:, c * NS:(c + 1) * NS], kp[:, c::C], ident[0:NS, 0:NS])
                pe.transpose(bank[7][:, 64 + c * NE:64 + (c + 1) * NE], sq[:, c::C], ident[0:NE, 0:NE])
                pe.transpose(bank[7][:, 96 + c * NE:96 + (c + 1) * NE], b2[:, c::C], ident[0:NE, 0:NE])
            pe.transpose(bank[7][:, 128:146], brow, ident[0:18, 0:18]).then_inc(pe_part, 1)

            def turn_weight(w, bk):
                for m in range(2):
                    for c in range(C):
                        mm = pe.transpose(bank[bk][:, (m * 2 + c) * P:(m * 2 + c + 1) * P], w[:, c, m * P:(m + 1) * P],
                                          ident[:, :])
                mm.then_inc(pe_part, 1)

            turn_weight(aWq, 5)
            pe.wait_ge(dve_part, M_MISC)
            for m in range(2):
                for c in range(C):
                    mm = pe.matmul(bank[4][:, m * NS:(m + 1) * NS], aWk[:, c, m * P:(m + 1) * P], kpT[:, c, :],
                                   start=(c == 0), stop=(c == 1))
            mm.then_inc(pe_part, 1)
            turn_y(0)
            pe.wait_ge(dve_part, M_KQ)
            for c in range(C):
                for m in range(2):
                    mm = pe.matmul(bZ[c][:, m * 256:(m + 1) * 256], aWqT[:, m, c, :], bdK[:, m, :, :],
                                   start=True, stop=True)
            mm.then_inc(pe_part, 1)
            for m in range(2):
                mm = pe.matmul(bank[6][0:3, m * 256:(m + 1) * 256], bq3[:, 0, m, :], bdK[:, m, :, :], start=True, stop=True)
            mm.then_inc(pe_part, 1)
            pe.wait_ge(dve_part, M_ZB)
            scores_of(0, range(2))
            pe.wait_ge(w_in1, 16 * N_W1)
            turn_weight(dWk, 5)
            for m in range(2):
                for c in range(C):
                    mm = pe.matmul(bank[4][:, 64 + m * NE:64 + (m + 1) * NE], dWq[:, c, m * P:(m + 1) * P], sqT[:, c, :],
                                   start=(c == 0), stop=(c == 1))
            mm.then_inc(pe_part, 1)
            for m in range(2):
                pe.matmul(bank[6][:, 0:D], aKT4[:, m, :], aWv[:, m, :], start=(m == 0), stop=False)
            pe.matmul(bank[6][:, 0:D], ones1, bvrow, start=False, stop=True).then_inc(pe_part, 1)
            turn_y(1)
            scores_of(0, range(2, TG))
            pe.wait_ge(dve_part, M_DQ)
            for c in range(C):
                for m in range(2):
                    pe.matmul(bank[4][:, c * D + m * P:c * D + (m + 1) * P], dWkT[:, m, c, :], bdQ[:, m, :, :],
                              start=True, stop=True)
            for m in range(2):
                mm = pe.matmul(bank[7][:, m:m + 1], bdQ[:, m, :, :], bcol[:, DBK, m:m + 1], start=True, stop=True)
            mm.then_inc(pe_part, 1)
            scores_of(1, range(2))
            for i in range(NG):
                g = i - GB
                if g == 0:
                    pe.wait_ge(dve_part, PREP)
                if g >= 0:
                    heads_of(g, range(3))
                if i + 1 < NG:
                    scores_of(i + 1, range(2, TG))
                if g >= 0:
                    heads_of(g, range(3, TG + 2))
                if i + 2 < NG:
                    turn_y(i + 2)
                if g > 0:
                    turn_norm(g - 1)
                    slot_scores(g - 1)
                if i + 2 < NG:
                    scores_of(i + 2, range(2))
            heads_of(4)
            turn_norm(3)
            heads_of(5, range(2))
            slot_scores(3)
            heads_of(5, range(2, TG + 2))
            pe.wait_ge(w_in2, 16 * N_W2)
            sums(0)
            heads_of(6, range(2))
            turn_norm(4)
            heads_of(6, range(2, 4))
            slot_scores(4)
            heads_of(6, range(4, TG + 2))
            turn_norm(5)
            to_slots(0, 0)
            heads_of(7, range(2))
            slot_scores(5)
            heads_of(7, range(2, TG + 2))
            to_slots(0, 1)
            turn_norm(6)
            slot_scores(6)
            to_slots(0, 2)
            turn_norm(7)
            slot_scores(7)
            to_slots(0, 3)
            pe.wait_ge(dve_part, PREP + MS)
            sums(1)
            for step in range(4):
                to_slots(1, step)

            pe.wait_ge(w_in3, 16 * N_W3)
            for m in range(2):
                for c in range(C):
                    mm = pe.transpose(bank[6][:, (m * 2 + c) * P:(m * 2 + c + 1) * P], cWq[:, c, m * P:(m + 1) * P], ident[:, :])
            for g, rows_ in ((0, b1), (1, bg)):
                mm = pe.transpose(bank[7][:, g * P:(g + 1) * P], rows_, ident[:, :])
            mm.then_inc(pe_part, 1)

            pe.wait_ge(dve_part, PREP + 2 * MS)

            def grow(e, it, q, g, recent=True):
                if g == 0:
                    pe.wait_ge(hcol_ready, e + 1)
                    if recent:
                        pe.wait_ge(ug_sb, e - 2)
                pe.wait_ge(e_in[q][g], it * 16 + 16)
                for c in range(C):
                    for half in range(2):
                        k = 2 * g + half
                        mm = pe.matmul(bank[q][32 * k:32 * k + 32, :], hcol[:, q, c, :],
                                       ring[q][:, g, c * FF + half * 512:c * FF + (half + 1) * 512],
                                       start=(c == 0), stop=(c == C - 1))
                mm.then_inc(up_ps, 1)

            def turn_up(e, q):
                pe.wait_ge(ug_sb, e + 1)
                for j in range(4):
                    mm = pe.transpose(bank[3 + q][:, j * P:(j + 1) * P], ugT[q][:, j * P:(j + 1) * P], ident[:, :])
                mm.then_inc(ugT_ps, 1)

            def turn_down(e, first=False):
                pe.wait_ge(dn_sb, e + 1)
                if not first:
                    pe.wait_ge(down_sb, e)
                pe.nop(nofuse=True)
                for c in range(C):
                    mm = pe.transpose(bank[7][:, c * NB:(c + 1) * NB], dn[:, c::C], ident[0:NB, 0:NB])
                mm.then_inc(dnT_ps, 1)

            def shrink(e, it, q):
                pe.wait_ge(e_in[q][2], it * 16 + 16)
                pe.wait_ge(ug_ready, e + 1)
                for j in range(J):
                    mm = pe.matmul(bank[6][0:NB, 0:D], ug[:, q, j, :], ring[q][:, 2, j * D:(j + 1) * D],
                                   start=(j == 0), stop=(j == J - 1))
                mm.then_inc(down_ps, 1)

            def expert(h, k, first=False, last=False, recent=True):
                e, q, n = h * 3 + k, k % 3, (k + 1) % 3
                if not last:
                    grow(e + 1, h + (k + 1) // 3, n, 0, recent)
                turn_up(e, q)
                if not first:
                    turn_down(e - 1, first=recent is False and k == 1)
                if not last:
                    grow(e + 1, h + (k + 1) // 3, n, 1, recent)
                shrink(e, h + k // 3, q)

            pe.wait_ge(hbias, 1)
            grow(0, 0, 0, 0, recent=False)
            grow(0, 0, 0, 1, recent=False)
            expert(0, 0, first=True, recent=False)
            expert(0, 1, recent=False)
            with pe.Fori(0, 4) as h:
                for k in range(2, 5):
                    expert(h, k)
            expert(4, 2)
            expert(4, 3, last=True)
            turn_down(NE - 1)

            pe.wait_ge(down_sb, NE)
            for w, at in ((cWk, 0), (cWv, 64)):
                for m in range(2):
                    for c in range(C):
                        mm = pe.matmul(bank[0][:, at + m * 32:at + (m + 1) * 32], w[:, c, m * P:(m + 1) * P],
                                       newT[:, c, :, :], start=(c == 0), stop=(c == C - 1))
            mm.then_inc(pe_part, 1)

            def fold_queries(b):
                for c in range(C):
                    for m in range(2):
                        pe.matmul(bank[1 + b][:, c * D + m * P:c * D + (m + 1) * P], cWqT[:, m, c, :], cbK[:, m, b, :, :],
                                  start=True, stop=True)
                for m in range(2):
                    mm = pe.matmul(bank[(7, 3)[b]][0:3, m * P:(m + 1) * P], bq3[:, 1, m, :], cbK[:, m, b, :, :],
                                   start=True, stop=True)
                mm.then_inc(pe_part, 1)

            def fold_values(b):
                for m in range(2):
                    mm = pe.matmul(bank[4 + b][:, m * D:(m + 1) * D], cbV[:, m, b, :, :], cWo[:, m, :], start=True, stop=True)
                mm.then_inc(pe_part, 1)

            pe.wait_ge(dve_part, CS + 1)
            fold_queries(0)
            pe.wait_ge(dve_part, CS + 2)
            fold_values(0)
            pe.wait_ge(dve_part, CS + 3)
            fold_queries(1)
            fold_values(1)
            pe.wait_ge(dve_part, CS + 4)

            def scores(j):
                b = j // GB
                for t in range(TG):
                    u = t // 2
                    if t % 2 == 0 and j > 0:
                        pe.wait_ge(c_sub, j * 2 + (u - 1))
                    ps = bank[u][:, (t % 2) * D:(t % 2 + 1) * D]
                    at = (j % GB) * GT + t * P
                    pe.matmul(ps, ones3[:, :], cb3[:, b * D:(b + 1) * D], start=True, stop=False)
                    for c in range(C):
                        mm = pe.matmul(ps, ynT[:, b, c, at:at + P], Wc[:, b, c, :], start=False, stop=(c == C - 1))
                    if t % 2:
                        mm.then_inc(c_ps, 1)

            def outputs(j):
                q, b, first = j % 2, j // GB, j == 0
                for u in range(2):
                    pe.wait_ge(c_prob, j * 2 + (u + 1))
                    if not first:
                        pe.wait_ge(c_pT_sb, j * 2 + (u - 1))
                    for v in range(2):
                        for m in range(2):
                            mm = pe.transpose(bA[u][:, (v * 2 + m) * P:(v * 2 + m + 1) * P],
                                              prob[:, q, 2 * u + v, m * P:(m + 1) * P], ident[:, :])
                    mm.then_inc(c_pT_ps, 1)
                for u in range(2):
                    pe.wait_ge(c_pT_sb, j * 2 + (u + 1))
                    if not first:
                        pe.wait_ge(co_sb, j * 2 + (u - 1))
                    for v in range(2):
                        ps = bank[6 + u][:, v * D:(v + 1) * D]
                        pe.matmul(ps, ones3[:, :], ab3[:, D:2 * D], start=True, stop=False)
                        for m in range(2):
                            mm = pe.matmul(ps, cpT[:, u, (v * 2 + m) * P:(v * 2 + m + 1) * P], Vc[:, b, m, :],
                                           start=False, stop=(m == 1))
                    mm.then_inc(co_ps, 1)

            scores(0)
            scores(1)
            pe.wait_ge(laid, 3)
            for j in range(NG):
                if j + 2 == GB:
                    pe.wait_ge(dve_part, CS + 5)
                outputs(j)
                if j + 2 < NG:
                    scores(j + 2)

        @block.vector
        def _(v):
            steps = [0]

            def hold(s, value):
                v.wait_ge(s, value)
                v.nop(nofuse=True)

            def own(ins, wait=True):
                steps[0] += 1
                ins.then_inc(prep, 1)
                if wait:
                    v.wait_ge(prep, steps[0])

            def split3(dst, src):
                h = aT[0:3, :, :].rearrange("p a n -> p (a n)").bitcast(BF16)
                n = src.shape[1]
                hs = [h[:, 512 * k:512 * k + n] for k in range(3)]
                r = o[0:3, 0, :, :].rearrange("p t n -> p (t n)")
                r1, r2 = r[:, 0:n], r[:, 512:512 + n]
                t0, t1 = scr1[0:3, 2048:2048 + n], scr1[0:3, 2560:2560 + n]
                own(v.tensor_copy(hs[0], src))
                own(v.tensor_tensor(r1, src, hs[0], ALU.subtract))
                own(v.tensor_copy(hs[1], r1))
                own(v.tensor_tensor(r2, r1, hs[1], ALU.subtract))
                own(v.tensor_copy(hs[2], r2))
                own(v.tensor_scalar(t0, hs[0], ident[0:3, 0:1], None, ALU.mult))
                own(v.scalar_tensor_tensor(out=t1, in0=hs[1], scalar=ident[0:3, 1:2], in1=t0, op0=ALU.mult, op1=ALU.add))
                return v.scalar_tensor_tensor(out=dst, in0=hs[2], scalar=ident[0:3, 2:3], in1=t1, op0=ALU.mult, op1=ALU.add)

            def spread(dst, src, m):
                n = src.shape[1]
                return v.tensor_tensor(dst, src.unsqueeze(1).broadcast_to([P, 8, n]),
                                       m[:, :].unsqueeze(2).broadcast_to([P, 8, n]), ALU.mult)

            v.wait_ge(consts, 14 + TOP)
            def statistics(k, i, src):
                for t in range(TG):
                    v.bn_stats(stats[:, k, t, :], src(t)).then_inc(stat[k], 1)
                hold(stat[k], i * TG + TG)
                for t in range(TG):
                    v.bn_aggr(mv[:, k, t, :], stats[:, k, t, :]).then_inc(mean[k], 1)

            def xtile(i, t):
                return x[:, bass.ds(i * TG + t, 1), :].rearrange("p o d -> p (o d)")

            def first_statistics(i):
                hold(xin_in, i * 16 + 16)
                statistics(0, i, lambda t: xin[:, t, :])

            first_statistics(0)
            own(v.tensor_reduce(sel[:, :], ident[:, :].rearrange("p (h e) -> p e h", e=NE), AX_X, ALU.add))
            v.wait_ge(pe_part, M_MISC)
            v.tensor_copy(miscT[:, :], bank[7][:, 0:146]).then_inc(dve_part, 1)
            v.wait_ge(pe_part, M_AQ)
            v.tensor_copy(aWqT.rearrange("p m c q -> p (m c q)"), bank[5][:, :]).then_inc(dve_part, 1)
            v.wait_ge(dve_part, M_AQ)
            v.wait_ge(pe_part, M_KQ)
            for m in range(2):
                own(v.tensor_scalar(aKT[:, m, :], bank[4][:, m * NS:(m + 1) * NS], bcol[:, ABK, m:m + 1], None, ALU.add), wait=m == 1)
            for a, k in ((0, ABQ), (1, CBQ)):
                for m in range(2):
                    own(v.tensor_copy(bq3[:, a, m, :], bcol[:, k, m:m + 1].broadcast_to([P, 3])), wait=False)
            own(spread(bdK[:, 0, :, :], aKT[:, 0, :], masks), wait=False)
            spread(bdK[:, 1, :, :], aKT[:, 1, :], masks).then_inc(dve_part, 1)
            for m in range(2):
                own(v.tensor_copy(aKT4[:, m, :].rearrange("p (j s) -> p j s", j=4),
                                  aKT[:, m, :].unsqueeze(1).broadcast_to([P, 4, NS])), wait=False)
            v.wait_ge(pe_part, M_WZ)
            own(v.tensor_copy(Wz[:, 0, :], bZ[0][:, :]), wait=False)
            v.tensor_copy(Wz[:, 1, :], bZ[1][:, :]).then_inc(dve_part, 1)
            v.wait_ge(pe_part, M_ZB)
            split3(zb3[:, :], bank[6][0:3, :]).then_inc(dve_part, 1)

            def fold_dispatch():
                v.wait_ge(pe_part, M_DK)
                v.tensor_copy(dWkT.rearrange("p m c q -> p (m c q)"), bank[5][:, :]).then_inc(dve_part, 1)
                v.wait_ge(pe_part, M_DQ)
                for m in range(2):
                    own(v.tensor_scalar(dQT[:, m, :], bank[4][:, 64 + m * NE:64 + (m + 1) * NE], bcol[:, DBQ, m:m + 1], None,
                                        ALU.add), wait=m == 1)
                own(spread(bdQ[:, 0, :, :], dQT[:, 0, :], masks), wait=False)
                spread(bdQ[:, 1, :, :], dQT[:, 1, :], masks).then_inc(dve_part, 1)
                v.wait_ge(pe_part, M_V)
                v.tensor_copy(vrep[:, :, :].rearrange("p h e -> p (h e)"), bank[6][:, 0:D]).then_inc(dve_part, 1)

            def keep_dispatch():
                v.wait_ge(pe_part, M_WD)
                own(v.tensor_copy(Wd[:, :, :].rearrange("p c n -> p (c n)"), bank[4][:, :]), wait=False)
                v.tensor_copy(dconst[:, :], bank[7][:, 0:2]).then_inc(dve_part, 1)

            rows = [P, NH, TG, NS]
            d3 = d[:, :].rearrange("p (h t s) -> p h t s", h=NH, t=TG)
            a3 = above[:, :].rearrange("p (h t s) -> p h t s", h=NH, t=TG)
            tau3 = tau[:, :].rearrange("p (h t) -> p h t", h=NH).unsqueeze(3).broadcast_to(rows)
            rcnt3 = rcnt[:, :].rearrange("p (h t) -> p h t", h=NH).unsqueeze(3).broadcast_to(rows)

            def sort_top(i, tiles):
                for t in tiles:
                    hold(z_sb, i * TG + (t + 1))
                    for h in range(NH):
                        mx = v.max(top[:, h * TG + t, :], bZ[t % 2][:, h * NS:(h + 1) * NS])
                    mx.then_inc(topped, 1)

            def threshold(i):
                v.wait_ge(topped, i * TG + TG)
                for k in range(1, TOP):
                    v.tensor_tensor(top[:, :, k], top[:, :, k], top[:, :, k - 1], ALU.add).then_inc(cum, 1)
                    v.wait_ge(cum, i * 9 + k)
                v.scalar_tensor_tensor(out=top[:, :, :], in0=top[:, :, :], scalar=-1.0,
                                       in1=rk[:, :].unsqueeze(1).broadcast_to([P, HR, TOP]),
                                       op0=ALU.add, op1=ALU.mult).then_inc(cum, 1)
                v.wait_ge(cum, i * 9 + 8)
                v.tensor_reduce(tau[:, :], top[:, :, :], AX_X, ALU.max).then_inc(cum, 1)

            def scores_at(i, b):
                return scr[b][:, :, bass.ds(i * TG - b * KT, TG), :]

            def subtract(i, b):
                v.wait_ge(cum, i * 9 + 9)
                v.tensor_tensor(d3, scores_at(i, b), tau3, ALU.subtract).then_inc(diff, 1)

            def count(i):
                v.wait_ge(relued, i + 1)
                if not (isinstance(i, int) and i == 0):
                    v.wait_ge(signed, i)
                v.tensor_scalar(above[:, :], d[:, :], 0.0, None, ALU.is_gt).then_inc(newton, 1)
                v.tensor_reduce(exc[:, :], d3, AX_X, ALU.add).then_inc(newton, 1)
                v.wait_ge(newton, i * NW + 1)
                v.tensor_reduce(cnt[:, :], a3, AX_X, ALU.add).then_inc(newton, 1)

            def settle(i, b, last=False):
                v.wait_ge(newton, i * NW + 3)
                v.tensor_scalar(cnt[:, :], cnt[:, :], 1.0, None, ALU.max).then_inc(newton, 1)
                v.wait_ge(newton, i * NW + 4)
                v.tensor_reduce(tot[:, 0, bass.ds(i - b * GB, 1)], cnt[:, :], AX_X, ALU.add).then_inc(newton, 1)
                v.reciprocal(rcnt[:, :], cnt[:, :]).then_inc(newton, 1)
                v.wait_ge(newton, i * NW + 6)
                v.scalar_tensor_tensor(out=rcnt[:, :], in0=exc[:, :], scalar=-1.0, in1=rcnt[:, :],
                                       op0=ALU.add, op1=ALU.mult).then_inc(newton, 1)
                if not (isinstance(i, int) and i == 0):
                    v.wait_ge(lowered, i)
                v.wait_ge(newton, i * NW + 7)
                v.tensor_tensor(tauf[:, :], tau[:, :], rcnt[:, :], ALU.add).then_inc(tau_ready, 1)
                if last:
                    v.wait_ge(tau_ready, i + 1)
                    v.tensor_tensor(scores_at(i, b), scores_at(i, b), tauf[:, :].rearrange("p (h t) -> p h t", h=NH)
                                    .unsqueeze(3).broadcast_to(rows), ALU.subtract).then_inc(lowered, 1)

            def check(b):
                v.wait_ge(signed, GB * (b + 1))
                v.wait_ge(newton, GB * (b + 1) * NW)
                v.tensor_scalar(tot[:, 1, :], ahead[:, b * GB:(b + 1) * GB], float(HR * NS), 0.5, ALU.add, ALU.mult)\
                    .then_inc(checked, 1)
                v.wait_ge(checked, b * 5 + 1)
                v.tensor_tensor(tot[:, 1, :], tot[:, 1, :], tot[:, 0, :], ALU.not_equal).then_inc(checked, 1)
                v.wait_ge(checked, b * 5 + 2)
                v.tensor_reduce(moved[:, 0:1], tot[:, 1, :], AX_X, ALU.max).then_inc(checked, 1)
                v.wait_ge(checked, b * 5 + 3)
                v.transpose(movedT[:, :], moved[:, :]).then_inc(checked, 1)
                v.wait_ge(checked, b * 5 + 4)
                v.tensor_reduce(flagi[:, :], movedT[:, :], AX_X, ALU.max).then_inc(checked, 1)
                hold(checked, b * 5 + 5)
                parts = [v.value_load(flagi[32 * k:32 * k + 1, 0:1]) for k in range(4)]
                with v.If(parts[0] + parts[1] + parts[2] + parts[3] > 0):
                    with v.Fori(0, GB) as g:
                        z3 = scr[b][:, :, bass.ds(g * TG, TG), :]
                        with v.Fori(0, FIXES) as s:
                            at = g * (FIXES * 8) + s * 8 + b * (GB * FIXES * 8)
                            v.tensor_scalar(a3, z3, 0.0, None, ALU.is_gt).then_inc(fix, 1)
                            v.tensor_scalar(d3, z3, 0.0, None, ALU.max).then_inc(fix, 1)
                            v.wait_ge(fix, at + 2)
                            v.tensor_reduce(cnt[:, :], a3, AX_X, ALU.add).then_inc(fix, 1)
                            v.tensor_reduce(exc[:, :], d3, AX_X, ALU.add).then_inc(fix, 1)
                            v.wait_ge(fix, at + 4)
                            v.tensor_scalar(cnt[:, :], cnt[:, :], 1.0, None, ALU.max).then_inc(fix, 1)
                            v.wait_ge(fix, at + 5)
                            v.reciprocal(rcnt[:, :], cnt[:, :]).then_inc(fix, 1)
                            v.wait_ge(fix, at + 6)
                            v.scalar_tensor_tensor(out=rcnt[:, :], in0=exc[:, :], scalar=-1.0, in1=rcnt[:, :],
                                                   op0=ALU.add, op1=ALU.mult).then_inc(fix, 1)
                            v.wait_ge(fix, at + 7)
                            v.tensor_tensor(z3, z3, rcnt3, ALU.subtract).then_inc(fix, 1)
                            v.wait_ge(fix, at + 8)
                with v.Else():
                    v.sem_inc(fix, GB * FIXES * 8)
                v.tensor_copy(flag[:, :], moved[:, 0:1]).then_inc(settled, 1)

            def output_statistics(g):
                for t in range(TG):
                    v.wait_ge(o_sb, g * TG + (t + 1))
                    v.bn_stats(stats[:, 1, t, :], o[:, g % 2, t, :]).then_inc(stat[1], 1)
                v.wait_ge(stat[1], g * TG + TG)
                for t in range(TG):
                    v.bn_aggr(mv[:, 1, t, :], stats[:, 1, t, :]).then_inc(mean[1], 1)

            def join(g):
                v.wait_ge(o_norm, g * TG + TG)
                tiles = x[:, g * TG:(g + 1) * TG, :]
                v.tensor_tensor(tiles, tiles, o[:, g % 2, :, :], ALU.add).then_inc(x_new, 1)
                v.wait_ge(x_new, g + 1)
                if g > 0:
                    v.wait_ge(rst[2], g)
                statistics(2, g, lambda t: x[:, g * TG + t, :])

            def group_maximum(g):
                v.wait_ge(s_sb, 2 * g + 2)
                at = (g % GB) * GT
                for m in range(2):
                    v.tensor_reduce(pmax[:, m, g % GB:g % GB + 1], s_all[:, m, at:at + GT], AX_X, ALU.max).then_inc(maxed, 1)

            def batch_maximum(b):
                v.wait_ge(maxed, NMX * b + NMX - 2)
                v.tensor_reduce(smax[:, :], pmax[:, :, :], AX_X, ALU.max).then_inc(maxed, 1)
                v.wait_ge(maxed, NMX * b + NMX - 1)
                v.tensor_scalar(nmax[:, :], smax[:, :], -1.0, None, ALU.mult).then_inc(maxed, 1)

            def to_slots(b, step):
                p0, s0 = PREP + b * ND, b * NSL
                if step == 0:
                    v.wait_ge(exped, 2 * b + 2)
                    v.reciprocal(rsum[:, :], ssum[:, :]).then_inc(slots, 1)
                    v.wait_ge(slots, s0 + 1)
                    v.wait_ge(g_ps, (b + 1) * (KT // 2))
                    v.tensor_copy(gT[:, 0, :, :], bZ[0][:, 0:2 * P].rearrange("p (m n) -> p m n", m=2)).then_inc(slots, 1)
                    v.tensor_copy(gT[:, 1, :, :], bZ[1][:, 0:2 * P].rearrange("p (m n) -> p m n", m=2)).then_inc(dve_part, 1)
                elif step == 1:
                    v.wait_ge(pe_part, p0 + D_Z)
                    for m in range(2):
                        z_ = v.scalar_tensor_tensor(out=zm[:, m, :].rearrange("p (h j) -> p h j", h=8),
                                                    in0=bZ[0][:, m * P:(m + 1) * P].rearrange("p (h j) -> p h j", h=8),
                                                    scalar=rsum[:, m:m + 1],
                                                    in1=mask[:, :].unsqueeze(2).broadcast_to([P, 8, DH]),
                                                    op0=ALU.mult, op1=ALU.mult)
                        z_.then_inc((slots, dve_part)[m], 1)
                elif step == 2:
                    v.wait_ge(pe_part, p0 + D_H)
                    for m in range(2):
                        h_ = v.tensor_scalar(hT[:, m, :], bZ[1][:, m * NE:(m + 1) * NE], bcol[:, DBV, m:m + 1], None, ALU.add)
                        h_.then_inc((slots, dve_part)[m], 1)
                elif step == 3:
                    v.wait_ge(pe_part, p0 + D_SLOT)
                    v.tensor_tensor(slot, bZ[0][0:NE, 0:D], sq[:, :], ALU.add).then_inc(slots, 1)
                    v.wait_ge(slots, s0 + 5)
                    v.bn_stats(sstats[:, :], slot).then_inc(smean, 1)
                    v.wait_ge(smean, 2 * b + 1)
                    v.bn_aggr(smv[:, :], sstats[:, :]).then_inc(smean, 1)
                    v.wait_ge(smean, 2 * b + 2)
                    v.wait_ge(srst, 2 * b + 2)
                    v.tensor_scalar(hid, slot, smv[:, 0:1], srstd[:, 0:1], ALU.subtract, ALU.mult).then_inc(slots, 1)
                    v.wait_ge(slots, s0 + 6)
                    v.tensor_tensor(hid, hid, lng, ALU.mult).then_inc(slots, 1)
                    v.wait_ge(slots, s0 + 7)
                    v.tensor_tensor(hid, hid, lnb, ALU.add).then_inc(dve_part, 1)
                else:
                    v.wait_ge(pe_part, p0 + D_T)
                    v.tensor_copy(slotT[:, :, b, :], bZ[1][:, 0:32].rearrange("p (c e) -> p c e", c=C)).then_inc(slots, 1)
                    v.tensor_copy(hidT[:, :, b, :], bZ[1][:, 32:64].rearrange("p (c e) -> p c e", c=C)).then_inc(dve_part, 1)
                    v.wait_ge(slots, s0 + NSL)

            NW = 7
            NSL = 8
            first_statistics(1)
            v.wait_ge(bo_in, 32)
            own(split3(ab3[:, :], bo3.rearrange("p a d -> p (a d)")))
            sort_top(0, range(2))
            fold_dispatch()
            sort_top(0, range(2, TG))
            threshold(0)
            keep_dispatch()

            def batch_of_scores(i, b, last=False):
                subtract(i, b)
                first_statistics(i + 2)
                sort_top(i + 1, range(2))
                count(i)
                sort_top(i + 1, range(2, TG))
                settle(i, b, last)
                threshold(i + 1)

            batch_of_scores(0, 0)
            with v.Fori(1, GB - 1) as i:
                batch_of_scores(i, 0)
            batch_of_scores(GB - 1, 0, last=True)
            check(0)
            v.wait_ge(x_in, 16)
            for i in range(GB, NG):
                g = i - GB
                subtract(i, 1)
                if g > 0:
                    output_statistics(g - 1)
                if i + 2 < NG:
                    first_statistics(i + 2)
                if i + 1 < NG:
                    sort_top(i + 1, range(2))
                if g > 0:
                    join(g - 1)
                count(i)
                if i + 1 < NG:
                    sort_top(i + 1, range(2, TG))
                settle(i, 1, last=i == NG - 1)
                if i + 1 < NG:
                    threshold(i + 1)
                if g > 1:
                    group_maximum(g - 2)
            output_statistics(3)
            check(1)
            join(3)
            group_maximum(2)
            output_statistics(4)
            join(4)
            group_maximum(3)
            batch_maximum(0)
            v.wait_ge(w_in2, 16 * N_W2)
            own(v.tensor_tensor(sq[:, :], sq[:, :], dbo, ALU.add))
            output_statistics(5)
            join(5)
            to_slots(0, 0)
            output_statistics(6)
            group_maximum(4)
            to_slots(0, 1)
            join(6)
            group_maximum(5)
            output_statistics(7)
            to_slots(0, 2)
            join(7)
            to_slots(0, 3)
            group_maximum(6)
            group_maximum(7)
            batch_maximum(1)
            to_slots(0, 4)
            for step in range(5):
                to_slots(1, step)

            v.wait_ge(pe_part, CP + 1)
            own(v.tensor_copy(cWqT.rearrange("p m c q -> p (m c q)"), bank[6][:, :]), wait=False)
            v.tensor_copy(bT1.rearrange("p e g j -> p g e j"), bank[7][:, 0:2 * P].rearrange("p (g e j) -> p g e j", g=2, j=J))\
                .then_inc(hbias, 1)
            v.wait_ge(hbias, 1)
            for b in range(NB):
                own(v.tensor_tensor(slotT[:, :, b, :], slotT[:, :, b, :], b2T, ALU.add), wait=b == NB - 1)

            def keep_down(e):
                v.wait_ge(down_ps, e + 1)
                v.tensor_copy(dn, bank[6][0:NB, 0:D]).then_inc(dn_sb, 1)

            def add_down(e):
                v.wait_ge(dnT_ps, e + 1)
                v.tensor_tensor(newT[:, :, :, bass.ds(e, 1)].rearrange("p c b o -> p c (b o)"),
                                bank[7][:, 0:C * NB].rearrange("p (c b) -> p c b", c=C),
                                slotT[:, :, :, bass.ds(e, 1)].rearrange("p c b o -> p c (b o)"), ALU.add).then_inc(down_sb, 1)

            def expert(h, k, first=False):
                e, q = h * 3 + k, k % 3
                v.wait_ge(up_ps, e * 2 + 2)
                v.tensor_copy(ugT[q], bank[q][:, :]).then_inc(ug_sb, 1)
                if not first:
                    keep_down(e - 1)
                v.wait_ge(ugT_ps, e + 1)
                v.tensor_tensor(pre.rearrange("p g (a j) b -> p (g a) j b", a=2),
                                bank[3 + q][:, :].rearrange("p (j k x) -> p k j x", j=4, k=4)[:, :, :, 0:NB],
                                bT1[:, bass.ds(e, 1), :, :].rearrange("p o g (a j) -> p (o g a) j", a=2).unsqueeze(3)
                                .broadcast_to([P, 4, 4, NB]), ALU.add).then_inc(pred, 1)
                v.wait_ge(silued, e + 1)
                v.tensor_tensor(ug[:, q, :, :], gate[:, 0, :, :], gate[:, 1, :, :], ALU.mult).then_inc(ug_ready, 1)
                if not first:
                    add_down(e - 1)

            expert(0, 0, first=True)
            with v.Fori(0, 5) as h:
                for k in range(1, 4):
                    expert(h, k)
            keep_down(NE - 1)
            add_down(NE - 1)

            v.wait_ge(pe_part, CP + 2)
            for m in range(2):
                own(v.tensor_scalar(cKT[:, m, :, :], bank[0][:, m * 32:(m + 1) * 32].rearrange("p (b e) -> p b e", b=NB),
                                    bcol[:, CBK, m:m + 1], None, ALU.add), wait=m == 1)
            own(spread(cbK[:, 0, 0, :, :], cKT[:, 0, 0, :], masks), wait=False)
            spread(cbK[:, 1, 0, :, :], cKT[:, 1, 0, :], masks).then_inc(dve_part, 1)
            for m in range(2):
                own(v.tensor_scalar(cVT[:, m, :, :], bank[0][:, 64 + m * 32:64 + (m + 1) * 32].rearrange("p (b e) -> p b e", b=NB),
                                    bcol[:, CBV, m:m + 1], None, ALU.add), wait=m == 1)
            own(spread(cbV[:, 0, 0, :, :], cVT[:, 0, 0, :], mask), wait=False)
            spread(cbV[:, 1, 0, :, :], cVT[:, 1, 0, :], mask).then_inc(dve_part, 1)
            own(spread(cbK[:, 0, 1, :, :], cKT[:, 0, 1, :], masks), wait=False)
            own(spread(cbK[:, 1, 1, :, :], cKT[:, 1, 1, :], masks), wait=False)
            own(spread(cbV[:, 0, 1, :, :], cVT[:, 0, 1, :], mask), wait=False)
            spread(cbV[:, 1, 1, :, :], cVT[:, 1, 1, :], mask).then_inc(dve_part, 1)
            v.wait_ge(pe_part, CP + 3)
            own(v.tensor_copy(Wc[:, 0, :, :].rearrange("p c n -> p (c n)"), bank[1][:, :]), wait=False)
            split3(cb3[:, 0:D], bank[7][0:3, 0:D]).then_inc(dve_part, 1)

            def soften(j, q):
                for u in range(2):
                    v.wait_ge(c_ps, j * 2 + (u + 1))
                    ps = bank[u][:, :].rearrange("p (r e) -> p r e", e=NE)
                    cm = cmax[:, u * 32:(u + 1) * 32]
                    v.tensor_reduce(cm, ps, AX_X, ALU.max).then_inc(c_max, 1)
                    v.wait_ge(c_max, j * 2 + (u + 1))
                    v.tensor_tensor(prob[:, q, 2 * u:2 * u + 2, :].rearrange("p t (h e) -> p (t h) e", e=NE), ps,
                                    cm.unsqueeze(2).broadcast_to([P, 32, NE]), ALU.subtract).then_inc(c_sub, 1)

            def total(j, q, first=False):
                for u in range(2):
                    half = slice(u * 32, (u + 1) * 32)
                    v.wait_ge(c_exp, j * 2 + (u + 1))
                    v.tensor_reduce(csum[:, half], prob[:, q, 2 * u:2 * u + 2, :].rearrange("p t (h e) -> p (t h) e", e=NE),
                                    AX_X, ALU.add).then_inc(c_sum, 1)
                    v.wait_ge(c_sum, j * 2 + (u + 1))
                    if not first:
                        v.wait_ge(c_prob, j * 2 + (u - 1))
                    v.reciprocal(crs[:, half], csum[:, half]).then_inc(c_rs, 1)

            def norm_out(j, q, first=False):
                if not first:
                    v.wait_ge(c_mean, j * TG)
                for t in range(TG):
                    hold(co_sb, j * 2 + (t // 2 + 1))
                    v.bn_stats(stats[:, 0, t, :], co[:, q, t, :]).then_inc(c_stat, 1)
                if not first:
                    v.wait_ge(c_rst, j)
                hold(c_stat, j * TG + TG)
                for t in range(TG):
                    v.bn_aggr(mv[:, 0, t, :], stats[:, 0, t, :]).then_inc(c_mean, 1)

            def add_stream(j, q):
                v.wait_ge(c_norm, j * TG + TG)
                tiles = co[:, q, :, :]
                v.tensor_tensor(tiles, tiles, x[:, bass.ds(j * TG, TG), :], ALU.add).then_inc(c_out, 1)

            def combine(j, q, first=False):
                total(j, q)
                norm_out(j - 1, 1 - q, first)
                soften(j + 1, 1 - q)
                if not first:
                    add_stream(j - 2, q)

            soften(0, 0)
            total(0, 0, first=True)
            soften(1, 1)
            v.wait_ge(pe_part, CP + 5)
            split3(cb3[:, D:2 * D], bank[3][0:3, 0:D]).then_inc(dve_part, 1)
            combine(1, 1, first=True)
            combine(2, 0)
            with v.Fori(1, NG // 2 - 1) as h:
                combine(h * 2 + 1, 1)
                combine(h * 2 + 2, 0)
            total(NG - 1, 1)
            norm_out(NG - 2, 0)
            add_stream(NG - 3, 1)
            norm_out(NG - 1, 1)
            add_stream(NG - 2, 0)
            add_stream(NG - 1, 1)


_INS = ['L0_attn_query', 'L0_attn_key_param', 'L0_attn_Wq', 'L0_attn_bq', 'L0_attn_Wk', 'L0_attn_bk', 'L0_attn_Wv',
        'L0_attn_bv', 'L0_attn_Wo', 'L0_attn_bo', 'L0_ffn_slot_query', 'L0_ffn_d_Wq', 'L0_ffn_d_Wk', 'L0_ffn_d_Wv',
        'L0_ffn_d_Wo', 'L0_ffn_d_bq', 'L0_ffn_d_bk', 'L0_ffn_d_bv', 'L0_ffn_d_bo', 'L0_ffn_c_Wq', 'L0_ffn_c_Wk',
        'L0_ffn_c_Wv', 'L0_ffn_c_Wo', 'L0_ffn_c_bq', 'L0_ffn_c_bk', 'L0_ffn_c_bv', 'L0_ffn_c_bo', 'L0_ffn_e_ln_g',
        'L0_ffn_e_ln_b', 'L0_ffn_e_W1', 'L0_ffn_e_b1', 'L0_ffn_e_Wg', 'L0_ffn_e_bg', 'L0_ffn_e_W2', 'L0_ffn_e_b2']
_OUTS = [((2, 2048, 256), 'float32')]


def kernel(**inputs):
    import numpy as _np
    import concourse.bacc as _bacc
    from concourse import mybir as _mybir
    from concourse.bass_utils import run_bass_kernel_spmd as _run

    nc = _bacc.Bacc("TRN2", target_bir_lowering=False, num_devices=1)
    arrays, args = {}, {}
    for name in _INS:
        a = _np.ascontiguousarray(inputs[name])
        arrays[f"in_{name}_dram"] = a
        args[name] = nc.dram_tensor(f"in_{name}_dram", a.shape, _mybir.dt.from_np(a.dtype), kind="ExternalInput").ap()
    shape, dtype = _OUTS[0]
    out = nc.dram_tensor("out_0_dram", shape, _mybir.dt.from_np(_np.dtype(dtype)), kind="ExternalOutput").ap()
    build(nc, args, out)
    r = _run(nc, [arrays], core_ids=[0])
    return r.results[0]["out_0_dram"]
```
